# Optimizing a Trainium2 kernel written in Bass

```python
import numpy as np
import jax
import jax.numpy as jnp

def _softmax(x, axis=-1):
    return jax.nn.softmax(x, axis=axis)

def _gelu(x):
    return jax.nn.gelu(x, approximate=True)

def _silu(x):
    return jax.nn.silu(x)

def _sigmoid(x):
    return jax.nn.sigmoid(x)

def _layernorm(x, axis=-1, eps=1e-05):
    m = jnp.mean(x, axis=axis, keepdims=True)
    v = jnp.var(x, axis=axis, keepdims=True)
    return (x - m) / jnp.sqrt(v + eps)

def _scatter_add(tgt, idx, src, axis=0):
    return tgt.at[idx].add(src)

def _segment_sum(src, seg, n):
    return jax.ops.segment_sum(src, seg, n)
kernel_name = 'mk_sandwich_d2_jaxref_r8_096dd7'

def setup_inputs(seed: int=0):
    np.random.seed(seed)
    _w = jnp.asarray

    def _L0_attn_setup():
        import jax, jax.numpy as jnp
        import numpy as np
        NUM_HEADS = 16
        D_MODEL = 128
        HEAD_DIM = D_MODEL // NUM_HEADS
        WINDOW = 64
        SCALE = 8.0 / HEAD_DIM
        LN_EPS = 1e-05

        def _layernorm(t, gamma, beta):
            mu = jnp.mean(t, axis=-1, keepdims=True)
            var = jnp.var(t, axis=-1, keepdims=True)
            return (t - mu) * jax.lax.rsqrt(var + LN_EPS) * gamma + beta
        key = jax.random.key(seed)
        ks = jax.random.split(key, 4)
        x = jax.random.normal(ks[0], (4, 1024, D_MODEL), dtype=jnp.float32)
        W_qkv = jax.random.normal(ks[1], (D_MODEL, 3 * D_MODEL), dtype=jnp.float32) * D_MODEL ** (-0.5)
        ln_gamma = jnp.ones((HEAD_DIM,), dtype=jnp.float32)
        ln_beta = jnp.zeros((HEAD_DIM,), dtype=jnp.float32)
        W_proj = jax.random.normal(ks[2], (D_MODEL, D_MODEL), dtype=jnp.float32) * D_MODEL ** (-0.5)
        b_proj = jax.random.normal(ks[3], (D_MODEL,), dtype=jnp.float32) * 0.02
        return {'x': x, 'W_qkv': W_qkv, 'ln_gamma': ln_gamma, 'ln_beta': ln_beta, 'W_proj': W_proj, 'b_proj': b_proj}
    _L0_attn_in = _L0_attn_setup()

    def _L0_ffn_setup():
        import jax, jax.numpy as jnp
        import numpy as np
        DIM = 128
        DEPTH = 2
        HEADS = 8
        DIM_HEAD = 64
        WINDOW = 64
        INNER = HEADS * DIM_HEAD
        HID = int(DIM * 4 * 2 / 3)
        B, N = (2, 1024)
        QK_SCALE = 8.0

        def shift_token(t):
            t1, t2 = jnp.split(t, 2, axis=-1)
            t2 = jnp.pad(t2, ((0, 0), (1, 0), (0, 0)))[:, :-1]
            return jnp.concatenate([t1, t2], axis=-1)

        def l2norm(t):
            return t / jnp.clip(jnp.linalg.norm(t, axis=-1, keepdims=True), 1e-12)

        def rotate_half(x):
            x1, x2 = jnp.split(x, 2, axis=-1)
            return jnp.concatenate([-x2, x1], axis=-1)

        def rotary_xpos(q, k):
            n = q.shape[-2]
            half_idx = jnp.arange(0, DIM_HEAD, 2, dtype=jnp.float32)
            inv_freq = 1.0 / 10000.0 ** (half_idx / DIM_HEAD)
            t = jnp.arange(n, dtype=jnp.float32)
            freqs = t[:, None] * inv_freq[None, :]
            freqs = jnp.concatenate([freqs, freqs], axis=-1)
            base = (half_idx + 0.4 * DIM_HEAD) / (1.4 * DIM_HEAD)
            power = (t - n // 2) / float(WINDOW // 2)
            scale = base[None, :] ** power[:, None]
            scale = jnp.concatenate([scale, scale], axis=-1)
            cos, sin = (jnp.cos(freqs), jnp.sin(freqs))
            q = q * cos * scale + rotate_half(q) * sin * scale
            k = k * cos / scale + rotate_half(k) * sin / scale
            return (q, k)

        def local_attention(q, k, v):
            b, h, n, d = q.shape
            w = n // WINDOW
            bq = q.reshape(b, h, w, WINDOW, d) * QK_SCALE
            bk = k.reshape(b, h, w, WINDOW, d)
            bv = v.reshape(b, h, w, WINDOW, d)

            def look_around(t):
                p = jnp.pad(t, ((0, 0), (0, 0), (1, 0), (0, 0), (0, 0)))
                return jnp.concatenate([p[:, :, :w], p[:, :, 1:]], axis=3)
            bk, bv = (look_around(bk), look_around(bv))
            bt = jnp.arange(n).reshape(w, WINDOW)
            btp = jnp.pad(bt, ((1, 0), (0, 0)), constant_values=-1)
            btk = jnp.concatenate([btp[:w], btp[1:]], axis=1)
            sim = jnp.einsum('bhwid,bhwjd->bhwij', bq, bk)
            i = bt[:, :, None]
            j = btk[:, None, :]
            mask = (i < j) | (i > j + WINDOW) | (j == -1)
            sim = jnp.where(mask, -jnp.finfo(sim.dtype).max, sim)
            attn = jax.nn.softmax(sim, axis=-1)
            out = jnp.einsum('bhwij,bhwjd->bhwid', attn, bv)
            return out.reshape(b, h, n, d)

        def _layer(x, wqkv, qs, ksc, wo, lg, lb, w1, b1, w2, b2):
            b, n, _ = x.shape
            h = shift_token(x)
            qkv = h @ wqkv
            q, k, v = jnp.split(qkv, 3, axis=-1)
            to_heads = lambda t: t.reshape(b, n, HEADS, DIM_HEAD).transpose(0, 2, 1, 3)
            q, k, v = (to_heads(q), to_heads(k), to_heads(v))
            q = l2norm(q) * qs
            k = l2norm(k) * ksc
            q, k = rotary_xpos(q, k)
            o = local_attention(q, k, v)
            o = o.transpose(0, 2, 1, 3).reshape(b, n, INNER)
            x = x + o @ wo
            h = shift_token(x)
            mu = h.mean(-1, keepdims=True)
            var = h.var(-1, keepdims=True)
            h = (h - mu) / jnp.sqrt(var + 1e-05) * lg + lb
            h = h @ w1 + b1
            a, g = jnp.split(h, 2, axis=-1)
            h = a * jax.nn.gelu(g, approximate=False)
            x = x + h @ w2 + b2
            return x
        key = jax.random.key(seed)
        ks = jax.random.split(key, 6)
        return {'x': jax.random.normal(ks[0], (B, N, DIM), jnp.float32), 'wqkv': jax.random.normal(ks[1], (DEPTH, DIM, 3 * INNER), jnp.float32) * 0.02, 'q_scale': jnp.ones((DEPTH, DIM_HEAD), jnp.float32), 'k_scale': jnp.ones((DEPTH, DIM_HEAD), jnp.float32), 'wo': jax.random.normal(ks[2], (DEPTH, INNER, DIM), jnp.float32) * 0.02, 'ln_g': jnp.ones((DEPTH, DIM), jnp.float32), 'ln_b': jnp.zeros((DEPTH, DIM), jnp.float32), 'w1': jax.random.normal(ks[3], (DEPTH, DIM, 2 * HID), jnp.float32) * 0.02, 'b1': jnp.zeros((DEPTH, 2 * HID), jnp.float32), 'w2': jax.random.normal(ks[4], (DEPTH, HID, DIM), jnp.float32) * 0.02, 'b2': jnp.zeros((DEPTH, DIM), jnp.float32)}
    _L0_ffn_in = _L0_ffn_setup()

    def _L1_attn_setup():
        import jax, jax.numpy as jnp
        import numpy as np
        LN_EPS = 1e-05
        key = jax.random.key(seed)
        k0, k1, k2, k3 = jax.random.split(key, 4)
        B, T, D = (8, 256, 128)
        x = jax.random.normal(k0, (B, T, D), dtype=jnp.float32)
        u = jax.random.normal(k1, (D,), dtype=jnp.float32) * 0.1
        W = jax.random.normal(k2, (3 * D, D), dtype=jnp.float32) * (1.0 / np.sqrt(D))
        b = jax.random.normal(k3, (3 * D,), dtype=jnp.float32) * 0.01
        gamma = jnp.ones((D,), dtype=jnp.float32)
        beta = jnp.zeros((D,), dtype=jnp.float32)
        return {'x': x, 'u': u, 'W': W, 'b': b, 'gamma': gamma, 'beta': beta}
    _L1_attn_in = _L1_attn_setup()

    def _L1_ffn_setup():
        import jax, jax.numpy as jnp
        import numpy as np
        D = 128
        H = 512
        E = 8
        K = 2
        B, S = (4, 256)
        key = jax.random.key(seed)
        ks = jax.random.split(key, 8)

        def lin(k, fan_in, shape):
            bound = 1.0 / np.sqrt(fan_in)
            return jax.random.uniform(k, shape, jnp.float32, -bound, bound)
        return {'x': jax.random.normal(ks[0], (B, S, D), jnp.float32), 'Wg': lin(ks[1], D, (D, E)), 'bg': lin(ks[2], D, (E,)), 'W1': lin(ks[3], D, (E, D, H)), 'b1': lin(ks[4], D, (E, H)), 'W2': lin(ks[5], H, (E, H, D)), 'b2': lin(ks[6], H, (E, D))}
    _L1_ffn_in = _L1_ffn_setup()
    _d = {'L0_attn_x': _L0_attn_in['x'], 'L0_attn_W_qkv': _L0_attn_in['W_qkv'], 'L0_attn_ln_gamma': _L0_attn_in['ln_gamma'], 'L0_attn_ln_beta': _L0_attn_in['ln_beta'], 'L0_attn_W_proj': _L0_attn_in['W_proj'], 'L0_attn_b_proj': _L0_attn_in['b_proj'], 'L0_ffn_wqkv': _L0_ffn_in['wqkv'], 'L0_ffn_q_scale': _L0_ffn_in['q_scale'], 'L0_ffn_k_scale': _L0_ffn_in['k_scale'], 'L0_ffn_wo': _L0_ffn_in['wo'], 'L0_ffn_ln_g': _L0_ffn_in['ln_g'], 'L0_ffn_ln_b': _L0_ffn_in['ln_b'], 'L0_ffn_w1': _L0_ffn_in['w1'], 'L0_ffn_b1': _L0_ffn_in['b1'], 'L0_ffn_w2': _L0_ffn_in['w2'], 'L0_ffn_b2': _L0_ffn_in['b2'], 'L1_attn_u': _L1_attn_in['u'], 'L1_attn_W': _L1_attn_in['W'], 'L1_attn_b': _L1_attn_in['b'], 'L1_attn_gamma': _L1_attn_in['gamma'], 'L1_attn_beta': _L1_attn_in['beta'], 'L1_ffn_Wg': _L1_ffn_in['Wg'], 'L1_ffn_bg': _L1_ffn_in['bg'], 'L1_ffn_W1': _L1_ffn_in['W1'], 'L1_ffn_b1': _L1_ffn_in['b1'], 'L1_ffn_W2': _L1_ffn_in['W2'], 'L1_ffn_b2': _L1_ffn_in['b2']}
    _x0 = _d['L0_attn_x']
    _d['L0_attn_x'] = jax.random.normal(jax.random.fold_in(jax.random.key(seed), 1), (8, 512, 128), dtype=_x0.dtype)
    del _x0
    return _d

def reference(L0_attn_x, L0_attn_W_qkv, L0_attn_ln_gamma, L0_attn_ln_beta, L0_attn_W_proj, L0_attn_b_proj, L0_ffn_wqkv, L0_ffn_q_scale, L0_ffn_k_scale, L0_ffn_wo, L0_ffn_ln_g, L0_ffn_ln_b, L0_ffn_w1, L0_ffn_b1, L0_ffn_w2, L0_ffn_b2, L1_attn_u, L1_attn_W, L1_attn_b, L1_attn_gamma, L1_attn_beta, L1_ffn_Wg, L1_ffn_bg, L1_ffn_W1, L1_ffn_b1, L1_ffn_W2, L1_ffn_b2):

    def _L0_attn_ref(x, W_qkv, ln_gamma, ln_beta, W_proj, b_proj):
        import jax, jax.numpy as jnp
        import numpy as np
        NUM_HEADS = 16
        D_MODEL = 128
        HEAD_DIM = D_MODEL // NUM_HEADS
        WINDOW = 64
        SCALE = 8.0 / HEAD_DIM
        LN_EPS = 1e-05

        def _layernorm(t, gamma, beta):
            mu = jnp.mean(t, axis=-1, keepdims=True)
            var = jnp.var(t, axis=-1, keepdims=True)
            return (t - mu) * jax.lax.rsqrt(var + LN_EPS) * gamma + beta
        B, N, C = x.shape
        nw = N // WINDOW
        xw = x.reshape(B * nw, WINDOW, C)
        qkv = (xw @ W_qkv).reshape(B * nw, WINDOW, 3, NUM_HEADS, HEAD_DIM)
        q, k, v = (qkv[:, :, 0], qkv[:, :, 1], qkv[:, :, 2])
        q = _layernorm(q, ln_gamma, ln_beta)
        k = _layernorm(k, ln_gamma, ln_beta)
        attn = jnp.einsum('bqhd,bkhd->bhqk', q * SCALE, k)
        attn = jax.nn.softmax(attn, axis=-1)
        out = jnp.einsum('bhqk,bkhd->bqhd', attn, v).reshape(B * nw, WINDOW, C)
        out = out @ W_proj + b_proj
        return out.reshape(B, N, C)

    def _L0_ffn_ref(x, wqkv, q_scale, k_scale, wo, ln_g, ln_b, w1, b1, w2, b2):
        import jax, jax.numpy as jnp
        import numpy as np
        DIM = 128
        DEPTH = 2
        HEADS = 8
        DIM_HEAD = 64
        WINDOW = 64
        INNER = HEADS * DIM_HEAD
        HID = int(DIM * 4 * 2 / 3)
        B, N = (2, 1024)
        QK_SCALE = 8.0

        def shift_token(t):
            t1, t2 = jnp.split(t, 2, axis=-1)
            t2 = jnp.pad(t2, ((0, 0), (1, 0), (0, 0)))[:, :-1]
            return jnp.concatenate([t1, t2], axis=-1)

        def l2norm(t):
            return t / jnp.clip(jnp.linalg.norm(t, axis=-1, keepdims=True), 1e-12)

        def rotate_half(x):
            x1, x2 = jnp.split(x, 2, axis=-1)
            return jnp.concatenate([-x2, x1], axis=-1)

        def rotary_xpos(q, k):
            n = q.shape[-2]
            half_idx = jnp.arange(0, DIM_HEAD, 2, dtype=jnp.float32)
            inv_freq = 1.0 / 10000.0 ** (half_idx / DIM_HEAD)
            t = jnp.arange(n, dtype=jnp.float32)
            freqs = t[:, None] * inv_freq[None, :]
            freqs = jnp.concatenate([freqs, freqs], axis=-1)
            base = (half_idx + 0.4 * DIM_HEAD) / (1.4 * DIM_HEAD)
            power = (t - n // 2) / float(WINDOW // 2)
            scale = base[None, :] ** power[:, None]
            scale = jnp.concatenate([scale, scale], axis=-1)
            cos, sin = (jnp.cos(freqs), jnp.sin(freqs))
            q = q * cos * scale + rotate_half(q) * sin * scale
            k = k * cos / scale + rotate_half(k) * sin / scale
            return (q, k)

        def local_attention(q, k, v):
            b, h, n, d = q.shape
            w = n // WINDOW
            bq = q.reshape(b, h, w, WINDOW, d) * QK_SCALE
            bk = k.reshape(b, h, w, WINDOW, d)
            bv = v.reshape(b, h, w, WINDOW, d)

            def look_around(t):
                p = jnp.pad(t, ((0, 0), (0, 0), (1, 0), (0, 0), (0, 0)))
                return jnp.concatenate([p[:, :, :w], p[:, :, 1:]], axis=3)
            bk, bv = (look_around(bk), look_around(bv))
            bt = jnp.arange(n).reshape(w, WINDOW)
            btp = jnp.pad(bt, ((1, 0), (0, 0)), constant_values=-1)
            btk = jnp.concatenate([btp[:w], btp[1:]], axis=1)
            sim = jnp.einsum('bhwid,bhwjd->bhwij', bq, bk)
            i = bt[:, :, None]
            j = btk[:, None, :]
            mask = (i < j) | (i > j + WINDOW) | (j == -1)
            sim = jnp.where(mask, -jnp.finfo(sim.dtype).max, sim)
            attn = jax.nn.softmax(sim, axis=-1)
            out = jnp.einsum('bhwij,bhwjd->bhwid', attn, bv)
            return out.reshape(b, h, n, d)

        def _layer(x, wqkv, qs, ksc, wo, lg, lb, w1, b1, w2, b2):
            b, n, _ = x.shape
            h = shift_token(x)
            qkv = h @ wqkv
            q, k, v = jnp.split(qkv, 3, axis=-1)
            to_heads = lambda t: t.reshape(b, n, HEADS, DIM_HEAD).transpose(0, 2, 1, 3)
            q, k, v = (to_heads(q), to_heads(k), to_heads(v))
            q = l2norm(q) * qs
            k = l2norm(k) * ksc
            q, k = rotary_xpos(q, k)
            o = local_attention(q, k, v)
            o = o.transpose(0, 2, 1, 3).reshape(b, n, INNER)
            x = x + o @ wo
            h = shift_token(x)
            mu = h.mean(-1, keepdims=True)
            var = h.var(-1, keepdims=True)
            h = (h - mu) / jnp.sqrt(var + 1e-05) * lg + lb
            h = h @ w1 + b1
            a, g = jnp.split(h, 2, axis=-1)
            h = a * jax.nn.gelu(g, approximate=False)
            x = x + h @ w2 + b2
            return x
        for l in range(DEPTH):
            x = _layer(x, wqkv[l], q_scale[l], k_scale[l], wo[l], ln_g[l], ln_b[l], w1[l], b1[l], w2[l], b2[l])
        return x

    def _L1_attn_ref(x, u, W, b, gamma, beta):
        import jax, jax.numpy as jnp
        import numpy as np
        LN_EPS = 1e-05
        B, T, D = x.shape
        mean = jnp.mean(x, axis=-1, keepdims=True)
        var = jnp.var(x, axis=-1, keepdims=True)
        xn = (x - mean) * jax.lax.rsqrt(var + LN_EPS) * gamma + beta
        proj = jnp.einsum('btd,ed->bte', xn, W) + b
        cand, g_z, g_r = jnp.split(proj, 3, axis=-1)
        z = jax.nn.sigmoid(g_z)
        r = jax.nn.sigmoid(g_r)

        def step(s, inp):
            c_t, z_t, r_t = inp
            h_tilde = jnp.tanh(c_t + r_t * (u * s))
            s_new = z_t * s + (1.0 - z_t) * h_tilde
            return (s_new, s_new)
        s0 = jnp.zeros((B, D), dtype=x.dtype)
        _, ys = jax.lax.scan(step, s0, (cand.transpose(1, 0, 2), z.transpose(1, 0, 2), r.transpose(1, 0, 2)))
        return ys.transpose(1, 0, 2)

    def _L1_ffn_ref(x, Wg, bg, W1, b1, W2, b2):
        import jax, jax.numpy as jnp
        import numpy as np
        D = 128
        H = 512
        E = 8
        K = 2
        B, S = (4, 256)
        B_, S_, D_ = x.shape
        xt = x.reshape(-1, D_)
        logits = xt @ Wg + bg
        scores = jax.nn.softmax(logits, axis=-1)
        topk_probs, topk_idx = jax.lax.top_k(scores, K)
        h = jnp.einsum('nd,edh->enh', xt, W1) + b1[:, None, :]
        h = jax.nn.gelu(h, approximate=False)
        eo = jnp.einsum('enh,ehd->end', h, W2) + b2[:, None, :]
        eo = jnp.transpose(eo, (1, 0, 2))
        sel = jnp.take_along_axis(eo, topk_idx[:, :, None], axis=1)
        out = jnp.einsum('nk,nkd->nd', topk_probs, sel)
        return out.reshape(B_, S_, D_)
    x = L0_attn_x
    x = x + _layernorm(_L0_attn_ref(_layernorm(x, axis=-1), L0_attn_W_qkv, L0_attn_ln_gamma, L0_attn_ln_beta, L0_attn_W_proj, L0_attn_b_proj), axis=-1)
    x = x + _layernorm(_L0_ffn_ref(_layernorm(x, axis=-1), L0_ffn_wqkv, L0_ffn_q_scale, L0_ffn_k_scale, L0_ffn_wo, L0_ffn_ln_g, L0_ffn_ln_b, L0_ffn_w1, L0_ffn_b1, L0_ffn_w2, L0_ffn_b2), axis=-1)
    x = x + _layernorm(_L1_attn_ref(_layernorm(x, axis=-1), L1_attn_u, L1_attn_W, L1_attn_b, L1_attn_gamma, L1_attn_beta), axis=-1)
    x = x + _layernorm(_L1_ffn_ref(_layernorm(x, axis=-1), L1_ffn_Wg, L1_ffn_bg, L1_ffn_W1, L1_ffn_b1, L1_ffn_W2, L1_ffn_b2), axis=-1)
    return x

_drawn_inputs = setup_inputs


def setup_inputs(seed=0):
    import zlib

    import numpy as np

    out = dict(_drawn_inputs(seed))
    spreads = {'L0_attn_ln_gamma': (1.0, 0.2),
     'L0_attn_ln_beta': (0.0, 0.1),
     'L0_ffn_q_scale': (1.0, 0.6),
     'L0_ffn_k_scale': (1.0, 0.6),
     'L0_ffn_ln_g': (1.0, 0.6),
     'L0_ffn_ln_b': (0.0, 0.656),
     'L0_ffn_b1': (0.0, 0.36),
     'L0_ffn_b2': (0.0, 0.1),
     'L1_attn_gamma': (1.0, 0.2),
     'L1_attn_beta': (0.0, 0.1)}
    factors = {'L1_attn_b': 2.872}
    for name, (base, spread) in spreads.items():
        noise = np.random.default_rng([zlib.crc32(name.encode()), seed]).standard_normal(out[name].shape)
        drawn = base * np.exp(spread * noise) if base else spread * noise
        out[name] = jnp.asarray(drawn.astype(out[name].dtype))
    for name, factor in factors.items():
        out[name] = (out[name] * factor).astype(out[name].dtype)
    return out
```

```python
from contextlib import ExitStack

import numpy as np

import concourse.bass as bass
from concourse import mybir

F32 = mybir.dt.float32
BF16 = mybir.dt.bfloat16
ALU = mybir.AluOpType
ACT = mybir.ActivationFunctionType
AX = mybir.AxisListType.X
ds = bass.ds

P = 128
B, T = 8, 512
NT = B * T // P
NB = T // P
WIN = 64
NG = NT // 4
EPS = 1e-5
WH, WD = 16, 8
WP = WH // 2
LH, LD = 8, 64
LP = LH // 2
INNER = LH * LD
LAYERS = 2
HID = 341
HC = [(0, 128), (128, 128), (256, HID - 256)]
E, H, HCH = 8, 512, 4
NEG = -1e30


def pipeline(eng, count, stages):
    last = max(lag for _, lag in stages)
    for k in range(last):
        for stage, lag in stages:
            if k >= lag:
                stage(k - lag)
    with eng.Fori(last, count) as k:
        for stage, lag in stages:
            stage(k - lag)
    for k in range(count, count + last):
        for stage, lag in stages:
            if k - lag < count:
                stage(k - lag)


def window_attention(nc, ps, X, Y, x, w_qkv, ln_gamma, ln_beta, w_proj, b_proj, c_ident, c_lane):
    with ExitStack() as ctx:
        def sb(name, shape, dt=F32):
            return ctx.enter_context(nc.sbuf_tensor("wa_" + name, shape, dt))

        def sem(name):
            return nc.alloc_semaphore("wa_" + name)

        wqkv = sb("wqkv", [P, 3 * P])
        wproj = sb("wproj", [P, P])
        bproj = sb("bproj", [P, P])
        gam, bet = sb("gam", [P, WD]), sb("bet", [P, WD])
        ident, lane = sb("ident", [P, P]), sb("lane", [P, 4])
        power, epsilon = sb("power", [P, 1]), sb("epsilon", [P, 1])
        st, mv, rs = sb("st", [P, 6]), sb("mv", [P, 2]), sb("rs", [P, 1])
        ve = sb("ve", [P, 1])
        xn, xnT = sb("xn", [P, P]), sb("xnT", [P, P])
        gsum, gvar, grs = sb("gsum", [P, 2 * WH]), sb("gvar", [P, 2 * WH]), sb("grs", [P, 2 * WH])
        cen, sq, qk = sb("cen", [P, 2 * P]), sb("sq", [P, 2 * P]), sb("qk", [P, 2 * P])
        qm = sb("qm", [P, 4, P])
        kT = sb("kT", [P, P])
        vz = sb("vz", [P, 2, WP, 2, WD + 1])
        mx = sb("mx", [P, WH])
        prob = sb("prob", [P, WH, WIN])
        pT = sb("pT", [P, WP, P])
        rden = sb("rden", [P, WH])
        o, oT = sb("o", [P, P]), sb("oT", [P, P])
        y = sb("y", [P, P])
        st2, mv2, rs2, ve2 = sb("st2", [P, 6]), sb("mv2", [P, 2]), sb("rs2", [P, 1]), sb("ve2", [P, 1])
        yn = sb("yn", [P, P])
        st3, mv3, rs3, ve3 = sb("st3", [P, 6]), sb("mv3", [P, 2]), sb("rs3", [P, 1]), sb("ve3", [P, 1])

        T_XT, T_QK, T_V, T_OUT = 0, 1, 2, 3
        HH, HP = WH // 2, WP // 2

        def result_half(half):
            return ps[:, 5 + 2 * half, 0:HH * (WD + 1)].rearrange("p (h d) -> p h d", d=WD + 1)

        x_in, const_in = sem("x_in"), sem("const_in")
        zeroed = sem("zeroed")
        stats, meanvar, eps_added, rstd = sem("stats"), sem("meanvar"), sem("eps_added"), sem("rstd")
        normed, xT_ps, xT_sb = sem("normed"), sem("xT_ps"), sem("xT_sb")
        qk_ps, v_ps = sem("qk_ps"), sem("v_ps")
        summed, centred, squared, varsum = sem("summed"), sem("centred"), sem("squared"), sem("varsum")
        logged, grstd, scaled, gammad, qk_sb = sem("logged"), sem("grstd"), sem("scaled"), sem("gammad"), sem("qk_sb")
        qT_ps, kT_ps, qm_sb, kT_sb, v_sb = sem("qT_ps"), sem("kT_ps"), sem("qm_sb"), sem("kT_sb"), sem("v_sb")
        scored, maxed, shifted, expd = sem("scored"), sem("maxed"), sem("shifted"), sem("expd")
        pT_ps, pT_sb, pv_ps, recip, o_sb = sem("pT_ps"), sem("pT_sb"), sem("pv_ps"), sem("recip"), sem("o_sb")
        oT_ps, oT_sb, proj_ps, y_sb = sem("oT_ps"), sem("oT_sb"), sem("proj_ps"), sem("y_sb")
        stats2, meanvar2, eps2, rstd2, yn_sb, added = (sem("stats2"), sem("meanvar2"), sem("eps2"), sem("rstd2"),
                                                       sem("yn_sb"), sem("added"))
        stats3, meanvar3, eps3, rstd3, out = sem("stats3"), sem("meanvar3"), sem("eps3"), sem("rstd3"), sem("out")
        meaned = sem("meaned")
        N_CONST = 7

        block = ctx.enter_context(nc.Block())

        @block.sync
        def _(sp):
            for dst, src in ((wqkv[:, :], w_qkv), (ident[:, :], c_ident), (lane[:, :], c_lane),
                             (gam[:, :], ln_gamma.partition_broadcast(P)), (bet[:, :], ln_beta.partition_broadcast(P)),
                             (wproj[:, :], w_proj), (bproj[:, :], b_proj.partition_broadcast(P)),):
                sp.dma_start(dst, src).then_inc(const_in, 16)
            xv = x.rearrange("b (i p) d -> i p b d", p=P)
            for i in range(NB):
                if i:
                    sp.wait_ge(x_in, 16 * i)
                sp.dma_start(X[:, 8 * i:8 * i + 8, :], xv[i]).then_inc(x_in, 16)

        @block.gpsimd
        def _(pool):
            pool.memset(Y[:, 0:8, :], 0.0).then_inc(zeroed, 1)
            pool.memset(power[:, :], -0.5).then_inc(zeroed, 1)
            pool.memset(vz[:, :, :, :, :], 0.0).then_inc(zeroed, 1)
            pool.wait_ge(zeroed, 3)
            pool.memset(vz[0:64, :, :, 0, WD:WD + 1], 1.0).then_inc(zeroed, 1)
            pool.memset(vz[64:128, :, :, 1, WD:WD + 1], 1.0).then_inc(zeroed, 1)
            pool.wait_ge(zeroed, 5)
            pool.memset(epsilon[:, :], EPS).then_inc(zeroed, 1)
            pool.wait_ge(zeroed, 6)

            def rsqrt(mean_var, with_eps, out_, source, eps_sem, done, n):
                pool.wait_ge(source, n + 1)
                pool.tensor_tensor(with_eps[:, :], mean_var[:, 1:2], epsilon[:, :], ALU.add).then_inc(eps_sem, 1)
                pool.wait_ge(eps_sem, n + 1)
                pool.tensor_tensor(out_[:, :], with_eps[:, :], power[:, :], ALU.pow).then_inc(done, 1)

            def rsqrt_in(n):
                pool.wait_ge(normed, n)
                rsqrt(mv, ve, rs, meanvar, eps_added, rstd, n)

            def rsqrt_out(n):
                rsqrt(mv2, ve2, rs2, meanvar2, eps2, rstd2, n)

            def rsqrt_next(n):
                rsqrt(mv3, ve3, rs3, meanvar3, eps3, rstd3, n)

            pipeline(pool, NT, [(rsqrt_in, 0), (rsqrt_out, 3), (rsqrt_next, 4)])

        @block.tensor
        def _(pe):
            pe.wait_ge(const_in, 16 * N_CONST)
            pe.wait_ge(zeroed, 6)

            def turn_x(n):
                pe.wait_ge(normed, n + 1)
                pe.wait_ge(qm_sb, n)
                pe.transpose(ps[:, T_XT, 0:P], xn[:, :], ident[:, :]).then_inc(xT_ps, 1)

            def qkv(n):
                pe.wait_ge(xT_sb, n + 1)
                pe.wait_ge(kT_sb, n)
                pe.matmul(ps[:, T_QK, 0:2 * P], xnT[:, :], wqkv[:, 0:2 * P], start=True, stop=True)\
                    .then_inc(qk_ps, 1)
                pe.wait_ge(v_sb, n)
                wv = wqkv[:, 2 * P:3 * P].rearrange("p (c h d) -> p c h d", h=2, d=WD)
                for w in range(2):
                    for h in range(2):
                        mm = pe.matmul(ps[64 * h:64 * h + 64, T_V, 64 * w:64 * w + 64], xnT[:, 64 * w:64 * w + 64],
                                       wv[:, :, h, :], start=True, stop=True)
                mm.then_inc(v_ps, 1)

            def transposes(n):
                pe.wait_ge(qk_sb, n + 1)
                pe.wait_ge(xT_sb, n + 1)
                pe.transpose(ps[:, T_XT, 0:P], qk[:, 0:P], ident[:, :]).then_inc(qT_ps, 1)
                pe.transpose(ps[:, T_QK, 0:P], qk[:, P:2 * P], ident[:, :]).then_inc(kT_ps, 1)

            def score(n):
                pe.wait_ge(qm_sb, n + 1)
                pe.wait_ge(kT_sb, n + 1)
                for half in range(2):
                    pe.wait_ge(pT_sb, 2 * n)
                    pe.wait_ge(o_sb, 2 * n)
                    for j in range(4):
                        for r in (2 * half, 2 * half + 1):
                            for w in range(2):
                                mm = pe.matmul(ps[64 * w:64 * w + 64, 4 + r, WIN * j:WIN * j + WIN],
                                               qm[32 * r:32 * r + 32, j, 64 * w:64 * w + 64],
                                               kT[32 * r:32 * r + 32, 64 * w:64 * w + 64], start=True, stop=True)
                    mm.then_inc(scored, 1)

            def turn_p(n, half):
                pe.wait_ge(expd, 2 * n + 1 + half)
                for c in range(HP):
                    h = HH * half + 2 * c
                    mm = pe.transpose(ps[:, 4 + 2 * half, P * c:P * c + P],
                                      prob[:, h:h + 2, :].rearrange("p a b -> p (a b)"), ident[:, :])
                mm.then_inc(pT_ps, 1)

            def attend(n, half):
                pe.wait_ge(pT_sb, 2 * n + 1 + half)
                pe.wait_ge(v_sb, n + 1)
                for c in range(HP):
                    for w in range(2):
                        mm = pe.matmul(ps[64 * w:64 * w + 64, 5 + 2 * half, 18 * c:18 * c + 18],
                                       pT[:, HP * half + c, 64 * w:64 * w + 64],
                                       vz[:, w, HP * half + c, :, :].rearrange("p a b -> p (a b)"),
                                       start=True, stop=True)
                mm.then_inc(pv_ps, 1)

            def turn_and_attend(n):
                turn_p(n, 0)
                turn_p(n, 1)
                attend(n, 0)
                attend(n, 1)

            def turn_o(n):
                pe.wait_ge(o_sb, 2 * n + 2)
                pe.wait_ge(y_sb, n)
                pe.transpose(ps[:, T_OUT, 0:P], o[:, :], ident[:, :]).then_inc(oT_ps, 1)

            def project(n):
                pe.wait_ge(oT_sb, n + 1)
                pe.matmul(ps[:, T_OUT, P:2 * P], oT[:, :], wproj[:, :], start=True, stop=True).then_inc(proj_ps, 1)

            pipeline(pe, NT, [(score, 2), (turn_x, 1), (turn_o, 3), (qkv, 1), (project, 3), (turn_and_attend, 2),
                              (transposes, 1)])

        @block.scalar
        def _(act):
            act.preload_act_table_set("natural_log_exp_and_others")
            act.wait_ge(zeroed, 6)

            def copy_xT(n):
                act.wait_ge(xT_ps, n + 1)
                act.wait_ge(v_ps, n)
                act.copy(xnT[:, :], ps[:, T_XT, 0:P]).then_inc(xT_sb, 1)

            def exps(n, half):
                act.wait_ge(shifted, 2 * n + 1 + half)
                part = prob[:, HH * half:HH * half + HH, :]
                act.activation(part, part, ACT.Exp).then_inc(expd, 1)

            def square(n):
                act.wait_ge(centred, n + 1)
                act.activation(sq[:, :], cen[:, :], ACT.Square).then_inc(squared, 1)

            def group_rstd(n):
                act.wait_ge(varsum, n + 1)
                act.activation(gvar[:, :], gvar[:, :], ACT.Ln, bias=EPS, scale=1.0 / WD).then_inc(logged, 1)
                act.wait_ge(logged, n + 1)
                act.activation(grs[:, :], gvar[:, :], ACT.Exp, scale=-0.5).then_inc(grstd, 1)

            def copy_pT(n, half):
                act.wait_ge(pT_ps, 2 * n + 1 + half)
                act.wait_ge(pv_ps, 2 * n)
                act.copy(pT[:, HP * half:HP * half + HP, :].rearrange("p c n -> p (c n)"), ps[:, 4 + 2 * half, :])\
                    .then_inc(pT_sb, 1)

            def exps_0(n):
                exps(n, 0)

            def exps_1(n):
                exps(n, 1)

            def copy_pT_0(n):
                copy_pT(n, 0)

            def copy_pT_1(n):
                copy_pT(n, 1)

            def copy_oT(n):
                act.wait_ge(oT_ps, n + 1)
                act.wait_ge(proj_ps, n)
                act.copy(oT[:, :], ps[:, T_OUT, 0:P]).then_inc(oT_sb, 1)

            def copy_v(n):
                act.wait_ge(v_ps, n + 1)
                act.wait_ge(pv_ps, 2 * n)
                for h in range(2):
                    rows = slice(64 * h, 64 * h + 64)
                    src = ps[rows, T_V, 0:2 * 64].rearrange("p (w c d) -> p w c d", w=2, d=WD)
                    last = act.copy(vz[rows, :, :, h, 0:WD], src)
                last.then_inc(v_sb, 1)

            def copy_kT(n):
                act.wait_ge(kT_ps, n + 1)
                act.wait_ge(scored, 2 * n)
                act.copy(kT[:, :], ps[:, T_QK, 0:P]).then_inc(kT_sb, 1)

            pipeline(act, NT, [(copy_xT, 1), (copy_oT, 3), (exps_0, 2), (square, 1), (exps_1, 2), (group_rstd, 1),
                               (copy_pT_0, 2), (copy_pT_1, 2), (copy_v, 1), (copy_kT, 1)])

        @block.vector
        def _(dve):
            dve.wait_ge(const_in, 16 * N_CONST)

            def normalize(n):
                dve.wait_ge(rstd, n + 1)
                dve.wait_ge(xT_ps, n)
                dve.tensor_scalar(xn[:, :], X[:, ds(n, 1), :].rearrange("p a d -> p (a d)"), mv[:, 0:1], rs[:, :],
                                  ALU.subtract, ALU.mult).then_inc(normed, 1)

            def input_stats(n):
                dve.wait_ge(const_in, 16)
                dve.wait_ge(x_in, 16 * (n // 8 + 1))
                dve.wait_ge(normed, n)
                dve.bn_stats(st[:, :], X[:, ds(n, 1), :].rearrange("p a d -> p (a d)")).then_inc(stats, 1)
                dve.wait_ge(const_in, 16)
                dve.wait_ge(stats, n + 1)
                dve.bn_aggr(mv[:, :], st[:, :]).then_inc(meanvar, 1)

            qk3 = ps[:, T_QK, 0:2 * P].rearrange("p (g d) -> p g d", d=WD)

            def g3(t):
                return t[:, :].rearrange("p (g d) -> p g d", d=WD)

            def wide(t):
                return t[:, :].unsqueeze(2).to_broadcast([P, 2 * WH, WD])

            def centre(n):
                dve.wait_ge(qk_ps, n + 1)
                dve.tensor_reduce(gsum[:, :], qk3, AX, ALU.add).then_inc(summed, 1)
                dve.wait_ge(summed, n + 1)
                dve.tensor_scalar(gsum[:, :], gsum[:, :], 1.0 / WD, None, ALU.mult).then_inc(meaned, 1)
                dve.wait_ge(meaned, n + 1)
                dve.tensor_tensor(g3(cen), qk3, wide(gsum), ALU.subtract).then_inc(centred, 1)

            def group_variance(n):
                dve.wait_ge(squared, n + 1)
                dve.wait_ge(grstd, n)
                dve.tensor_reduce(gvar[:, :], g3(sq), AX, ALU.add).then_inc(varsum, 1)

            def qk_normal(n):
                dve.wait_ge(grstd, n + 1)
                dve.tensor_tensor(g3(cen), g3(cen), wide(grs), ALU.mult).then_inc(scaled, 1)
                dve.wait_ge(scaled, n + 1)
                dve.tensor_tensor(g3(cen), g3(cen), gam[:, :].unsqueeze(1).to_broadcast([P, 2 * WH, WD]),
                                  ALU.mult).then_inc(gammad, 1)
                dve.wait_ge(gammad, n + 1)
                dve.wait_ge(kT_ps, n)
                dve.tensor_tensor(g3(qk), g3(cen), bet[:, :].unsqueeze(1).to_broadcast([P, 2 * WH, WD]),
                                  ALU.add).then_inc(qk_sb, 1)

            def mask_q(n):
                dve.wait_ge(qT_ps, n + 1)
                dve.wait_ge(scored, 2 * n)
                dve.tensor_tensor(qm[:, :, :], ps[:, T_XT, 0:P].unsqueeze(1).to_broadcast([P, 4, P]),
                                  lane[:, :].unsqueeze(2).to_broadcast([P, 4, P]), ALU.mult).then_inc(qm_sb, 1)

            def softmax_shift(n, half):
                s4 = ps[:, 4 + 2 * half:6 + 2 * half, 0:4 * WIN].rearrange("p r (j k) -> p r j k", k=WIN)
                heads = slice(HH * half, HH * half + HH)
                mx4 = mx[:, heads].rearrange("p (r j) -> p r j", j=4)
                dve.wait_ge(scored, 2 * n + 1 + half)
                dve.tensor_reduce(mx4, s4, AX, ALU.max).then_inc(maxed, 1)
                dve.wait_ge(maxed, 2 * n + 1 + half)
                dve.wait_ge(pT_ps, 2 * n)
                dve.tensor_tensor(prob[:, heads, :].rearrange("p (r j) k -> p r j k", j=4), s4,
                                  mx4.unsqueeze(3).to_broadcast([P, 2, 4, WIN]), ALU.subtract).then_inc(shifted, 1)

            def softmax_shift_0(n):
                softmax_shift(n, 0)

            def softmax_shift_1(n):
                softmax_shift(n, 1)

            def divide(n, half):
                heads = slice(HH * half, HH * half + HH)
                dve.wait_ge(pv_ps, 2 * n + 1 + half)
                dve.reciprocal(rden[:, heads].unsqueeze(2), result_half(half)[:, :, WD:WD + 1]).then_inc(recip, 1)
                dve.wait_ge(recip, 2 * n + 1 + half)
                dve.wait_ge(oT_ps, n)
                dve.tensor_tensor(o[:, :].rearrange("p (h d) -> p h d", d=WD)[:, heads, :],
                                  result_half(half)[:, :, 0:WD],
                                  rden[:, heads].unsqueeze(2).to_broadcast([P, HH, WD]), ALU.mult).then_inc(o_sb, 1)

            def divide_0(n):
                divide(n, 0)

            def divide_1(n):
                divide(n, 1)

            def result_stats(n):
                dve.wait_ge(proj_ps, n + 1)
                dve.wait_ge(yn_sb, n)
                dve.tensor_tensor(y[:, :], ps[:, T_OUT, P:2 * P], bproj[:, :], ALU.add).then_inc(y_sb, 1)
                dve.wait_ge(const_in, 16)
                dve.wait_ge(y_sb, n + 1)
                dve.bn_stats(st2[:, :], y[:, :]).then_inc(stats2, 1)
                dve.wait_ge(const_in, 16)
                dve.wait_ge(stats2, n + 1)
                dve.bn_aggr(mv2[:, :], st2[:, :]).then_inc(meanvar2, 1)

            def add_result(n):
                Xn = X[:, ds(n, 1), :].rearrange("p a d -> p (a d)")
                dve.wait_ge(rstd2, n + 1)
                dve.tensor_scalar(yn[:, :], y[:, :], mv2[:, 0:1], rs2[:, :], ALU.subtract, ALU.mult)\
                    .then_inc(yn_sb, 1)
                dve.wait_ge(yn_sb, n + 1)
                dve.tensor_tensor(Xn, Xn, yn[:, :], ALU.add).then_inc(added, 1)
                dve.wait_ge(const_in, 16)
                dve.wait_ge(added, n + 1)
                dve.bn_stats(st3[:, :], Xn).then_inc(stats3, 1)
                dve.wait_ge(const_in, 16)
                dve.wait_ge(stats3, n + 1)
                dve.wait_ge(out, n)
                dve.bn_aggr(mv3[:, :], st3[:, :]).then_inc(meanvar3, 1)

            def next_input(n):
                dve.wait_ge(rstd3, n + 1)
                dve.tensor_scalar(Y[:, ds(n + 8, 1), :].rearrange("p a d -> p (a d)"),
                                  X[:, ds(n, 1), :].rearrange("p a d -> p (a d)"), mv3[:, 0:1], rs3[:, :],
                                  ALU.subtract, ALU.mult).then_inc(out, 1)

            pipeline(dve, NT, [(softmax_shift_0, 3), (centre, 2), (softmax_shift_1, 3), (group_variance, 2),
                               (input_stats, 1), (next_input, 6), (qk_normal, 2), (add_result, 5), (divide_0, 3),
                               (result_stats, 4), (divide_1, 3), (mask_q, 2), (normalize, 1)])
            dve.wait_ge(out, NT)


def local_transformer(nc, ps, Y, A, w_qkv, q_scale, k_scale, w_o, ln_g, ln_b, w_1, b_1, w_2, b_2,
                      c_ident, c_shift, c_carry, c_masks, c_rot):
    with ExitStack() as ctx:
        def sb(name, shape, dt=F32):
            return ctx.enter_context(nc.sbuf_tensor("lt_" + name, shape, dt))

        def sem(name):
            return nc.alloc_semaphore("lt_" + name)

        ident, shift, carry = sb("ident", [P, P]), sb("shift", [P, P]), sb("carry", [P, P])
        ident16 = sb("ident16", [P, P], BF16)
        masks = sb("masks", [P, NB + 1, P])
        masks16 = sb("masks16", [P, NB + 1, LP * P], BF16)
        rot_base, rot = sb("rot_base", [P, NB, 4 * LD]), sb("rot", [P, NB, 2, 2, LD])
        qk_scale = sb("qk_scale", [P, 2, 2, LD])
        wqkv, wo = sb("wqkv", [P, 3 * INNER]), sb("wo", [P, 4, P])
        h, hT = sb("h", [P, P]), sb("hT", [P, P])
        sq = sb("sq", [P, 2 * INNER])
        ssum, rn = sb("ssum", [P, 2 * LH]), sb("rn", [P, 2 * LH])
        unit = sb("unit", [P, 2 * INNER])
        t_cos, t_sin = sb("t_cos", [P, 2 * INNER]), sb("t_sin", [P, 2 * INNER])
        qz = sb("qz", [P, LP, 2, 2, WIN])
        kT = sb("kT", [P, LP, P])
        k_last = sb("k_last", [P, 8, LP, WIN])
        v_next, v = sb("v_next", [P, INNER]), sb("v", [P, LH, LD + 1])
        v_pair = sb("v_pair", [P, 8, LH, LD + 1])
        mx = sb("mx", [P, 2, LP])
        prob, pT = sb("prob", [P, 2, LP, P]), sb("pT", [P, 2, LP * P])
        rden = sb("rden", [P, LH])
        o, oT = sb("o", [P, INNER]), sb("oT", [P, INNER])
        w1, w2 = sb("w1", [P, 2 * HID]), sb("w2", [P, 3, P])
        b1a, b1g = sb("b1a", [P, 3]), sb("b1g", [P, 3])
        lg, lb, b2 = sb("lg", [P, 1]), sb("lb", [P, 1]), sb("b2", [P, P])
        mean, var, eps4, power4 = sb("mean", [P, 4]), sb("var", [P, 4]), sb("eps4", [P, 4]), sb("power4", [P, 4])
        frs = sb("frs", [P, 4])
        cen, fsq, hn = sb("cen", [P, 4, P]), sb("fsq", [P, 4 * P]), sb("hn", [P, 4, P])
        fT = sb("fT", [P, 4 * P])
        gate, hid = sb("gate", [P, 2, 4 * P]), sb("hid", [P, 3, 4 * P])
        ab2 = sb("ab2", [P, 4, P])

        T_H, T_QK, T_V, T_S, T_O = 0, 1, 3, 4, 6
        F_H, F_T, F_A, F_G, F_Y = 0, 1, 2, 4, 6

        zeroed, const_in, const16 = sem("zeroed"), sem("const_in"), sem("const16")
        attn_w, ffn_w, rot_ready = sem("attn_w"), sem("ffn_w"), sem("rot_ready")
        cleared = sem("cleared")
        h_ps, h_sb, hT_ps, hT_sb, qk_ps, v_ps = (sem("h_ps"), sem("h_sb"), sem("hT_ps"), sem("hT_sb"), sem("qk_ps"),
                                                sem("v_ps"))
        squared, summed, clipped, logged, rnorm, united = (sem("squared"), sem("summed"), sem("clipped"),
                                                           sem("logged"), sem("rnorm"), sem("united"))
        cos_done, sin_done, roped, qkT_ps, q_sb, k_sb, v_sb = (sem("cos_done"), sem("sin_done"), sem("roped"),
                                                               sem("qkT_ps"), sem("q_sb"), sem("k_sb"), sem("v_sb"))
        v_moved = sem("v_moved")
        k_carried, v_carried = sem("k_carried"), sem("v_carried")
        scored, maxed, shifted, expd = sem("scored"), sem("maxed"), sem("shifted"), sem("expd")
        pT_ps, pT_sb, pv_ps, recip, o_sb = sem("pT_ps"), sem("pT_sb"), sem("pv_ps"), sem("recip"), sem("o_sb")
        oT_ps, oT_sb, wo_ps, a_sb = sem("oT_ps"), sem("oT_sb"), sem("wo_ps"), sem("a_sb")
        fh_ps, fmean, fscaled, fcen, fsqd, fvar, feps, frstd, fhn, fT_ps, fT_sb = (
            sem("fh_ps"), sem("fmean"), sem("fscaled"), sem("fcen"), sem("fsqd"), sem("fvar"), sem("feps"),
            sem("frstd"), sem("fhn"), sem("fT_ps"), sem("fT_sb"))
        fa_ps, gelu_sb, hid_sb, fy_ps, ab2_sb, y_sb = (sem("fa_ps"), sem("gelu_sb"), sem("hid_sb"), sem("fy_ps"),
                                                       sem("ab2_sb"), sem("y_sb"))
        N_CONST, N_ATTN_W, N_FFN_W, N_ZERO = 5, 8, 13, 8

        block = ctx.enter_context(nc.Block())

        @block.sync
        def _(sp):
            for dst, src in ((ident[:, :], c_ident), (shift[:, :], c_shift), (carry[:, :], c_carry),
                             (masks[:, :, :], c_masks.rearrange("p (i k) -> p i k", k=P)),
                             (rot_base[:, :, :], c_rot.rearrange("p (i k) -> p i k", i=NB))):
                sp.dma_start(dst, src).then_inc(const_in, 16)
            half = LD // 2
            with sp.Fori(0, LAYERS) as l:
                sp.wait_ge(a_sb, l * NT)
                one = ds(l, 1)
                sp.dma_start(wqkv[:, :], w_qkv[one, :, :].rearrange("a p n -> (a p) n")).then_inc(attn_w, 16)
                sp.dma_start(wo[:, :, :], w_o[one, :, :].rearrange("a (c p) n -> p (a c) n", p=P)).then_inc(attn_w, 16)
                for i, scale in enumerate((q_scale, k_scale)):
                    row = scale[one, :]
                    sp.dma_start(qk_scale[:, 0, i, :], row.to_broadcast([P, LD])).then_inc(attn_w, 16)
                    sp.dma_start(qk_scale[:, 1, i, 0:half], scale[one, half:LD].to_broadcast([P, half]))\
                        .then_inc(attn_w, 16)
                    sp.dma_start(qk_scale[:, 1, i, half:LD], scale[one, 0:half].to_broadcast([P, half]))\
                        .then_inc(attn_w, 16)
                sp.wait_ge(y_sb, l * NG)
                sp.dma_start(w1[:, :], w_1[one, :, :].rearrange("a p n -> (a p) n")).then_inc(ffn_w, 16)
                for c, (at, size) in enumerate(HC):
                    sp.dma_start(w2[0:size, c, :], w_2[one, at:at + size, :].rearrange("a p n -> (a p) n"))\
                        .then_inc(ffn_w, 16)
                    sp.dma_start(b1a[0:size, c:c + 1], b_1[one, at:at + size].rearrange("a p -> p a"))\
                        .then_inc(ffn_w, 16)
                    sp.dma_start(b1g[0:size, c:c + 1], b_1[one, HID + at:HID + at + size].rearrange("a p -> p a"))\
                        .then_inc(ffn_w, 16)
                sp.dma_start(lg[:, :], ln_g[one, :].rearrange("a p -> p a")).then_inc(ffn_w, 16)
                sp.dma_start(lb[:, :], ln_b[one, :].rearrange("a p -> p a")).then_inc(ffn_w, 16)
                sp.dma_start(b2[:, :], b_2[one, :].to_broadcast([P, P])).then_inc(ffn_w, 16)

        @block.gpsimd
        def _(pool):
            pool.memset(A[:, 0:8, :], 0.0).then_inc(zeroed, 1)
            pool.memset(qz[:, :, :, :, :], 0.0).then_inc(zeroed, 1)
            pool.memset(v[:, :, LD:LD + 1], 1.0).then_inc(zeroed, 1)
            pool.memset(v_pair[:, :, :, LD:LD + 1], 1.0).then_inc(zeroed, 1)
            pool.memset(eps4[:, :], EPS * P).then_inc(zeroed, 1)
            pool.memset(power4[:, :], -0.5).then_inc(zeroed, 1)
            pool.memset(k_last[:, :, :, :], 0.0).then_inc(zeroed, 1)
            pool.wait_ge(zeroed, N_ZERO - 1)
            pool.memset(v_pair[64:128, :, :, 0:LD], 0.0).then_inc(zeroed, 1)
            pool.wait_ge(zeroed, N_ZERO)
            half = LD // 2

            with pool.Fori(0, LAYERS) as l:
                pool.wait_ge(rot_ready, l + 1)

                def rotate(n):
                    m = l * NT + n
                    pool.wait_ge(united, m + 1)
                    pool.wait_ge(scored, 2 * m)
                    pool.wait_ge(roped, m)
                    u = unit[:, :].rearrange("p (a h d) -> p a h d", a=2, d=LD)
                    t = t_sin[:, :].rearrange("p (a h d) -> p a h d", a=2, d=LD)
                    r = rot[:, ds(n // 8, 1), 1, :, :].rearrange("p i a d -> p (i a) d")
                    for to, frm in ((slice(0, half), slice(half, LD)), (slice(half, LD), slice(0, half))):
                        pool.tensor_tensor(t[:, :, :, to], u[:, :, :, frm],
                                           r[:, :, to].unsqueeze(2).to_broadcast([P, 2, LH, half]), ALU.mult)\
                            .then_inc(sin_done, 1)

                def carry_k(n):
                    if isinstance(n, int) and n == NT - 1:
                        return
                    pool.tensor_copy(k_last[:, ds(n % 8, 1), :, :].rearrange("p a c k -> p (a c) k"),
                                     kT[:, :, WIN:P]).then_inc(k_carried, 1)

                pipeline(pool, NT, [(rotate, 0), (carry_k, 1)])

                def rsqrt(g):
                    m = l * NG + g
                    pool.wait_ge(fvar, m + 1)
                    pool.tensor_tensor(frs[:, :], var[:, :], eps4[:, :], ALU.add).then_inc(feps, 1)
                    pool.wait_ge(feps, m + 1)
                    pool.tensor_tensor(frs[:, :], frs[:, :], power4[:, :], ALU.pow).then_inc(frstd, 1)

                def add_b2(g):
                    m = l * NG + g
                    pool.wait_ge(y_sb, m)
                    pool.tensor_tensor(ab2[:, :, :], A[:, ds(8 + 4 * g, 4), :],
                                       b2[:, :].unsqueeze(1).to_broadcast([P, 4, P]), ALU.add).then_inc(ab2_sb, 1)

                pool.wait_ge(ffn_w, 16 * N_FFN_W * (l + 1))
                pipeline(pool, NG, [(rsqrt, 0), (add_b2, 1)])

        @block.tensor
        def _(pe):
            pe.wait_ge(const_in, 16 * N_CONST)
            pe.wait_ge(const16, 2)
            pe.wait_ge(zeroed, N_ZERO)
            with pe.Fori(0, LAYERS) as l:
                pe.wait_ge(attn_w, 16 * N_ATTN_W * (l + 1))
                pe.wait_ge(y_sb, l * NG)

                def tokens(src, n, count, half):
                    return src[:, ds(n, count), 64 * half:64 * half + 64]

                def shift_h(n):
                    m = l * NT + n
                    pe.wait_ge(a_sb, l * NT if isinstance(n, int) and n < 3 else m - 3)
                    pe.wait_ge(hT_sb, m)
                    one = "p a d -> p (a d)"
                    pe.matmul(ps[:, T_H, 0:64], ident[:, :], tokens(Y, n + 8, 1, 0).rearrange(one),
                              start=True, stop=True)
                    pe.matmul(ps[:, T_H, 64:128], shift[:, :], tokens(Y, n + 8, 1, 1).rearrange(one),
                              start=True, stop=False)
                    pe.matmul(ps[:, T_H, 64:128], carry[:, :], tokens(Y, n, 1, 1).rearrange(one),
                              start=False, stop=True).then_inc(h_ps, 1)

                def turn_h(n):
                    m = l * NT + n
                    pe.wait_ge(h_sb, m + 1)
                    pe.transpose(ps[:, T_H, P:2 * P], h[:, :], ident[:, :]).then_inc(hT_ps, 1)

                def qk(n):
                    m = l * NT + n
                    pe.wait_ge(hT_sb, m + 1)
                    pe.wait_ge(k_sb, m)
                    pe.wait_ge(q_sb, 2 * m)
                    for i in range(2):
                        mm = pe.matmul(ps[:, T_QK + i, :], hT[:, :], wqkv[:, i * INNER:(i + 1) * INNER],
                                       start=True, stop=True)
                    mm.then_inc(qk_ps, 1)

                def values(n):
                    m = l * NT + n
                    pe.wait_ge(hT_sb, m + 1)
                    pe.wait_ge(oT_sb, l * NT if isinstance(n, int) and n < 2 else m - 2)
                    pe.matmul(ps[:, T_V, :], hT[:, :], wqkv[:, 2 * INNER:3 * INNER], start=True, stop=True)\
                        .then_inc(v_ps, 1)

                def turn_qk(n):
                    m = l * NT + n
                    pe.wait_ge(roped, m + 1)
                    for c in range(8):
                        mm = pe.transpose(ps[:, T_QK + c // 4, P * (c % 4):P * (c % 4) + P],
                                          t_cos[:, P * c:P * c + P], ident[:, :])
                    mm.then_inc(qkT_ps, 1)

                def score(n):
                    m = l * NT + n
                    pe.wait_ge(q_sb, 2 * m + 2)
                    pe.wait_ge(k_sb, m + 1)
                    for w in range(2):
                        pe.wait_ge(pT_sb, 2 * m)
                        i = NB if w else n // 8
                        pe.matmul(ps[:, T_S + w, :], ident16[:, :],
                                  masks16[:, ds(i, 1), :].rearrange("p a k -> p (a k)"),
                                  start=True, stop=False, skip_group_check=True)
                        for c in range(LP):
                            q = qz[:, c, w, :, :].rearrange("p a k -> p (a k)")
                            out = ps[:, T_S + w, P * c:P * c + P]
                            if w:
                                mm = pe.matmul(out, q, kT[:, c, :], start=False, stop=True, skip_group_check=True)
                                continue
                            if c == 0:
                                pe.wait_ge(k_carried, l * (NT - 1) + n)
                                pe.wait_ge(cleared, 2 * l)
                            pe.matmul(out[:, 0:WIN], q, kT[:, c, 0:WIN], start=False, stop=True,
                                      skip_group_check=True)
                            mm = pe.matmul(out[:, WIN:P], q,
                                           k_last[:, ds(n % 8, 1), c, :].rearrange("p a k -> p (a k)"),
                                           start=False, stop=True, skip_group_check=True)
                        mm.then_inc(scored, 1)

                def turn_p(n, w):
                    m = l * NT + n
                    pe.wait_ge(expd, 2 * m + 1 + w)
                    for c in range(LP):
                        mm = pe.transpose(ps[:, T_S + w, P * c:P * c + P], prob[:, w, c, :], ident[:, :])
                    mm.then_inc(pT_ps, 1)

                def turn_p_0(n):
                    turn_p(n, 0)

                def turn_p_1(n):
                    turn_p(n, 1)

                def attend(n):
                    m = l * NT + n
                    pe.wait_ge(v_moved, m + 1)
                    pe.wait_ge(v_sb, 2 * m + 2)
                    pe.wait_ge(cleared, 2 * l)
                    pe.wait_ge(v_carried, m)
                    pe.wait_ge(o_sb, m)
                    for w in range(2):
                        pe.wait_ge(pT_sb, 2 * m + 1 + w)
                        for i in range(LH):
                            out = ps[64 * w:64 * w + 64, T_O + i // 4, 65 * (i % 4):65 * (i % 4) + 65]
                            rhs = v[:, i, :] if w else \
                                v_pair[:, ds(n % 8, 1), i, :].rearrange("p a d -> p (a d)")
                            mm = pe.matmul(out, pT[:, w, WIN * i:WIN * i + WIN], rhs, start=True, stop=True)
                        mm.then_inc(pv_ps, 1)

                def turn_o(n):
                    m = l * NT + n
                    pe.wait_ge(o_sb, m + 1)
                    ahead = min(n + 2, NT - 1) if isinstance(n, int) else n + 2
                    pe.wait_ge(v_sb, 2 * (l * NT + ahead) + 2)
                    for c in range(4):
                        mm = pe.transpose(ps[:, T_V, P * c:P * c + P], o[:, P * c:P * c + P], ident[:, :])
                    mm.then_inc(oT_ps, 1)

                def project(n):
                    m = l * NT + n
                    ahead = min(n + 4, NT) if isinstance(n, int) else n + 4
                    pe.wait_ge(hT_sb, l * NT + ahead)
                    pe.wait_ge(oT_sb, m + 1)
                    for c in range(4):
                        mm = pe.matmul(ps[:, T_H, 2 * P:3 * P], oT[:, P * c:P * c + P], wo[:, c, :],
                                       start=(c == 0), stop=(c == 3))
                    mm.then_inc(wo_ps, 1)

                pipeline(pe, NT, [(values, 1), (qk, 1), (score, 2), (shift_h, 0), (turn_o, 3), (turn_h, 0),
                                  (turn_p_0, 2), (project, 3), (turn_p_1, 2), (attend, 2), (turn_qk, 1)])

                pe.wait_ge(a_sb, (l + 1) * NT)
                pe.wait_ge(ffn_w, 16 * N_FFN_W * (l + 1))

                def f_shift(g):
                    m = l * NG + g
                    pe.wait_ge(fcen, m)
                    out = ps[:, F_H, :].rearrange("p (t d) -> p t d", d=P)
                    pe.matmul(out[:, :, 0:64], ident[:, :], tokens(A, 4 * g + 8, 4, 0), start=True, stop=True)
                    pe.matmul(out[:, :, 64:128], shift[:, :], tokens(A, 4 * g + 8, 4, 1), start=True, stop=False)
                    pe.matmul(out[:, :, 64:128], carry[:, :], tokens(A, 4 * g, 4, 1), start=False, stop=True)\
                        .then_inc(fh_ps, 1)

                def f_turn(g):
                    m = l * NG + g
                    pe.wait_ge(fhn, m + 1)
                    pe.wait_ge(fT_sb, m)
                    for t in range(4):
                        mm = pe.transpose(ps[:, F_T, P * t:P * t + P], hn[:, t, :], ident[:, :])
                    mm.then_inc(fT_ps, 1)

                def f_up(g):
                    m = l * NG + g
                    pe.wait_ge(fT_sb, m + 1)
                    for c, (at, size) in enumerate(HC):
                        pe.wait_ge(hid_sb, 3 * m + (c - 1 if c else 0))
                        for bank, col in ((F_A, at), (F_G, HID + at)):
                            mm = pe.matmul(ps[0:size, bank + c % 2, :], w1[:, col:col + size], fT[:, :],
                                           start=True, stop=True)
                        mm.then_inc(fa_ps, 1)

                def f_down(g):
                    m = l * NG + g
                    pe.wait_ge(hid_sb, 3 * m + 3)
                    pe.wait_ge(y_sb, m)
                    for t in range(4):
                        for c, (at, size) in enumerate(HC):
                            mm = pe.matmul(ps[:, F_Y, P * t:P * t + P], hid[0:size, c, P * t:P * t + P],
                                           w2[0:size, c, :], start=(c == 0), stop=(c == 2))
                    mm.then_inc(fy_ps, 1)

                pipeline(pe, NG, [(f_turn, 1), (f_shift, 0), (f_up, 1), (f_down, 1)])

        @block.scalar
        def _(act):
            act.wait_ge(zeroed, N_ZERO)
            with act.Fori(0, LAYERS) as l:
                act.preload_act_table_set("natural_log_exp_and_others")

                def copy_h(n):
                    m = l * NT + n
                    act.wait_ge(h_ps, m + 1)
                    act.wait_ge(hT_ps, m)
                    act.copy(h[:, :], ps[:, T_H, 0:P]).then_inc(h_sb, 1)

                def copy_hT(n):
                    m = l * NT + n
                    act.wait_ge(hT_ps, m + 1)
                    act.wait_ge(qk_ps, m)
                    act.wait_ge(v_ps, m)
                    act.copy(hT[:, :], ps[:, T_H, P:2 * P]).then_inc(hT_sb, 1)

                def square(n):
                    m = l * NT + n
                    act.wait_ge(qk_ps, m + 1)
                    act.wait_ge(summed, m)
                    act.activation(sq[:, :], ps[:, T_QK:T_QK + 2, :].rearrange("p a n -> p (a n)"), ACT.Square)\
                        .then_inc(squared, 1)

                def rnorms(n):
                    m = l * NT + n
                    act.wait_ge(clipped, m + 1)
                    act.activation(rn[:, :], ssum[:, :], ACT.Ln).then_inc(logged, 1)
                    act.wait_ge(logged, m + 1)
                    act.activation(rn[:, :], rn[:, :], ACT.Exp, scale=-0.5).then_inc(rnorm, 1)

                def exps(n, w):
                    m = l * NT + n
                    act.wait_ge(shifted, 2 * m + 1 + w)
                    part = prob[:, w, :, :]
                    act.activation(part, part, ACT.Exp).then_inc(expd, 1)

                def exps_0(n):
                    exps(n, 0)

                def exps_1(n):
                    exps(n, 1)

                def copy_pT(n):
                    m = l * NT + n
                    for w in range(2):
                        act.wait_ge(pT_ps, 2 * m + 1 + w)
                        act.wait_ge(pv_ps, 2 * m)
                        act.copy(pT[:, w, :], ps[:, T_S + w, :]).then_inc(pT_sb, 1)

                def copy_v(n):
                    m = l * NT + n
                    act.wait_ge(v_ps, m + 1)
                    act.wait_ge(v_moved, m)
                    vv = ps[:, T_V, :].rearrange("p (h d) -> p h d", d=LD)
                    act.copy(v_next[:, :], ps[:, T_V, :]).then_inc(v_sb, 1)
                    act.copy(v_pair[0:64, ds(n % 8, 1), :, 0:LD].rearrange("p a h d -> p (a h) d"), vv[0:64, :, :])\
                        .then_inc(v_sb, 1)

                def carry_v(n):
                    m = l * NT + n
                    act.wait_ge(v_moved, m + 1)
                    act.wait_ge(pv_ps, 2 * m + 2)
                    act.copy(v_pair[64:128, ds(n % 8, 1), :, 0:LD].rearrange("p a h d -> p (a h) d"),
                             v[64:128, :, 0:LD]).then_inc(v_carried, 1)

                def move_v(n):
                    m = l * NT + n
                    act.wait_ge(v_sb, 2 * m + 2)
                    act.wait_ge(v_carried, m)
                    act.copy(v[:, :, 0:LD], v_next[:, :].rearrange("p (h d) -> p h d", d=LD)).then_inc(v_moved, 1)

                def copy_q(n):
                    m = l * NT + n
                    act.wait_ge(qkT_ps, m + 1)
                    act.wait_ge(scored, 2 * m)
                    qT = ps[:, T_QK, :].rearrange("p (c w k) -> p c w k", c=LP, w=2)
                    for i in range(2):
                        rows = slice(64 * i, 64 * i + 64)
                        act.copy(qz[rows, :, :, i, :], qT[rows, :, :, :]).then_inc(q_sb, 1)

                def copy_oT(n):
                    m = l * NT + n
                    act.wait_ge(oT_ps, m + 1)
                    act.wait_ge(wo_ps, m)
                    act.copy(oT[:, :], ps[:, T_V, :]).then_inc(oT_sb, 1)

                pipeline(act, NT, [(copy_v, 1), (square, 1), (rnorms, 1), (copy_h, 0), (copy_oT, 3),
                                   (copy_hT, 0), (exps_0, 2), (exps_1, 2), (copy_pT, 2), (copy_q, 1), (carry_v, 2),
                                   (move_v, 1)])

                act.preload_act_table_set("gelu_and_others")
                act.wait_ge(ffn_w, 16 * N_FFN_W * (l + 1))

                def f_square(g):
                    m = l * NG + g
                    act.wait_ge(fcen, m + 1)
                    act.wait_ge(fvar, m)
                    act.activation(fsq[:, :], cen[:, :, :].rearrange("p t d -> p (t d)"), ACT.Square)\
                        .then_inc(fsqd, 1)

                def f_copy(g):
                    m = l * NG + g
                    act.wait_ge(fT_ps, m + 1)
                    act.wait_ge(fa_ps, 3 * m)
                    act.activation(fT[:, :], ps[:, F_T, :], ACT.Identity, bias=lb[:, :], scale=lg[:, :])\
                        .then_inc(fT_sb, 1)

                def f_gelu(g):
                    m = l * NG + g
                    for c, (at, size) in enumerate(HC):
                        act.wait_ge(fa_ps, 3 * m + c + 1)
                        act.wait_ge(hid_sb, 3 * m + (c - 1 if c else 0))
                        act.activation(gate[0:size, c % 2, :], ps[0:size, F_G + c % 2, :], ACT.Gelu,
                                       bias=b1g[0:size, c:c + 1]).then_inc(gelu_sb, 1)

                pipeline(act, NG, [(f_copy, 1), (f_square, 0), (f_gelu, 1)])

        @block.vector
        def _(dve):
            dve.wait_ge(const_in, 16 * N_CONST)
            dve.tensor_copy(ident16[:, :], ident[:, :]).then_inc(const16, 1)
            dve.tensor_copy(masks16[:, :, :].rearrange("p i (c k) -> p i c k", c=LP),
                            masks[:, :, :].unsqueeze(2).to_broadcast([P, NB + 1, LP, P])).then_inc(const16, 1)
            with dve.Fori(0, LAYERS) as l:
                dve.wait_ge(attn_w, 16 * N_ATTN_W * (l + 1))
                dve.tensor_tensor(rot[:, :, :, :, :].rearrange("p i a b d -> p i (a b d)"), rot_base[:, :, :],
                                  qk_scale[:, :, :, :].rearrange("p a b d -> p (a b d)").unsqueeze(1)
                                  .to_broadcast([P, NB, 4 * LD]), ALU.mult).then_inc(rot_ready, 1)
                dve.wait_ge(rot_ready, l + 1)

                def norm_squares(n):
                    m = l * NT + n
                    dve.wait_ge(squared, m + 1)
                    dve.wait_ge(rnorm, m)
                    dve.tensor_reduce(ssum[:, :], sq[:, :].rearrange("p (g d) -> p g d", d=LD), AX, ALU.add)\
                        .then_inc(summed, 1)
                    dve.wait_ge(summed, m + 1)
                    dve.tensor_scalar(ssum[:, :], ssum[:, :], 1e-24, None, ALU.max).then_inc(clipped, 1)

                def unit_qk(n):
                    m = l * NT + n
                    dve.wait_ge(rnorm, m + 1)
                    dve.wait_ge(sin_done, 2 * m)
                    dve.tensor_tensor(unit[:, :].rearrange("p (g d) -> p g d", d=LD),
                                      ps[:, T_QK:T_QK + 2, :].rearrange("p a (h d) -> p (a h) d", d=LD),
                                      rn[:, :].unsqueeze(2).to_broadcast([P, 2 * LH, LD]), ALU.mult)\
                        .then_inc(united, 1)

                def cosines(n):
                    m = l * NT + n
                    dve.wait_ge(united, m + 1)
                    dve.wait_ge(qkT_ps, m)
                    r = rot[:, ds(n // 8, 1), 0, :, :].rearrange("p i a d -> p (i a) d")
                    dve.tensor_tensor(t_cos[:, :].rearrange("p (a h d) -> p a h d", a=2, d=LD),
                                      unit[:, :].rearrange("p (a h d) -> p a h d", a=2, d=LD),
                                      r.unsqueeze(2).to_broadcast([P, 2, LH, LD]), ALU.mult).then_inc(cos_done, 1)

                def rope(n):
                    m = l * NT + n
                    dve.wait_ge(sin_done, 2 * m + 2)
                    dve.wait_ge(cos_done, m + 1)
                    dve.tensor_tensor(t_cos[:, :], t_cos[:, :], t_sin[:, :], ALU.add).then_inc(roped, 1)

                def copy_k(n):
                    m = l * NT + n
                    dve.wait_ge(qkT_ps, m + 1)
                    dve.wait_ge(scored, 2 * m)
                    dve.wait_ge(k_carried, l * (NT - 1) + n)
                    dve.tensor_copy(kT[:, :, :].rearrange("p c k -> p (c k)"), ps[:, T_QK + 1, :]).then_inc(k_sb, 1)

                def softmax_shift(n, w):
                    m = l * NT + n
                    s = ps[:, T_S + w, :].rearrange("p (c k) -> p c k", k=P)
                    dve.wait_ge(scored, 2 * m + 1 + w)
                    dve.tensor_reduce(mx[:, w, :], s, AX, ALU.max).then_inc(maxed, 1)
                    dve.wait_ge(maxed, 2 * m + 1 + w)
                    dve.wait_ge(pT_ps, 2 * m)
                    dve.tensor_tensor(prob[:, w, :, :], s, mx[:, w, :].unsqueeze(2).to_broadcast([P, LP, P]),
                                      ALU.subtract).then_inc(shifted, 1)

                def softmax_shift_0(n):
                    softmax_shift(n, 0)

                def softmax_shift_1(n):
                    softmax_shift(n, 1)

                def divide(n):
                    m = l * NT + n
                    out = ps[:, T_O:T_O + 2, 0:4 * (LD + 1)].rearrange("p a (h d) -> p a h d", d=LD + 1)
                    r = rden[:, :].rearrange("p (a h) -> p a h", a=2)
                    dve.wait_ge(pv_ps, 2 * m + 2)
                    dve.reciprocal(r.unsqueeze(3), out[:, :, :, LD:LD + 1]).then_inc(recip, 1)
                    dve.wait_ge(recip, m + 1)
                    dve.wait_ge(oT_ps, m)
                    dve.tensor_tensor(o[:, :].rearrange("p (a h d) -> p a h d", a=2, d=LD), out[:, :, :, 0:LD],
                                      r.unsqueeze(3).to_broadcast([P, 2, 4, LD]), ALU.mult).then_inc(o_sb, 1)

                def residual(n):
                    m = l * NT + n
                    dve.wait_ge(wo_ps, m + 1)
                    one = "p a d -> p (a d)"
                    dve.tensor_tensor(A[:, ds(n + 8, 1), :].rearrange(one), ps[:, T_H, 2 * P:3 * P],
                                      Y[:, ds(n + 8, 1), :].rearrange(one), ALU.add).then_inc(a_sb, 1)

                def clear_carried():
                    dve.wait_ge(a_sb, (l + 1) * NT)
                    dve.wait_ge(k_carried, (l + 1) * (NT - 1))
                    dve.wait_ge(v_carried, (l + 1) * NT)
                    dve.memset(k_last[:, :, :, :], 0.0).then_inc(cleared, 1)
                    dve.memset(v_pair[64:128, :, :, 0:LD], 0.0).then_inc(cleared, 1)

                pipeline(dve, NT, [(norm_squares, 1), (unit_qk, 1), (softmax_shift_0, 2), (softmax_shift_1, 2),
                                   (cosines, 1), (rope, 1), (residual, 3), (copy_k, 1), (divide, 2)])
                clear_carried()

                dve.wait_ge(ffn_w, 16 * N_FFN_W * (l + 1))
                rows4 = ps[:, F_H, :].rearrange("p (t d) -> p t d", d=P)

                def f_centre(g):
                    m = l * NG + g
                    dve.wait_ge(fh_ps, m + 1)
                    dve.tensor_reduce(mean[:, :], rows4, AX, ALU.add).then_inc(fmean, 1)
                    dve.wait_ge(fmean, m + 1)
                    dve.tensor_scalar(mean[:, :], mean[:, :], 1.0 / P, None, ALU.mult).then_inc(fscaled, 1)
                    dve.wait_ge(fscaled, m + 1)
                    dve.wait_ge(fhn, m)
                    dve.tensor_tensor(cen[:, :, :], rows4, mean[:, :].unsqueeze(2).to_broadcast([P, 4, P]),
                                      ALU.subtract).then_inc(fcen, 1)

                def f_normal(g):
                    m = l * NG + g
                    dve.wait_ge(fsqd, m + 1)
                    dve.wait_ge(frstd, m)
                    dve.tensor_reduce(var[:, :], fsq[:, :].rearrange("p (t d) -> p t d", d=P), AX, ALU.add)\
                        .then_inc(fvar, 1)
                    dve.wait_ge(frstd, m + 1)
                    dve.wait_ge(fT_ps, m)
                    dve.scalar_tensor_tensor(out=hn[:, :, :], in0=cen[:, :, :], scalar=float(np.sqrt(P)),
                                             in1=frs[:, :].unsqueeze(2).to_broadcast([P, 4, P]),
                                             op0=ALU.mult, op1=ALU.mult).then_inc(fhn, 1)

                def f_gate(g, c):
                    m = l * NG + g
                    for at, size in HC[c:c + 1]:
                        dve.wait_ge(gelu_sb, 3 * m + c + 1)
                        dve.wait_ge(fy_ps, m)
                        dve.scalar_tensor_tensor(out=hid[0:size, c, :], in0=ps[0:size, F_A + c % 2, :],
                                                 scalar=b1a[0:size, c:c + 1], in1=gate[0:size, c % 2, :],
                                                 op0=ALU.add, op1=ALU.mult).then_inc(hid_sb, 1)

                def f_gate_0(g):
                    f_gate(g, 0)

                def f_gate_1(g):
                    f_gate(g, 1)

                def f_gate_2(g):
                    f_gate(g, 2)

                def f_result(g):
                    m = l * NG + g
                    dve.wait_ge(fy_ps, m + 1)
                    dve.wait_ge(ab2_sb, m + 1)
                    dve.tensor_tensor(Y[:, ds(8 + 4 * g, 4), :], ps[:, F_Y, :].rearrange("p (t d) -> p t d", d=P),
                                      ab2[:, :, :], ALU.add).then_inc(y_sb, 1)

                pipeline(dve, NG, [(f_centre, 0), (f_gate_0, 1), (f_normal, 0), (f_gate_1, 1), (f_gate_2, 1),
                                   (f_result, 1)])
            dve.wait_ge(y_sb, LAYERS * NG)


def gated_recurrence(nc, ps, X, Y, u_in, w_in, b_in, gamma, beta, c_ident):
    with ExitStack() as ctx:
        def sb(name, shape, dt=F32):
            return ctx.enter_context(nc.sbuf_tensor("gr_" + name, shape, dt))

        def sem(name):
            return nc.alloc_semaphore("gr_" + name)

        ident, w = sb("ident", [P, P]), sb("w", [P, 3 * P])
        u, g, b = sb("u", [P, 1]), sb("g", [P, 1]), sb("b", [P, 1])
        bc, bz, br, bz_neg = sb("bc", [P, 1]), sb("bz", [P, 1]), sb("br", [P, 1]), sb("bz_neg", [P, 1])
        total, var, rs = sb("total", [P, 4]), sb("var", [P, 4]), sb("rs", [P, 4])
        eps4, power4 = sb("eps4", [P, 4]), sb("power4", [P, 4])
        cen, sq, yn = sb("cen", [P, 4, P]), sb("sq", [P, 4, P]), sb("yn", [P, 4, P])
        xT, r = sb("xT", [P, 4 * P]), sb("r", [P, 4 * P])
        ROWS = P + 2
        mul, add = sb("mul", [P, ROWS, B, 3]), sb("add", [P, ROWS, B, 3])
        link, z = sb("link", [P, ROWS, B, 3]), sb("z", [P, ROWS, B])
        H_, S_, A_ = 0, 1, 2

        T_X, T_C, T_Z, T_R, T_Y = 0, 1, 2, 3, 4

        zeroed, loaded, negated = sem("zeroed"), sem("loaded"), sem("negated")
        totalled, centred, squared, summed, eps_in, rstd, normed = (
            sem("totalled"), sem("centred"), sem("squared"), sem("summed"), sem("eps_in"), sem("rstd"), sem("normed"))
        added, xT_ps, xT_sb, proj_ps, z_sb, r_sb, c_sb = (
            sem("added"), sem("xT_ps"), sem("xT_sb"), sem("proj_ps"), sem("z_sb"), sem("r_sb"), sem("c_sb"))
        ur_sb, a_part, linked, h_sb, zs_sb, y_ps = (sem("ur_sb"), sem("a_part"), sem("linked"), sem("h_sb"),
                                                    sem("zs_sb"), sem("y_ps"))
        GB = B // 4
        LNS = 3 * GB
        N_LOADS, N_ZERO = 8, 9

        block = ctx.enter_context(nc.Block())

        @block.sync
        def _(sp):
            sp.dma_start(ident[:, :], c_ident).then_inc(loaded, 16)
            sp.dma_start(w[:, :], w_in).then_inc(loaded, 16)
            for dst, src in ((u, u_in), (g, gamma), (b, beta), (bc, b_in[0:P]), (bz, b_in[P:2 * P]),
                             (br, b_in[2 * P:3 * P])):
                sp.dma_start(dst[:, :], src.unsqueeze(1)).then_inc(loaded, 16)

        @block.gpsimd
        def _(pool):
            pool.memset(eps4[:, :], EPS * P).then_inc(zeroed, 1)
            pool.memset(power4[:, :], -0.5).then_inc(zeroed, 1)
            pool.memset(mul[:, :, :, H_:H_ + 1], 0.0).then_inc(zeroed, 1)
            pool.memset(mul[:, P:P + 1, :, A_:A_ + 1], 0.0).then_inc(zeroed, 1)
            pool.memset(add[:, P:P + 1, :, A_:A_ + 1], 0.0).then_inc(zeroed, 1)
            pool.memset(z[:, P:P + 1, :], 0.0).then_inc(zeroed, 1)
            pool.memset(link[:, P:P + 1, :, :], 0.0).then_inc(zeroed, 1)
            pool.memset(z[:, P + 1:P + 2, :], 0.0).then_inc(zeroed, 1)
            pool.memset(add[:, 0:1, :, :], 0.0).then_inc(zeroed, 1)
            pool.wait_ge(zeroed, N_ZERO)
            with pool.Fori(0, NB * LNS) as k:
                pool.wait_ge(summed, k + 1)
                pool.tensor_tensor(rs[:, :], var[:, :], eps4[:, :], ALU.add).then_inc(eps_in, 1)
                pool.wait_ge(eps_in, k + 1)
                pool.tensor_tensor(rs[:, :], rs[:, :], power4[:, :], ALU.pow).then_inc(rstd, 1)

        @block.tensor
        def _(pe):
            pe.wait_ge(loaded, 16 * N_LOADS)
            with pe.Fori(0, NB) as i:
                for h in range(GB):
                    m = i * GB + h
                    pe.wait_ge(normed, i * LNS + 2 * h + 2)
                    pe.wait_ge(xT_sb, m)
                    for t in range(4):
                        mm = pe.transpose(ps[:, T_X, P * t:P * t + P], yn[:, t, :], ident[:, :])
                    mm.then_inc(xT_ps, 1)
                    pe.wait_ge(xT_sb, m + 1)
                    pe.wait_ge(c_sb, m)
                    pe.wait_ge(z_sb, 2 * m)
                    pe.wait_ge(r_sb, m)
                    for c, bank in enumerate((T_C, T_Z, T_R)):
                        mm = pe.matmul(ps[:, bank, :], w[:, P * c:P * c + P], xT[:, :], start=True, stop=True)
                    mm.then_inc(proj_ps, 1)
                for h in range(GB):
                    pe.wait_ge(linked, (i + 1) * (P + 1))
                    pe.wait_ge(centred, i * LNS + 2 * GB + h - GB)
                    for t in range(4):
                        mm = pe.transpose(ps[:, T_Y + h, P * t:P * t + P],
                                          link[:, 1:P + 1, 4 * h + t:4 * h + t + 1, S_:S_ + 1]
                                          .rearrange("p t b s -> p (t b s)"), ident[:, :])
                    mm.then_inc(y_ps, 1)

        @block.scalar
        def _(act):
            act.preload_act_table_set("sigmoid_and_others")
            act.wait_ge(loaded, 16 * N_LOADS)
            act.activation(bz_neg[:, :], bz[:, :], ACT.Identity, scale=-1.0).then_inc(negated, 1)
            act.wait_ge(negated, 1)

            def square(i, j):
                k = i * LNS + j
                act.wait_ge(centred, k + 1)
                act.wait_ge(summed, k)
                act.activation(sq[:, :, :].rearrange("p t d -> p (t d)"), cen[:, :, :].rearrange("p t d -> p (t d)"),
                               ACT.Square).then_inc(squared, 1)

            with act.Fori(0, NB) as i:
                for h in range(GB):
                    m = i * GB + h
                    square(i, 2 * h)
                    square(i, 2 * h + 1)
                    act.wait_ge(xT_ps, m + 1)
                    act.wait_ge(proj_ps, m)
                    act.activation(xT[:, :], ps[:, T_X, :], ACT.Identity, bias=b[:, :], scale=g[:, :])\
                        .then_inc(xT_sb, 1)
                    act.wait_ge(proj_ps, m + 1)
                    act.wait_ge(linked, i * (P + 1))
                    act.wait_ge(zs_sb, i * (P + 1))
                    act.wait_ge(ur_sb, m)

                    def by_step(table):
                        return table.rearrange("p t b -> p b t")
                    rows = slice(4 * h, 4 * h + 4)

                    def bank(n):
                        return ps[:, n, :].rearrange("p (b t) -> p b t", b=4)
                    act.activation(by_step(z[:, 0:P, rows]), bank(T_Z), ACT.Sigmoid, bias=bz[:, :]).then_inc(z_sb, 1)
                    act.activation(by_step(mul[:, 1:P + 1, rows, S_]), bank(T_Z), ACT.Sigmoid, bias=bz_neg[:, :],
                                   scale=-1.0).then_inc(z_sb, 1)
                    act.activation(r[:, :], ps[:, T_R, :], ACT.Sigmoid, bias=br[:, :]).then_inc(r_sb, 1)
                    act.activation(by_step(add[:, 0:P, rows, A_]), bank(T_C), ACT.Identity, bias=bc[:, :])\
                        .then_inc(c_sb, 1)
                for t in range(P):
                    act.wait_ge(linked, i * (P + 1) + t + 1)
                    act.activation(add[:, t + 1, :, H_], link[:, t, :, A_], ACT.Tanh).then_inc(h_sb, 1)
                for h in range(GB):
                    square(i, 2 * GB + h)

        @block.vector
        def _(dve):
            dve.wait_ge(loaded, 16 * N_LOADS)
            dve.wait_ge(zeroed, N_ZERO)

            def centre(i, j, src):
                k = i * LNS + j
                dve.tensor_reduce(total[:, :], src, AX, ALU.add).then_inc(totalled, 1)
                dve.wait_ge(totalled, k + 1)
                dve.wait_ge(normed, k)
                dve.scalar_tensor_tensor(out=cen[:, :, :], in0=total[:, :].unsqueeze(2).to_broadcast([P, 4, P]),
                                         scalar=-1.0 / P, in1=src, op0=ALU.mult, op1=ALU.add).then_inc(centred, 1)

            def normalize(i, j):
                k = i * LNS + j
                dve.wait_ge(squared, k + 1)
                dve.wait_ge(eps_in, k)
                dve.tensor_reduce(var[:, :], sq[:, :, :], AX, ALU.add).then_inc(summed, 1)
                dve.wait_ge(rstd, k + 1)
                dve.scalar_tensor_tensor(out=yn[:, :, :], in0=cen[:, :, :], scalar=float(np.sqrt(P)),
                                         in1=rs[:, :].unsqueeze(2).to_broadcast([P, 4, P]),
                                         op0=ALU.mult, op1=ALU.mult).then_inc(normed, 1)

            with dve.Fori(0, NB) as i:
                for h in range(GB):
                    m = i * GB + h
                    Xg, Yg = X[:, ds(8 * i + 4 * h, 4), :], Y[:, ds(8 * i + 4 * h + 8, 4), :]
                    dve.wait_ge(loaded, 16 * N_LOADS)
                    dve.wait_ge(centred, i * LNS + 2 * h)
                    centre(i, 2 * h, Yg)
                    dve.wait_ge(xT_ps, m)
                    normalize(i, 2 * h)
                    dve.wait_ge(normed, i * LNS + 2 * h + 1)
                    dve.tensor_tensor(Xg, Xg, yn[:, :, :], ALU.add).then_inc(added, 1 + h)
                    dve.wait_ge(loaded, 16 * N_LOADS)
                    dve.wait_ge(added, i * LNS + 2 * h + 1)
                    centre(i, 2 * h + 1, Xg)
                    normalize(i, 2 * h + 1)
                    dve.wait_ge(r_sb, m + 1)
                    dve.tensor_scalar(mul[:, 0:P, 4 * h:4 * h + 4, A_].rearrange("p t b -> p b t"),
                                      r[:, :].rearrange("p (b t) -> p b t", b=4), u[:, :], None, ALU.mult)\
                        .then_inc(ur_sb, 1)
                state = link[:, P, :, S_]
                dve.wait_ge(ur_sb, (i + 1) * GB)
                dve.wait_ge(c_sb, (i + 1) * GB)
                dve.wait_ge(z_sb, 2 * (i + 1) * GB)
                dve.wait_ge(y_ps, i * GB)
                dve.tensor_tensor(link[:, 0, :, S_], mul[:, 0, :, A_], state, ALU.mult).then_inc(a_part, 1)
                dve.tensor_tensor(add[:, 1, :, S_], z[:, 0, :], state, ALU.mult).then_inc(zs_sb, 1)
                dve.wait_ge(a_part, i + 1)
                dve.tensor_tensor(link[:, 0, :, A_], link[:, 0, :, S_], add[:, 0, :, A_], ALU.add).then_inc(linked, 1)
                for t in range(P):
                    row = [x[:, t + 1, :, :].rearrange("p b s -> p (b s)") for x in (link, mul, add)]
                    dve.wait_ge(h_sb, i * P + t + 1)
                    dve.wait_ge(zs_sb, i * (P + 1) + t + 1)
                    dve.tensor_tensor_scan(row[0], row[1], row[2], 0.0, ALU.mult, ALU.add).then_inc(linked, 1)
                    dve.wait_ge(linked, i * (P + 1) + t + 2)
                    dve.tensor_tensor(add[:, t + 2, :, S_], link[:, t + 1, :, S_], z[:, t + 1, :], ALU.mult)\
                        .then_inc(zs_sb, 1)
                for h in range(GB):
                    Xg = X[:, ds(8 * i + 4 * h, 4), :]
                    dve.wait_ge(y_ps, i * GB + h + 1)
                    centre(i, 2 * GB + h, ps[:, T_Y + h, :].rearrange("p (t d) -> p t d", d=P))
                    normalize(i, 2 * GB + h)
                    dve.wait_ge(normed, i * LNS + 2 * GB + h + 1)
                    dve.tensor_tensor(Xg, Xg, yn[:, :, :], ALU.add).then_inc(added, 2 - h)
            dve.wait_ge(added, LNS * NB)


def mixture_of_experts(nc, ps, X, A, out_dram, wg_in, bg_in, w1_in, b1_in, w2_in, b2_in, c_ident, c_ties):
    with ExitStack() as ctx:
        def sb(name, shape, dt=F32):
            return ctx.enter_context(nc.sbuf_tensor("me_" + name, shape, dt))

        def sem(name):
            return nc.alloc_semaphore("me_" + name)

        ident = sb("ident", [P, P])
        wg, bg = sb("wg", [P, E]), sb("bg", [P, E])
        w1, b1 = sb("w1", [P, E, H]), sb("b1", [P, E, HCH])
        w2, b2 = sb("w2", [P, E, HCH, P]), sb("b2", [E, P])
        b1_rows = sb("b1_rows", [E * HCH, P])
        ties = sb("ties", [P, 2, E, E])
        total, var, rs = sb("total", [P, 4]), sb("var", [P, 4]), sb("rs", [P, 4])
        eps4, power4 = sb("eps4", [P, 4]), sb("power4", [P, 4])
        cen, sq, yn = sb("cen", [P, 4, P]), sb("sq", [P, 4, P]), sb("yn", [P, 4, P])
        xT, xTs = sb("xT", [P, 4 * P]), sb("xTs", [P, NT * P])
        accs = sb("accs", [P, 4, P])
        lgt, mx, ex, den = sb("lgt", [P, 4, E]), sb("mx", [P, 4]), sb("ex", [P, 4, E]), sb("den", [P, 4])
        ge, gt, rank = sb("ge", [P, 4, E, E]), sb("gt", [P, 4, E, E]), sb("rank", [P, 4, E])
        wt, wtT = sb("wt", [P, 4, E]), sb("wtT", [E, 4 * P])
        weights, wgr = sb("weights", [P, NT, E]), sb("wgr", [P, 4, E])
        hid = sb("hid", [P, 2, HCH, 4 * P])

        T_X, T_L, T_W, T_B = 0, 1, 2, 3
        T_U, T_D = 0, 4

        loaded, loaded_e, zeroed = sem("loaded"), sem("loaded_e"), sem("zeroed")
        totalled, centred, squared, summed, eps_in, rstd, normed = (
            sem("totalled"), sem("centred"), sem("squared"), sem("summed"), sem("eps_in"), sem("rstd"), sem("normed"))
        xT_ps, xT_sb, lgt_ps, biased, maxed, lshift, expd, denned, recip, probs = (
            sem("xT_ps"), sem("xT_sb"), sem("lgt_ps"), sem("biased"), sem("maxed"), sem("lshift"), sem("expd"),
            sem("denned"), sem("recip"), sem("probs"))
        compared, masked, both, ranked, picked, wt_sb, wtT_ps, wtT_sb, base_ps, base_sb = (
            sem("compared"), sem("masked"), sem("both"), sem("ranked"), sem("picked"), sem("wt_sb"), sem("wtT_ps"),
            sem("wtT_sb"), sem("base_ps"), sem("base_sb"))
        up_ps, hid_sb, down_ps, acc_sb, wgr_sb, done, stored = (
            sem("up_ps"), sem("hid_sb"), sem("down_ps"), sem("acc_sb"), sem("wgr_sb"), sem("done"), sem("stored"))
        b1_ps, b1_sb = sem("b1_ps"), sem("b1_sb")
        N_LOADS, N_LOADS_E = 5, 3

        block = ctx.enter_context(nc.Block())

        @block.sync
        def _(sp):
            sp.dma_start(ident[:, :], c_ident).then_inc(loaded, 16)
            sp.dma_start(wg[:, :], wg_in).then_inc(loaded, 16)
            sp.dma_start(bg[:, :], bg_in.partition_broadcast(P)).then_inc(loaded, 16)
            sp.dma_start(ties[:, :, :, :].rearrange("p a e j -> p (a e j)"), c_ties.to_broadcast([P, 2 * E * E]))\
                .then_inc(loaded, 16)
            sp.dma_start(b2[:, :], b2_in).then_inc(loaded, 16)
            sp.dma_start(w1[:, :, :], w1_in.rearrange("e d h -> d e h")).then_inc(loaded_e, 16)
            sp.dma_start(b1_rows[:, :], b1_in.rearrange("e (c p) -> (e c) p", p=P)).then_inc(loaded_e, 16)
            sp.dma_start(w2[:, :, :, :], w2_in.rearrange("e (c p) d -> p e c d", p=P)).then_inc(loaded_e, 16)
            out_tiles = out_dram.rearrange("b (i p) d -> i p b d", p=P)
            for i in range(NB):
                sp.wait_ge(done, 2 * i + 2)
                sp.dma_start(out_tiles[i], X[:, 8 * i:8 * i + 8, :]).then_inc(stored, 16)
            sp.wait_ge(stored, 16 * NB)

        @block.gpsimd
        def _(pool):
            pool.memset(eps4[:, :], EPS * P).then_inc(zeroed, 1)
            pool.memset(power4[:, :], -0.5).then_inc(zeroed, 1)
            pool.wait_ge(zeroed, 2)
            with pool.Fori(0, 2 * NG) as k:
                pool.wait_ge(summed, k + 1)
                pool.tensor_tensor(rs[:, :], var[:, :], eps4[:, :], ALU.add).then_inc(eps_in, 1)
                pool.wait_ge(eps_in, k + 1)
                pool.tensor_tensor(rs[:, :], rs[:, :], power4[:, :], ALU.pow).then_inc(rstd, 1)

        @block.tensor
        def _(pe):
            pe.wait_ge(loaded, 16 * N_LOADS)

            def turn_x(g):
                pe.wait_ge(normed, g + 1)
                pe.wait_ge(xT_sb, 2 * g)
                for t in range(4):
                    mm = pe.transpose(ps[:, T_X, P * t:P * t + P], yn[:, t, :], ident[:, :])
                mm.then_inc(xT_ps, 1)

            def logits(g):
                pe.wait_ge(xT_sb, 2 * g + 2)
                pe.wait_ge(biased, g)
                for t in range(4):
                    mm = pe.matmul(ps[:, T_L, E * t:E * t + E], xT[:, P * t:P * t + P], wg[:, :], start=True, stop=True)
                mm.then_inc(lgt_ps, 1)

            def turn_weights(g):
                pe.wait_ge(wt_sb, g + 1)
                pe.wait_ge(wtT_sb, g)
                for t in range(4):
                    mm = pe.transpose(ps[0:E, T_W, P * t:P * t + P], wt[:, t, :], ident[:, :])
                mm.then_inc(wtT_ps, 1)
                pe.wait_ge(wtT_sb, g + 1)
                pe.wait_ge(base_sb, g)
                for t in range(4):
                    mm = pe.matmul(ps[:, T_B, P * t:P * t + P], wtT[:, P * t:P * t + P], b2[:, :],
                                   start=True, stop=True)
                mm.then_inc(base_ps, 1)

            pipeline(pe, NG, [(turn_x, 0), (turn_weights, 1), (logits, 0)])
            pe.wait_ge(base_sb, NG)
            pe.wait_ge(loaded_e, 16 * N_LOADS_E)
            pe.transpose(ps[:, T_D, 0:E * HCH], b1_rows[:, :], ident[0:E * HCH, 0:E * HCH]).then_inc(b1_ps, 1)
            pe.wait_ge(b1_sb, 1)

            def up(g, e):
                m = E * g + e
                for c in range(HCH):
                    if not isinstance(m, int) or m:
                        pe.wait_ge(hid_sb, HCH * (m - 1) + c + 1)
                    pe.matmul(ps[:, T_U + c, :], w1[:, e, P * c:P * c + P], xTs[:, ds(4 * P * g, 4 * P)],
                              start=True, stop=True).then_inc(up_ps, 1)

            def down(g, e):
                m = E * g + e
                pe.wait_ge(hid_sb, HCH * (m + 1))
                if not isinstance(m, int) or m > 1:
                    pe.wait_ge(acc_sb, m - 1)
                for t in range(4):
                    for c in range(HCH):
                        mm = pe.matmul(ps[:, T_D + e % 2, P * t:P * t + P], hid[:, e % 2, c, P * t:P * t + P],
                                       w2[:, e, c, :], start=(c == 0), stop=(c == HCH - 1))
                mm.then_inc(down_ps, 1)

            up(0, 0)
            for e in range(1, E):
                up(0, e)
                down(0, e - 1)
            with pe.Fori(1, NG) as g:
                up(g, 0)
                down(g - 1, E - 1)
                for e in range(1, E):
                    up(g, e)
                    down(g, e - 1)
            down(NG - 1, E - 1)

        @block.scalar
        def _(act):
            act.preload_act_table_set("natural_log_exp_and_others")

            def square(k):
                act.wait_ge(centred, k + 1)
                act.wait_ge(summed, k)
                act.activation(sq[:, :, :].rearrange("p t d -> p (t d)"), cen[:, :, :].rearrange("p t d -> p (t d)"),
                               ACT.Square).then_inc(squared, 1)

            def copy_xT(g):
                act.wait_ge(xT_ps, g + 1)
                act.wait_ge(lgt_ps, g)
                act.copy(xT[:, :], ps[:, T_X, :]).then_inc(xT_sb, 1)
                act.copy(xTs[:, ds(4 * P * g, 4 * P)], ps[:, T_X, :]).then_inc(xT_sb, 1)

            def exps(g):
                act.wait_ge(lshift, g + 1)
                act.wait_ge(probs, g)
                act.activation(ex[:, :, :].rearrange("p t e -> p (t e)"), lgt[:, :, :].rearrange("p t e -> p (t e)"),
                               ACT.Exp).then_inc(expd, 1)

            def copy_wT(g):
                act.wait_ge(wtT_ps, g + 1)
                act.wait_ge(base_ps, g)
                act.copy(wtT[:, :], ps[0:E, T_W, :]).then_inc(wtT_sb, 1)

            def copy_base(g):
                act.wait_ge(base_ps, g + 1)
                act.copy(A[:, ds(4 * g + 8, 4), :].rearrange("p t d -> p (t d)"), ps[:, T_B, :]).then_inc(base_sb, 1)

            pipeline(act, NG, [(square, 0), (copy_xT, 0), (copy_wT, 1), (copy_base, 1), (exps, 0)])
            act.preload_act_table_set("gelu_and_others")
            act.wait_ge(b1_ps, 1)
            act.copy(b1[:, :, :].rearrange("p e c -> p (e c)"), ps[:, T_D, 0:E * HCH]).then_inc(b1_sb, 1)
            act.wait_ge(b1_sb, 1)

            def gelus(g, e):
                m = E * g + e
                for c in range(HCH):
                    act.wait_ge(up_ps, HCH * m + c + 1)
                    if not isinstance(m, int) or m > 1:
                        act.wait_ge(down_ps, m - 1)
                    act.activation(hid[:, e % 2, c, :], ps[:, T_U + c, :], ACT.Gelu, bias=b1[:, e, c:c + 1])\
                        .then_inc(hid_sb, 1)

            def experts(g):
                for e in range(E):
                    gelus(g, e)
                    if e == 2 and not (isinstance(g, int) and g == 0):
                        square(NG + g - 1)

            experts(0)
            with act.Fori(1, NG) as g:
                experts(g)
            square(2 * NG - 1)

        @block.vector
        def _(dve):
            dve.wait_ge(loaded, 16 * N_LOADS)

            def centre(k, src):
                dve.tensor_reduce(total[:, :], src, AX, ALU.add).then_inc(totalled, 1)
                dve.wait_ge(totalled, k + 1)
                dve.wait_ge(normed, k)
                dve.scalar_tensor_tensor(out=cen[:, :, :], in0=total[:, :].unsqueeze(2).to_broadcast([P, 4, P]),
                                         scalar=-1.0 / P, in1=src, op0=ALU.mult, op1=ALU.add).then_inc(centred, 1)

            def normalize(k):
                dve.wait_ge(squared, k + 1)
                dve.wait_ge(eps_in, k)
                dve.tensor_reduce(var[:, :], sq[:, :, :], AX, ALU.add).then_inc(summed, 1)
                dve.wait_ge(rstd, k + 1)
                dve.scalar_tensor_tensor(out=yn[:, :, :], in0=cen[:, :, :], scalar=float(np.sqrt(P)),
                                         in1=rs[:, :].unsqueeze(2).to_broadcast([P, 4, P]),
                                         op0=ALU.mult, op1=ALU.mult).then_inc(normed, 1)

            def norm_in(g):
                dve.wait_ge(loaded, 16 * N_LOADS)
                dve.wait_ge(centred, g)
                centre(g, X[:, ds(4 * g, 4), :])
                dve.wait_ge(xT_ps, g)
                normalize(g)

            def by_expert(x):
                return x.unsqueeze(2).to_broadcast([P, 4, E])

            def route(g):
                dve.wait_ge(lgt_ps, g + 1)
                dve.wait_ge(expd, g)
                dve.tensor_tensor(lgt[:, :, :], ps[:, T_L, 0:4 * E].rearrange("p (t e) -> p t e", e=E),
                                  bg[:, :].unsqueeze(1).to_broadcast([P, 4, E]), ALU.add).then_inc(biased, 1)
                dve.wait_ge(biased, g + 1)
                dve.tensor_reduce(mx[:, :], lgt[:, :, :], AX, ALU.max).then_inc(maxed, 1)
                dve.wait_ge(maxed, g + 1)
                dve.tensor_tensor(lgt[:, :, :], lgt[:, :, :], by_expert(mx[:, :]), ALU.subtract).then_inc(lshift, 1)
                dve.wait_ge(expd, g + 1)
                dve.tensor_reduce(den[:, :], ex[:, :, :], AX, ALU.add).then_inc(denned, 1)
                dve.wait_ge(denned, g + 1)
                dve.reciprocal(den[:, :], den[:, :]).then_inc(recip, 1)
                dve.wait_ge(recip, g + 1)
                dve.wait_ge(wtT_ps, g)
                dve.tensor_tensor(wt[:, :, :], ex[:, :, :], by_expert(den[:, :]), ALU.mult).then_inc(probs, 1)
                dve.wait_ge(probs, g + 1)
                dve.wait_ge(ranked, g)
                pj = wt[:, :, :].unsqueeze(2).to_broadcast([P, 4, E, E])
                pe_ = wt[:, :, :].unsqueeze(3).to_broadcast([P, 4, E, E])
                dve.tensor_tensor(ge[:, :, :, :], pj, pe_, ALU.is_ge).then_inc(compared, 1)
                dve.tensor_tensor(gt[:, :, :, :], pj, pe_, ALU.is_gt).then_inc(compared, 1)
                dve.wait_ge(compared, 2 * g + 2)
                for x, c in ((ge, 0), (gt, 1)):
                    dve.tensor_tensor(x[:, :, :, :].rearrange("p t e j -> p t (e j)"),
                                      x[:, :, :, :].rearrange("p t e j -> p t (e j)"),
                                      ties[:, c, :, :].rearrange("p e j -> p (e j)").unsqueeze(1)
                                      .to_broadcast([P, 4, E * E]), ALU.mult).then_inc(masked, 1)
                dve.wait_ge(masked, 2 * g + 2)
                dve.tensor_tensor(ge[:, :, :, :], ge[:, :, :, :], gt[:, :, :, :], ALU.add).then_inc(both, 1)
                dve.wait_ge(both, g + 1)
                dve.tensor_reduce(rank[:, :, :], ge[:, :, :, :], AX, ALU.add).then_inc(ranked, 1)
                dve.wait_ge(ranked, g + 1)
                dve.scalar_tensor_tensor(out=wt[:, :, :], in0=rank[:, :, :], scalar=1.5, in1=wt[:, :, :],
                                         op0=ALU.is_lt, op1=ALU.mult).then_inc(wt_sb, 1)
                dve.wait_ge(wt_sb, g + 1)
                dve.tensor_copy(weights[:, ds(4 * g, 4), :], wt[:, :, :]).then_inc(picked, 1)

            pipeline(dve, NG, [(norm_in, 0), (route, 0)])

            def result(g):
                Xg = X[:, ds(4 * g, 4), :]
                normalize(NG + g)
                dve.wait_ge(normed, NG + g + 1)
                dve.tensor_tensor(Xg, Xg, yn[:, :, :], ALU.add).then_inc(done, 1)

            def weigh(g, e):
                m = E * g + e
                dve.wait_ge(down_ps, m + 1)
                dve.wait_ge(acc_sb, m)
                dve.wait_ge(wgr_sb, g + 1)
                dve.wait_ge(base_sb, NG)
                if e == 0:
                    dve.wait_ge(centred, NG + g)
                for t in range(4):
                    acc = accs[:, t, :]
                    base = A[:, ds(4 * g + t + 8, 1), :].rearrange("p a d -> p (a d)") if e == 0 else acc
                    op = dve.scalar_tensor_tensor(out=acc, in0=ps[:, T_D + e % 2, P * t:P * t + P],
                                                  scalar=wgr[:, t, e:e + 1], in1=base,
                                                  op0=ALU.mult, op1=ALU.add)
                op.then_inc(acc_sb, 1)

            def weights_of(g):
                dve.wait_ge(picked, NG)
                dve.wait_ge(acc_sb, E * g)
                dve.tensor_copy(wgr[:, :, :], weights[:, ds(4 * g, 4), :])\
                    .then_inc(wgr_sb, 1)

            def experts(g):
                weights_of(g)
                for e in range(E):
                    weigh(g, e)
                    if e == 1 and not (isinstance(g, int) and g == 0):
                        result(g - 1)
                dve.wait_ge(acc_sb, E * (g + 1))
                centre(NG + g, accs[:, :, :])

            experts(0)
            with dve.Fori(1, NG) as g:
                experts(g)
            result(NG - 1)
            dve.wait_ge(done, NG)


def sandwich_kernel(nc, L0_attn_x, L0_attn_W_qkv, L0_attn_ln_gamma, L0_attn_ln_beta, L0_attn_W_proj, L0_attn_b_proj,
                    L0_ffn_wqkv, L0_ffn_q_scale, L0_ffn_k_scale, L0_ffn_wo, L0_ffn_ln_g, L0_ffn_ln_b,
                    L0_ffn_w1, L0_ffn_b1, L0_ffn_w2, L0_ffn_b2, L1_attn_u, L1_attn_W, L1_attn_b,
                    L1_attn_gamma, L1_attn_beta, L1_ffn_Wg, L1_ffn_bg, L1_ffn_W1, L1_ffn_b1, L1_ffn_W2, L1_ffn_b2,
                    const_ident, const_shift, const_carry, const_lane, const_masks, const_rot, const_ties, out_0):
    with ExitStack() as ctx:
        X = ctx.enter_context(nc.sbuf_tensor("X", [P, NT, P], F32))
        Y = ctx.enter_context(nc.sbuf_tensor("Y", [P, NT + 8, P], F32))
        A = ctx.enter_context(nc.sbuf_tensor("A", [P, NT + 8, P], F32))
        ps = ctx.enter_context(nc.psum_tensor("ps", [P, 8, 512], F32))
        with nc.cleanup_on_exit():
            window_attention(nc, ps, X, Y, L0_attn_x, L0_attn_W_qkv, L0_attn_ln_gamma, L0_attn_ln_beta, L0_attn_W_proj,
                             L0_attn_b_proj, const_ident, const_lane)
        with nc.cleanup_on_exit():
            local_transformer(nc, ps, Y, A, L0_ffn_wqkv, L0_ffn_q_scale, L0_ffn_k_scale, L0_ffn_wo, L0_ffn_ln_g,
                              L0_ffn_ln_b, L0_ffn_w1, L0_ffn_b1, L0_ffn_w2, L0_ffn_b2, const_ident, const_shift,
                              const_carry, const_masks, const_rot)
        with nc.cleanup_on_exit():
            gated_recurrence(nc, ps, X, Y, L1_attn_u, L1_attn_W, L1_attn_b, L1_attn_gamma, L1_attn_beta, const_ident)
        with nc.cleanup_on_exit():
            mixture_of_experts(nc, ps, X, A, out_0, L1_ffn_Wg, L1_ffn_bg, L1_ffn_W1, L1_ffn_b1, L1_ffn_W2, L1_ffn_b2,
                               const_ident, const_ties)


def shape_constants():
    f = np.float32
    ident = np.eye(P, dtype=f)
    shift = np.zeros((P, P), f)
    shift[np.arange(P - 1), np.arange(1, P)] = 1
    carry = np.zeros((P, P), f)
    carry[P - 1, 0] = 1
    lane = np.zeros((P, 4), f)
    lane[np.arange(P), (np.arange(P) // WD) % 4] = 1
    q = np.arange(P)[:, None] % WIN
    c = np.arange(WIN)[None, :]
    own = np.where(c <= q, 0, NEG).astype(f)
    prev = np.where(c >= q, 0, NEG).astype(f)
    none = np.full((P, WIN), NEG, f)
    first = np.stack([np.concatenate([own, none if i == 0 else prev], 1) for i in range(NB)], 1)
    second = np.concatenate([prev, own], 1)[:, None]
    masks = np.concatenate([first, second], 1)
    half = np.arange(0, LD, 2, dtype=f)
    inv = (f(1.0) / f(10000.0) ** (half / f(LD))).astype(f)
    t = np.arange(T, dtype=f)
    fr = (t[:, None] * inv[None, :]).astype(f)
    base = ((half + f(0.4 * LD)) / f(1.4 * LD)).astype(f)
    power = ((t - T // 2) / f(WIN // 2)).astype(f)
    scale = (base[None, :].astype(np.float64) ** power[:, None]).astype(f)
    cos, sin = np.cos(fr), np.sin(fr)
    tabs = []
    for s in (scale * f(8.0), f(1) / scale):
        tabs.append((np.concatenate([cos * s, cos * s], 1), np.concatenate([-sin * s, sin * s], 1)))
    rot = np.stack([np.stack([a[0] for a in tabs], 1), np.stack([a[1] for a in tabs], 1)], 1)
    rot = rot.reshape(NB, P, 2, 2, LD).transpose(1, 0, 2, 3, 4).astype(f)
    before = np.tril(np.ones((E, E), f), -1)
    ties = np.stack([before, 1 - before - np.eye(E, dtype=f)]).reshape(1, -1)
    return {
        "ident": ident, "shift": shift, "carry": carry, "lane": lane,
        "masks": np.ascontiguousarray(masks.reshape(P, -1)), "rot": np.ascontiguousarray(rot.reshape(P, -1)),
        "ties": np.ascontiguousarray(ties.astype(f)),
    }


_INS = ['L0_attn_x', 'L0_attn_W_qkv', 'L0_attn_ln_gamma', 'L0_attn_ln_beta', 'L0_attn_W_proj', 'L0_attn_b_proj',
        'L0_ffn_wqkv', 'L0_ffn_q_scale', 'L0_ffn_k_scale', 'L0_ffn_wo', 'L0_ffn_ln_g', 'L0_ffn_ln_b',
        'L0_ffn_w1', 'L0_ffn_b1', 'L0_ffn_w2', 'L0_ffn_b2', 'L1_attn_u', 'L1_attn_W', 'L1_attn_b',
        'L1_attn_gamma', 'L1_attn_beta', 'L1_ffn_Wg', 'L1_ffn_bg', 'L1_ffn_W1', 'L1_ffn_b1', 'L1_ffn_W2',
        'L1_ffn_b2']
_OUTS = [((8, 512, 128), 'float32')]


def kernel(**inputs):
    import numpy as _np
    import concourse.bacc as _bacc
    from concourse import mybir as _mybir
    from concourse.bass_utils import run_bass_kernel_spmd as _run

    nc = _bacc.Bacc("TRN2", target_bir_lowering=False, num_devices=1)
    arrays = {}
    for name in _INS:
        a = _np.asarray(inputs[name])
        if name == 'L1_attn_W':
            a = a.T
        arrays[name] = _np.ascontiguousarray(a)
    for name, a in shape_constants().items():
        arrays["const_" + name] = a
    args = {name: nc.dram_tensor(name + "_dram", a.shape, _mybir.dt.from_np(a.dtype), kind="ExternalInput").ap()
            for name, a in arrays.items()}
    arrays = {name + "_dram": a for name, a in arrays.items()}
    for i, (shape, dtype) in enumerate(_OUTS):
        dt = _mybir.dt.from_np(_np.dtype(dtype))
        args[f"out_{i}"] = nc.dram_tensor(f"out_{i}_dram", shape, dt, kind="ExternalOutput").ap()
    sandwich_kernel(nc, **args)
    r = _run(nc, [arrays], core_ids=[0])
    got = tuple(r.results[0][f"out_{i}_dram"] for i in range(len(_OUTS)))
    return got[0]
```

```python
from contextlib import ExitStack

import numpy as np

import concourse.bass as bass
from concourse import mybir

F32 = mybir.dt.float32
BF16 = mybir.dt.bfloat16
ALU = mybir.AluOpType
ACT = mybir.ActivationFunctionType
AX = mybir.AxisListType.X
ds = bass.ds

P = 128
B, T = 8, 512
NT = B * T // P
NB = T // P
WIN = 64
NG = NT // 4
EPS = 1e-5
WH, WD = 16, 8
WP = WH // 2
LH, LD = 8, 64
LP = LH // 2
INNER = LH * LD
LAYERS = 2
HID = 341
HC = [(0, 128), (128, 128), (256, HID - 256)]
E, H, HCH = 8, 512, 4
NEG = -1e30


def pipeline(eng, count, stages):
    last = max(lag for _, lag in stages)
    for k in range(last):
        for stage, lag in stages:
            if k >= lag:
                stage(k - lag)
    with eng.Fori(last, count) as k:
        for stage, lag in stages:
            stage(k - lag)
    for k in range(count, count + last):
        for stage, lag in stages:
            if k - lag < count:
                stage(k - lag)


def window_attention(nc, ps, X, Y, x, w_qkv, ln_gamma, ln_beta, w_proj, b_proj, c_ident, c_lane):
    with ExitStack() as ctx:
        def sb(name, shape, dt=F32):
            return ctx.enter_context(nc.sbuf_tensor("wa_" + name, shape, dt))

        def sem(name):
            return nc.alloc_semaphore("wa_" + name)

        wqkv = sb("wqkv", [P, 3 * P])
        wproj = sb("wproj", [P, P])
        bproj = sb("bproj", [P, P])
        gam, bet = sb("gam", [P, WD]), sb("bet", [P, WD])
        spread = sb("spread", [P, 2, P])
        gam_col, bet_col = sb("gam_col", [P, 1]), sb("bet_col", [P, 1])
        gam_lane, bet_lane = sb("gam_lane", [P, 4]), sb("bet_lane", [P, 4])
        ident, lane = sb("ident", [P, P]), sb("lane", [P, 4])
        power, epsilon = sb("power", [P, 1]), sb("epsilon", [P, 1])
        st, mv, rs = sb("st", [P, 6]), sb("mv", [P, 2]), sb("rs", [P, 1])
        ve = sb("ve", [P, 1])
        xn, xnT = sb("xn", [P, P]), sb("xnT", [P, P])
        gsum, gvar, grs = sb("gsum", [P, 2 * WH]), sb("gvar", [P, 2 * WH]), sb("grs", [P, 2 * WH])
        cen, sq, qk = sb("cen", [P, 2 * P]), sb("sq", [P, 2 * P]), sb("qk", [P, 2 * P])
        qm = sb("qm", [P, 4, P])
        kT = sb("kT", [P, P])
        vz = sb("vz", [P, 2, WP, 2, WD + 1])
        mx = sb("mx", [P, WH])
        prob = sb("prob", [P, WH, WIN])
        pT = sb("pT", [P, WP, P])
        rden = sb("rden", [P, WH])
        o, oT = sb("o", [P, P]), sb("oT", [P, P])
        y = sb("y", [P, P])
        st2, mv2, rs2, ve2 = sb("st2", [P, 6]), sb("mv2", [P, 2]), sb("rs2", [P, 1]), sb("ve2", [P, 1])
        yn = sb("yn", [P, P])
        st3, mv3, rs3, ve3 = sb("st3", [P, 6]), sb("mv3", [P, 2]), sb("rs3", [P, 1]), sb("ve3", [P, 1])

        T_QT, T_QK, T_V, T_OUT = 0, 1, 2, 3
        HH, HP = WH // 2, WP // 2

        def result_half(half):
            return ps[:, 5 + 2 * half, 0:HH * (WD + 1)].rearrange("p (h d) -> p h d", d=WD + 1)

        x_in, const_in = sem("x_in"), sem("const_in")
        zeroed = sem("zeroed")
        stats, meanvar, eps_added, rstd = sem("stats"), sem("meanvar"), sem("eps_added"), sem("rstd")
        normed, xT_ps, xT_sb = sem("normed"), sem("xT_ps"), sem("xT_sb")
        qk_ps, v_ps = sem("qk_ps"), sem("v_ps")
        spread_sb, columns, lanes = sem("spread_sb"), sem("columns"), sem("lanes")
        summed, centred, squared, varsum = sem("summed"), sem("centred"), sem("squared"), sem("varsum")
        logged, grstd, qk_sb = sem("logged"), sem("grstd"), sem("qk_sb")
        qT_ps, kT_ps, qm_sb, kT_sb, v_sb = sem("qT_ps"), sem("kT_ps"), sem("qm_sb"), sem("kT_sb"), sem("v_sb")
        scored, maxed, shifted, expd = sem("scored"), sem("maxed"), sem("shifted"), sem("expd")
        pT_ps, pT_sb, pv_ps, recip, o_sb = sem("pT_ps"), sem("pT_sb"), sem("pv_ps"), sem("recip"), sem("o_sb")
        oT_ps, oT_sb, proj_ps, y_sb = sem("oT_ps"), sem("oT_sb"), sem("proj_ps"), sem("y_sb")
        stats2, meanvar2, eps2, rstd2, yn_sb, added = (sem("stats2"), sem("meanvar2"), sem("eps2"), sem("rstd2"),
                                                       sem("yn_sb"), sem("added"))
        stats3, meanvar3, eps3, rstd3, out = sem("stats3"), sem("meanvar3"), sem("eps3"), sem("rstd3"), sem("out")
        meaned = sem("meaned")
        N_CONST = 7

        block = ctx.enter_context(nc.Block())

        @block.sync
        def _(sp):
            for dst, src in ((wqkv[:, :], w_qkv), (ident[:, :], c_ident), (lane[:, :], c_lane),
                             (gam[:, :], ln_gamma.partition_broadcast(P)), (bet[:, :], ln_beta.partition_broadcast(P)),
                             (wproj[:, :], w_proj), (bproj[:, :], b_proj.partition_broadcast(P)),):
                sp.dma_start(dst, src).then_inc(const_in, 16)
            xv = x.rearrange("b (i p) d -> i p b d", p=P)
            for i in range(NB):
                if i:
                    sp.wait_ge(x_in, 16 * i)
                sp.dma_start(X[:, 8 * i:8 * i + 8, :], xv[i]).then_inc(x_in, 16)

        @block.gpsimd
        def _(pool):
            pool.memset(Y[:, 0:8, :], 0.0).then_inc(zeroed, 1)
            pool.memset(power[:, :], -0.5).then_inc(zeroed, 1)
            pool.memset(vz[:, :, :, :, :], 0.0).then_inc(zeroed, 1)
            pool.wait_ge(zeroed, 3)
            pool.memset(vz[0:64, :, :, 0, WD:WD + 1], 1.0).then_inc(zeroed, 1)
            pool.memset(vz[64:128, :, :, 1, WD:WD + 1], 1.0).then_inc(zeroed, 1)
            pool.wait_ge(zeroed, 5)
            pool.memset(epsilon[:, :], EPS).then_inc(zeroed, 1)
            pool.wait_ge(zeroed, 6)

            def rsqrt(mean_var, with_eps, out_, source, eps_sem, done, n):
                pool.wait_ge(source, n + 1)
                pool.tensor_tensor(with_eps[:, :], mean_var[:, 1:2], epsilon[:, :], ALU.add).then_inc(eps_sem, 1)
                pool.wait_ge(eps_sem, n + 1)
                pool.tensor_tensor(out_[:, :], with_eps[:, :], power[:, :], ALU.pow).then_inc(done, 1)

            def rsqrt_in(n):
                pool.wait_ge(normed, n)
                rsqrt(mv, ve, rs, meanvar, eps_added, rstd, n)

            def rsqrt_out(n):
                rsqrt(mv2, ve2, rs2, meanvar2, eps2, rstd2, n)

            def rsqrt_next(n):
                rsqrt(mv3, ve3, rs3, meanvar3, eps3, rstd3, n)

            pipeline(pool, NT, [(rsqrt_in, 0), (rsqrt_out, 3), (rsqrt_next, 4)])

        @block.tensor
        def _(pe):
            pe.wait_ge(const_in, 16 * N_CONST)
            pe.wait_ge(zeroed, 6)

            def turn_x(n):
                pe.wait_ge(normed, n + 1)
                if not isinstance(n, int) or n > 2:
                    pe.wait_ge(y_sb, n - 2)
                pe.transpose(ps[:, T_OUT, 2 * P:3 * P], xn[:, :], ident[:, :]).then_inc(xT_ps, 1)

            def qkv(n):
                pe.wait_ge(xT_sb, n + 1)
                pe.wait_ge(kT_sb, n)
                pe.matmul(ps[:, T_QK, 0:2 * P], xnT[:, :], wqkv[:, 0:2 * P], start=True, stop=True)\
                    .then_inc(qk_ps, 1)
                pe.wait_ge(v_sb, n)
                wv = wqkv[:, 2 * P:3 * P].rearrange("p (c h d) -> p c h d", h=2, d=WD)
                for w in range(2):
                    for h in range(2):
                        mm = pe.matmul(ps[64 * h:64 * h + 64, T_V, 64 * w:64 * w + 64], xnT[:, 64 * w:64 * w + 64],
                                       wv[:, :, h, :], start=True, stop=True)
                mm.then_inc(v_ps, 1)

            def transposes(n):
                pe.wait_ge(qk_sb, n + 1)
                pe.wait_ge(qm_sb, n)
                pe.transpose(ps[:, T_QT, 0:P], qk[:, 0:P], ident[:, :]).then_inc(qT_ps, 1)
                pe.transpose(ps[:, T_QK, 0:P], qk[:, P:2 * P], ident[:, :]).then_inc(kT_ps, 1)

            def score(n, half):
                pe.wait_ge(qm_sb, n + 1)
                pe.wait_ge(kT_sb, n + 1)
                if not isinstance(n, int) or n:
                    pe.wait_ge(pT_sb, 2 * n - 1 + half)
                    pe.wait_ge(o_sb, 2 * n - 1 + half)
                for j in range(4):
                    for r in (2 * half, 2 * half + 1):
                        for w in range(2):
                            mm = pe.matmul(ps[64 * w:64 * w + 64, 4 + r, WIN * j:WIN * j + WIN],
                                           qm[32 * r:32 * r + 32, j, 64 * w:64 * w + 64],
                                           kT[32 * r:32 * r + 32, 64 * w:64 * w + 64], start=True, stop=True)
                mm.then_inc(scored, 1)

            def turn_p(n, half):
                pe.wait_ge(expd, 2 * n + 1 + half)
                for c in range(HP):
                    h = HH * half + 2 * c
                    mm = pe.transpose(ps[:, 4 + 2 * half, P * c:P * c + P],
                                      prob[:, h:h + 2, :].rearrange("p a b -> p (a b)"), ident[:, :])
                mm.then_inc(pT_ps, 1)

            def attend(n, half):
                pe.wait_ge(pT_sb, 2 * n + 1 + half)
                pe.wait_ge(v_sb, n + 1)
                for c in range(HP):
                    for w in range(2):
                        mm = pe.matmul(ps[64 * w:64 * w + 64, 5 + 2 * half, 18 * c:18 * c + 18],
                                       pT[:, HP * half + c, 64 * w:64 * w + 64],
                                       vz[:, w, HP * half + c, :, :].rearrange("p a b -> p (a b)"),
                                       start=True, stop=True)
                mm.then_inc(pv_ps, 1)

            def score_0(n):
                score(n, 0)

            def score_1(n):
                score(n, 1)

            def turn_p_0(n):
                turn_p(n, 0)

            def attend_0(n):
                attend(n, 0)

            def turn_p_1(n):
                turn_p(n, 1)

            def attend_1(n):
                attend(n, 1)

            def turn_o(n):
                pe.wait_ge(o_sb, 2 * n + 2)
                pe.wait_ge(y_sb, n)
                pe.wait_ge(xT_sb, min(n + 3, NT) if isinstance(n, int) else n + 3)
                pe.transpose(ps[:, T_OUT, 0:P], o[:, :], ident[:, :]).then_inc(oT_ps, 1)

            def project(n):
                pe.wait_ge(oT_sb, n + 1)
                pe.matmul(ps[:, T_OUT, P:2 * P], oT[:, :], wproj[:, :], start=True, stop=True).then_inc(proj_ps, 1)

            pipeline(pe, NT, [(qkv, 1), (turn_o, 3), (score_0, 2), (score_1, 2), (turn_p_0, 2), (transposes, 1),
                              (project, 3), (turn_p_1, 2), (attend_0, 2), (turn_x, 0), (attend_1, 2)])

        @block.scalar
        def _(act):
            act.preload_act_table_set("natural_log_exp_and_others")
            act.wait_ge(zeroed, 6)

            def copy_xT(n):
                act.wait_ge(xT_ps, n + 1)
                act.wait_ge(v_ps, n)
                act.copy(xnT[:, :], ps[:, T_OUT, 2 * P:3 * P]).then_inc(xT_sb, 1)

            def exps(n, half):
                act.wait_ge(shifted, 2 * n + 1 + half)
                part = prob[:, HH * half:HH * half + HH, :]
                act.activation(part, part, ACT.Exp).then_inc(expd, 1)

            def square(n):
                act.wait_ge(centred, n + 1)
                act.activation(sq[:, :], cen[:, :], ACT.Square).then_inc(squared, 1)

            def group_rstd(n):
                act.wait_ge(varsum, n + 1)
                act.activation(gvar[:, :], gvar[:, :], ACT.Ln, bias=EPS, scale=1.0 / WD).then_inc(logged, 1)
                act.wait_ge(logged, n + 1)
                act.activation(grs[:, :], gvar[:, :], ACT.Exp, scale=-0.5).then_inc(grstd, 1)

            def copy_pT(n, half):
                act.wait_ge(pT_ps, 2 * n + 1 + half)
                if not isinstance(n, int) or n:
                    act.wait_ge(pv_ps, 2 * n - 1 + half)
                act.copy(pT[:, HP * half:HP * half + HP, :].rearrange("p c n -> p (c n)"), ps[:, 4 + 2 * half, :])\
                    .then_inc(pT_sb, 1)

            def exps_0(n):
                exps(n, 0)

            def exps_1(n):
                exps(n, 1)

            def copy_pT_0(n):
                copy_pT(n, 0)

            def copy_pT_1(n):
                copy_pT(n, 1)

            def copy_oT(n):
                act.wait_ge(oT_ps, n + 1)
                act.wait_ge(proj_ps, n)
                act.copy(oT[:, :], ps[:, T_OUT, 0:P]).then_inc(oT_sb, 1)

            def copy_v(n):
                act.wait_ge(v_ps, n + 1)
                act.wait_ge(pv_ps, 2 * n)
                for h in range(2):
                    rows = slice(64 * h, 64 * h + 64)
                    src = ps[rows, T_V, 0:2 * 64].rearrange("p (w c d) -> p w c d", w=2, d=WD)
                    last = act.copy(vz[rows, :, :, h, 0:WD], src)
                last.then_inc(v_sb, 1)

            def copy_kT(n):
                act.wait_ge(kT_ps, n + 1)
                act.wait_ge(scored, 2 * n)
                act.activation(kT[:, :], ps[:, T_QK, 0:P], ACT.Identity, bias=bet_col[:, :], scale=gam_col[:, :])\
                    .then_inc(kT_sb, 1)

            act.wait_ge(columns, 2)
            pipeline(act, NT, [(copy_oT, 3), (square, 1), (group_rstd, 1), (exps_0, 2), (exps_1, 2), (copy_pT_0, 2),
                               (copy_kT, 1), (copy_pT_1, 2), (copy_xT, 0), (copy_v, 1)])

        @block.vector
        def _(dve):
            dve.wait_ge(const_in, 16 * N_CONST)
            for k, (row, column, by_lane) in enumerate(((gam, gam_col, gam_lane), (bet, bet_col, bet_lane))):
                dve.tensor_tensor(spread[:, k, :].rearrange("p (g d) -> p g d", d=WD),
                                  ident[:, :].rearrange("p (g d) -> p g d", d=WD),
                                  row[:, :].unsqueeze(1).to_broadcast([P, WH, WD]), ALU.mult).then_inc(spread_sb, 1)
                dve.wait_ge(spread_sb, k + 1)
                dve.tensor_reduce(column[:, :], spread[:, k, :], AX, ALU.add).then_inc(columns, 1)
                dve.wait_ge(columns, k + 1)
                dve.tensor_scalar(by_lane[:, :], lane[:, :], column[:, :], None, ALU.mult).then_inc(lanes, 1)
            dve.wait_ge(lanes, 2)

            def normalize(n):
                dve.wait_ge(rstd, n + 1)
                dve.wait_ge(xT_ps, n)
                dve.tensor_scalar(xn[:, :], X[:, ds(n, 1), :].rearrange("p a d -> p (a d)"), mv[:, 0:1], rs[:, :],
                                  ALU.subtract, ALU.mult).then_inc(normed, 1)

            def input_stats(n):
                dve.wait_ge(const_in, 16)
                dve.wait_ge(x_in, 16 * (n // 8 + 1))
                dve.wait_ge(normed, n)
                dve.bn_stats(st[:, :], X[:, ds(n, 1), :].rearrange("p a d -> p (a d)")).then_inc(stats, 1)
                dve.wait_ge(const_in, 16)
                dve.wait_ge(stats, n + 1)
                dve.bn_aggr(mv[:, :], st[:, :]).then_inc(meanvar, 1)

            qk3 = ps[:, T_QK, 0:2 * P].rearrange("p (g d) -> p g d", d=WD)

            def g3(t):
                return t[:, :].rearrange("p (g d) -> p g d", d=WD)

            def wide(t):
                return t[:, :].unsqueeze(2).to_broadcast([P, 2 * WH, WD])

            def centre(n):
                dve.wait_ge(qk_ps, n + 1)
                dve.tensor_reduce(gsum[:, :], qk3, AX, ALU.add).then_inc(summed, 1)
                dve.wait_ge(summed, n + 1)
                dve.tensor_scalar(gsum[:, :], gsum[:, :], 1.0 / WD, None, ALU.mult).then_inc(meaned, 1)
                dve.wait_ge(meaned, n + 1)
                dve.tensor_tensor(g3(cen), qk3, wide(gsum), ALU.subtract).then_inc(centred, 1)

            def group_variance(n):
                dve.wait_ge(squared, n + 1)
                dve.wait_ge(grstd, n)
                dve.tensor_reduce(gvar[:, :], g3(sq), AX, ALU.add).then_inc(varsum, 1)

            def qk_normal(n):
                dve.wait_ge(grstd, n + 1)
                dve.wait_ge(kT_ps, n)
                dve.tensor_tensor(g3(qk), g3(cen), wide(grs), ALU.mult).then_inc(qk_sb, 1)

            def mask_q(n):
                dve.wait_ge(qT_ps, n + 1)
                dve.wait_ge(scored, 2 * n)
                for j in range(4):
                    last = dve.tensor_scalar(qm[:, j, :], ps[:, T_QT, 0:P], gam_lane[:, j:j + 1], bet_lane[:, j:j + 1],
                                             ALU.mult, ALU.add)
                last.then_inc(qm_sb, 1)

            def softmax_shift(n, half):
                s4 = ps[:, 4 + 2 * half:6 + 2 * half, 0:4 * WIN].rearrange("p r (j k) -> p r j k", k=WIN)
                heads = slice(HH * half, HH * half + HH)
                mx4 = mx[:, heads].rearrange("p (r j) -> p r j", j=4)
                dve.wait_ge(scored, 2 * n + 1 + half)
                dve.tensor_reduce(mx4, s4, AX, ALU.max).then_inc(maxed, 1)
                dve.wait_ge(maxed, 2 * n + 1 + half)
                if not isinstance(n, int) or n:
                    dve.wait_ge(pT_ps, 2 * n - 1 + half)
                dve.tensor_tensor(prob[:, heads, :].rearrange("p (r j) k -> p r j k", j=4), s4,
                                  mx4.unsqueeze(3).to_broadcast([P, 2, 4, WIN]), ALU.subtract).then_inc(shifted, 1)

            def softmax_shift_0(n):
                softmax_shift(n, 0)

            def softmax_shift_1(n):
                softmax_shift(n, 1)

            def divide(n, half):
                heads = slice(HH * half, HH * half + HH)
                dve.wait_ge(pv_ps, 2 * n + 1 + half)
                dve.reciprocal(rden[:, heads].unsqueeze(2), result_half(half)[:, :, WD:WD + 1]).then_inc(recip, 1)
                dve.wait_ge(recip, 2 * n + 1 + half)
                dve.wait_ge(oT_ps, n)
                dve.tensor_tensor(o[:, :].rearrange("p (h d) -> p h d", d=WD)[:, heads, :],
                                  result_half(half)[:, :, 0:WD],
                                  rden[:, heads].unsqueeze(2).to_broadcast([P, HH, WD]), ALU.mult).then_inc(o_sb, 1)

            def divide_0(n):
                divide(n, 0)

            def divide_1(n):
                divide(n, 1)

            def result_stats(n):
                dve.wait_ge(proj_ps, n + 1)
                dve.wait_ge(yn_sb, n)
                dve.tensor_tensor(y[:, :], ps[:, T_OUT, P:2 * P], bproj[:, :], ALU.add).then_inc(y_sb, 1)
                dve.wait_ge(const_in, 16)
                dve.wait_ge(y_sb, n + 1)
                dve.bn_stats(st2[:, :], y[:, :]).then_inc(stats2, 1)
                dve.wait_ge(const_in, 16)
                dve.wait_ge(stats2, n + 1)
                dve.bn_aggr(mv2[:, :], st2[:, :]).then_inc(meanvar2, 1)

            def add_result(n):
                Xn = X[:, ds(n, 1), :].rearrange("p a d -> p (a d)")
                dve.wait_ge(rstd2, n + 1)
                dve.tensor_scalar(yn[:, :], y[:, :], mv2[:, 0:1], rs2[:, :], ALU.subtract, ALU.mult)\
                    .then_inc(yn_sb, 1)
                dve.wait_ge(yn_sb, n + 1)
                dve.tensor_tensor(Xn, Xn, yn[:, :], ALU.add).then_inc(added, 1)
                dve.wait_ge(const_in, 16)
                dve.wait_ge(added, n + 1)
                dve.bn_stats(st3[:, :], Xn).then_inc(stats3, 1)
                dve.wait_ge(const_in, 16)
                dve.wait_ge(stats3, n + 1)
                dve.wait_ge(out, n)
                dve.bn_aggr(mv3[:, :], st3[:, :]).then_inc(meanvar3, 1)

            def next_input(n):
                dve.wait_ge(rstd3, n + 1)
                dve.tensor_scalar(Y[:, ds(n + 8, 1), :].rearrange("p a d -> p (a d)"),
                                  X[:, ds(n, 1), :].rearrange("p a d -> p (a d)"), mv3[:, 0:1], rs3[:, :],
                                  ALU.subtract, ALU.mult).then_inc(out, 1)

            pipeline(dve, NT, [(centre, 2), (next_input, 6), (add_result, 5), (group_variance, 2), (input_stats, 1),
                               (softmax_shift_0, 3), (qk_normal, 2), (softmax_shift_1, 3), (mask_q, 2),
                               (normalize, 1), (result_stats, 4), (divide_0, 3), (divide_1, 3)])
            dve.wait_ge(out, NT)


def local_transformer(nc, ps, Y, A, w_qkv, q_scale, k_scale, w_o, ln_g, ln_b, w_1, b_1, w_2, b_2,
                      c_ident, c_shift, c_carry, c_masks, c_rot):
    with ExitStack() as ctx:
        def sb(name, shape, dt=F32):
            return ctx.enter_context(nc.sbuf_tensor("lt_" + name, shape, dt))

        def sem(name):
            return nc.alloc_semaphore("lt_" + name)

        ident, shift, carry = sb("ident", [P, P]), sb("shift", [P, P]), sb("carry", [P, P])
        ident16 = sb("ident16", [P, P], BF16)
        masks = sb("masks", [P, NB + 1, P])
        masks16 = sb("masks16", [P, NB + 1, LP * P], BF16)
        rot_base, rot = sb("rot_base", [P, NB, 4 * LD]), sb("rot", [P, NB, 2, 2, LD])
        qk_scale = sb("qk_scale", [P, 2, 2, LD])
        wqkv, wo = sb("wqkv", [P, 3 * INNER]), sb("wo", [P, 4, P])
        h, hT = sb("h", [P, P]), sb("hT", [P, P])
        sq = sb("sq", [P, 2 * INNER])
        ssum, rn = sb("ssum", [P, 2 * LH]), sb("rn", [P, 2 * LH])
        raw = sb("raw", [P, 2 * INNER])
        t_cos, t_sin = sb("t_cos", [P, 2 * INNER]), sb("t_sin", [P, 2 * INNER])
        qz = sb("qz", [P, LP, 2, 2, WIN])
        kT = sb("kT", [P, LP, P])
        k_last = sb("k_last", [P, 8, LP, WIN])
        v_next, v = sb("v_next", [P, INNER]), sb("v", [P, LH, LD + 1])
        v_pair = sb("v_pair", [P, 8, LH, LD + 1])
        mx = sb("mx", [P, 2, LP])
        prob, pT = sb("prob", [P, 2, LP, P]), sb("pT", [P, 2, LP * P])
        rden = sb("rden", [P, LH])
        o, oT = sb("o", [P, INNER]), sb("oT", [P, INNER])
        w1, w2 = sb("w1", [P, 2 * HID]), sb("w2", [P, 3, P])
        b1a, b1g = sb("b1a", [P, 3]), sb("b1g", [P, 3])
        lg, lb, b2 = sb("lg", [P, 1]), sb("lb", [P, 1]), sb("b2", [P, P])
        mean, var, eps4, power4 = sb("mean", [P, 4]), sb("var", [P, 4]), sb("eps4", [P, 4]), sb("power4", [P, 4])
        frs = sb("frs", [P, 4])
        cen, fsq, hn = sb("cen", [P, 4, P]), sb("fsq", [P, 4 * P]), sb("hn", [P, 4, P])
        fT = sb("fT", [P, 4 * P])
        gate, hid = sb("gate", [P, 2, 4 * P]), sb("hid", [P, 3, 4 * P])
        ab2 = sb("ab2", [P, 4, P])

        T_H, T_QK, T_V, T_S, T_O = 0, 1, 3, 4, 6
        F_H, F_T, F_A, F_G, F_Y = 0, 1, 2, 4, 6

        zeroed, const_in, const16 = sem("zeroed"), sem("const_in"), sem("const16")
        attn_w, ffn_w, rot_ready = sem("attn_w"), sem("ffn_w"), sem("rot_ready")
        cleared = sem("cleared")
        h_ps, h_sb, hT_ps, hT_sb, qk_ps, v_ps = (sem("h_ps"), sem("h_sb"), sem("hT_ps"), sem("hT_sb"), sem("qk_ps"),
                                                sem("v_ps"))
        squared, summed, clipped, logged, rnorm, united = (sem("squared"), sem("summed"), sem("clipped"),
                                                           sem("logged"), sem("rnorm"), sem("united"))
        cos_done, sin_done, roped, qkT_ps, q_sb, k_sb, v_sb = (sem("cos_done"), sem("sin_done"), sem("roped"),
                                                               sem("qkT_ps"), sem("q_sb"), sem("k_sb"), sem("v_sb"))
        v_moved = sem("v_moved")
        raw_sb = sem("raw_sb")
        k_carried, v_carried = sem("k_carried"), sem("v_carried")
        scored, maxed, shifted, expd = sem("scored"), sem("maxed"), sem("shifted"), sem("expd")
        pT_ps, pT_sb, pv_ps, recip, o_sb = sem("pT_ps"), sem("pT_sb"), sem("pv_ps"), sem("recip"), sem("o_sb")
        oT_ps, oT_sb, wo_ps, a_sb = sem("oT_ps"), sem("oT_sb"), sem("wo_ps"), sem("a_sb")
        fh_ps, fmean, fscaled, fcen, fsqd, fvar, feps, frstd, fhn, fT_ps, fT_sb = (
            sem("fh_ps"), sem("fmean"), sem("fscaled"), sem("fcen"), sem("fsqd"), sem("fvar"), sem("feps"),
            sem("frstd"), sem("fhn"), sem("fT_ps"), sem("fT_sb"))
        fa_ps, gelu_sb, hid_sb, fy_ps, ab2_sb, y_sb = (sem("fa_ps"), sem("gelu_sb"), sem("hid_sb"), sem("fy_ps"),
                                                       sem("ab2_sb"), sem("y_sb"))
        N_CONST, N_ATTN_W, N_FFN_W, N_ZERO = 5, 8, 13, 8

        block = ctx.enter_context(nc.Block())

        @block.sync
        def _(sp):
            for dst, src in ((ident[:, :], c_ident), (shift[:, :], c_shift), (carry[:, :], c_carry),
                             (masks[:, :, :], c_masks.rearrange("p (i k) -> p i k", k=P)),
                             (rot_base[:, :, :], c_rot.rearrange("p (i k) -> p i k", i=NB))):
                sp.dma_start(dst, src).then_inc(const_in, 16)
            half = LD // 2
            with sp.Fori(0, LAYERS) as l:
                sp.wait_ge(a_sb, l * NT)
                one = ds(l, 1)
                sp.dma_start(wqkv[:, :], w_qkv[one, :, :].rearrange("a p n -> (a p) n")).then_inc(attn_w, 16)
                sp.dma_start(wo[:, :, :], w_o[one, :, :].rearrange("a (c p) n -> p (a c) n", p=P)).then_inc(attn_w, 16)
                for i, scale in enumerate((q_scale, k_scale)):
                    row = scale[one, :]
                    sp.dma_start(qk_scale[:, 0, i, :], row.to_broadcast([P, LD])).then_inc(attn_w, 16)
                    sp.dma_start(qk_scale[:, 1, i, 0:half], scale[one, half:LD].to_broadcast([P, half]))\
                        .then_inc(attn_w, 16)
                    sp.dma_start(qk_scale[:, 1, i, half:LD], scale[one, 0:half].to_broadcast([P, half]))\
                        .then_inc(attn_w, 16)
                sp.wait_ge(y_sb, l * NG)
                sp.dma_start(w1[:, :], w_1[one, :, :].rearrange("a p n -> (a p) n")).then_inc(ffn_w, 16)
                for c, (at, size) in enumerate(HC):
                    sp.dma_start(w2[0:size, c, :], w_2[one, at:at + size, :].rearrange("a p n -> (a p) n"))\
                        .then_inc(ffn_w, 16)
                    sp.dma_start(b1a[0:size, c:c + 1], b_1[one, at:at + size].rearrange("a p -> p a"))\
                        .then_inc(ffn_w, 16)
                    sp.dma_start(b1g[0:size, c:c + 1], b_1[one, HID + at:HID + at + size].rearrange("a p -> p a"))\
                        .then_inc(ffn_w, 16)
                sp.dma_start(lg[:, :], ln_g[one, :].rearrange("a p -> p a")).then_inc(ffn_w, 16)
                sp.dma_start(lb[:, :], ln_b[one, :].rearrange("a p -> p a")).then_inc(ffn_w, 16)
                sp.dma_start(b2[:, :], b_2[one, :].to_broadcast([P, P])).then_inc(ffn_w, 16)

        @block.gpsimd
        def _(pool):
            pool.memset(A[:, 0:8, :], 0.0).then_inc(zeroed, 1)
            pool.memset(qz[:, :, :, :, :], 0.0).then_inc(zeroed, 1)
            pool.memset(v[:, :, LD:LD + 1], 1.0).then_inc(zeroed, 1)
            pool.memset(v_pair[:, :, :, LD:LD + 1], 1.0).then_inc(zeroed, 1)
            pool.memset(eps4[:, :], EPS * P).then_inc(zeroed, 1)
            pool.memset(power4[:, :], -0.5).then_inc(zeroed, 1)
            pool.memset(k_last[:, :, :, :], 0.0).then_inc(zeroed, 1)
            pool.wait_ge(zeroed, N_ZERO - 1)
            pool.memset(v_pair[64:128, :, :, 0:LD], 0.0).then_inc(zeroed, 1)
            pool.wait_ge(zeroed, N_ZERO)
            half = LD // 2

            with pool.Fori(0, LAYERS) as l:
                pool.wait_ge(rot_ready, l + 1)

                def rotate(n):
                    m = l * NT + n
                    pool.wait_ge(raw_sb, 2 * m + 2)
                    pool.wait_ge(roped, m)
                    u = raw[:, :].rearrange("p (a h d) -> p a h d", a=2, d=LD)
                    t = t_sin[:, :].rearrange("p (a h d) -> p a h d", a=2, d=LD)
                    r = rot[:, ds(n // 8, 1), 1, :, :].rearrange("p i a d -> p (i a) d")
                    for to, frm in ((slice(0, half), slice(half, LD)), (slice(half, LD), slice(0, half))):
                        pool.tensor_tensor(t[:, :, :, to], u[:, :, :, frm],
                                           r[:, :, to].unsqueeze(2).to_broadcast([P, 2, LH, half]), ALU.mult)\
                            .then_inc(sin_done, 1)

                def rope(n):
                    m = l * NT + n
                    pool.wait_ge(cos_done, m + 1)
                    pool.wait_ge(sin_done, 2 * m + 2)
                    pool.tensor_tensor(t_cos[:, :], t_cos[:, :], t_sin[:, :], ALU.add).then_inc(roped, 1)

                def carry_k(n):
                    if isinstance(n, int) and n == NT - 1:
                        return
                    pool.wait_ge(scored, 2 * (l * NT + n) + 2)
                    pool.tensor_copy(k_last[:, ds(n % 8, 1), :, :].rearrange("p a c k -> p (a c) k"),
                                     kT[:, :, WIN:P]).then_inc(k_carried, 1)

                pipeline(pool, NT, [(rotate, 0), (rope, 0), (carry_k, 1)])

                def rsqrt(g):
                    m = l * NG + g
                    pool.wait_ge(fvar, m + 1)
                    pool.tensor_tensor(frs[:, :], var[:, :], eps4[:, :], ALU.add).then_inc(feps, 1)
                    pool.wait_ge(feps, m + 1)
                    pool.tensor_tensor(frs[:, :], frs[:, :], power4[:, :], ALU.pow).then_inc(frstd, 1)

                def add_b2(g):
                    m = l * NG + g
                    pool.wait_ge(y_sb, m)
                    pool.tensor_tensor(ab2[:, :, :], A[:, ds(8 + 4 * g, 4), :],
                                       b2[:, :].unsqueeze(1).to_broadcast([P, 4, P]), ALU.add).then_inc(ab2_sb, 1)

                pool.wait_ge(ffn_w, 16 * N_FFN_W * (l + 1))
                pipeline(pool, NG, [(rsqrt, 0), (add_b2, 1)])
                pool.memset(k_last[:, :, :, :], 0.0).then_inc(cleared, 1)

        @block.tensor
        def _(pe):
            pe.wait_ge(const_in, 16 * N_CONST)
            pe.wait_ge(const16, 2)
            pe.wait_ge(zeroed, N_ZERO)
            with pe.Fori(0, LAYERS) as l:
                pe.wait_ge(attn_w, 16 * N_ATTN_W * (l + 1))
                pe.wait_ge(y_sb, l * NG)

                def tokens(src, n, count, half):
                    return src[:, ds(n, count), 64 * half:64 * half + 64]

                def shift_h(n):
                    m = l * NT + n
                    pe.wait_ge(a_sb, l * NT if isinstance(n, int) and n < 3 else m - 3)
                    pe.wait_ge(hT_sb, m)
                    one = "p a d -> p (a d)"
                    pe.matmul(ps[:, T_H, 0:64], ident[:, :], tokens(Y, n + 8, 1, 0).rearrange(one),
                              start=True, stop=True)
                    pe.matmul(ps[:, T_H, 64:128], shift[:, :], tokens(Y, n + 8, 1, 1).rearrange(one),
                              start=True, stop=False)
                    pe.matmul(ps[:, T_H, 64:128], carry[:, :], tokens(Y, n, 1, 1).rearrange(one),
                              start=False, stop=True).then_inc(h_ps, 1)

                def turn_h(n):
                    m = l * NT + n
                    pe.wait_ge(h_sb, m + 1)
                    pe.transpose(ps[:, T_H, P:2 * P], h[:, :], ident[:, :]).then_inc(hT_ps, 1)

                def qk(n):
                    m = l * NT + n
                    pe.wait_ge(hT_sb, m + 1)
                    pe.wait_ge(k_sb, m)
                    pe.wait_ge(q_sb, 2 * m)
                    for i in range(2):
                        mm = pe.matmul(ps[:, T_QK + i, :], hT[:, :], wqkv[:, i * INNER:(i + 1) * INNER],
                                       start=True, stop=True)
                        mm.then_inc(qk_ps, 1)

                def values(n):
                    m = l * NT + n
                    pe.wait_ge(hT_sb, m + 1)
                    pe.wait_ge(oT_sb, l * NT if isinstance(n, int) and n < 2 else m - 2)
                    pe.matmul(ps[:, T_V, :], hT[:, :], wqkv[:, 2 * INNER:3 * INNER], start=True, stop=True)\
                        .then_inc(v_ps, 1)

                def turn_qk(n):
                    m = l * NT + n
                    pe.wait_ge(united, m + 1)
                    pe.wait_ge(raw_sb, 2 * m + 2)
                    for c in range(8):
                        mm = pe.transpose(ps[:, T_QK + c // 4, P * (c % 4):P * (c % 4) + P],
                                          t_cos[:, P * c:P * c + P], ident[:, :])
                    mm.then_inc(qkT_ps, 1)

                def score(n):
                    m = l * NT + n
                    pe.wait_ge(q_sb, 2 * m + 2)
                    pe.wait_ge(k_sb, m + 1)
                    for w in range(2):
                        pe.wait_ge(pT_sb, 2 * m)
                        i = NB if w else n // 8
                        pe.matmul(ps[:, T_S + w, :], ident16[:, :],
                                  masks16[:, ds(i, 1), :].rearrange("p a k -> p (a k)"),
                                  start=True, stop=False, skip_group_check=True)
                        for c in range(LP):
                            q = qz[:, c, w, :, :].rearrange("p a k -> p (a k)")
                            out = ps[:, T_S + w, P * c:P * c + P]
                            if w:
                                mm = pe.matmul(out, q, kT[:, c, :], start=False, stop=True, skip_group_check=True)
                                continue
                            if c == 0:
                                pe.wait_ge(k_carried, l * (NT - 1) + n)
                                pe.wait_ge(cleared, 2 * l)
                            pe.matmul(out[:, 0:WIN], q, kT[:, c, 0:WIN], start=False, stop=True,
                                      skip_group_check=True)
                            mm = pe.matmul(out[:, WIN:P], q,
                                           k_last[:, ds(n % 8, 1), c, :].rearrange("p a k -> p (a k)"),
                                           start=False, stop=True, skip_group_check=True)
                        mm.then_inc(scored, 1)

                def turn_p(n, w):
                    m = l * NT + n
                    pe.wait_ge(expd, 2 * m + 1 + w)
                    for c in range(LP):
                        mm = pe.transpose(ps[:, T_S + w, P * c:P * c + P], prob[:, w, c, :], ident[:, :])
                    mm.then_inc(pT_ps, 1)

                def turn_p_0(n):
                    turn_p(n, 0)

                def turn_p_1(n):
                    turn_p(n, 1)

                def attend(n):
                    m = l * NT + n
                    pe.wait_ge(v_moved, m + 1)
                    pe.wait_ge(v_sb, 2 * m + 2)
                    pe.wait_ge(cleared, 2 * l)
                    pe.wait_ge(v_carried, m)
                    pe.wait_ge(o_sb, m)
                    for w in range(2):
                        pe.wait_ge(pT_sb, 2 * m + 1 + w)
                        for i in range(LH):
                            out = ps[64 * w:64 * w + 64, T_O + i // 4, 65 * (i % 4):65 * (i % 4) + 65]
                            rhs = v[:, i, :] if w else \
                                v_pair[:, ds(n % 8, 1), i, :].rearrange("p a d -> p (a d)")
                            mm = pe.matmul(out, pT[:, w, WIN * i:WIN * i + WIN], rhs, start=True, stop=True)
                        mm.then_inc(pv_ps, 1)

                def turn_o(n):
                    m = l * NT + n
                    pe.wait_ge(o_sb, m + 1)
                    ahead = min(n + 2, NT - 1) if isinstance(n, int) else n + 2
                    pe.wait_ge(v_sb, 2 * (l * NT + ahead) + 2)
                    for c in range(4):
                        mm = pe.transpose(ps[:, T_V, P * c:P * c + P], o[:, P * c:P * c + P], ident[:, :])
                    mm.then_inc(oT_ps, 1)

                def project(n):
                    m = l * NT + n
                    ahead = min(n + 4, NT) if isinstance(n, int) else n + 4
                    pe.wait_ge(hT_sb, l * NT + ahead)
                    pe.wait_ge(a_sb, m)
                    pe.wait_ge(oT_sb, m + 1)
                    for c in range(4):
                        mm = pe.matmul(ps[:, T_H, 2 * P:3 * P], oT[:, P * c:P * c + P], wo[:, c, :],
                                       start=(c == 0), stop=(c == 3))
                    mm.then_inc(wo_ps, 1)

                pipeline(pe, NT, [(values, 1), (qk, 1), (score, 2), (shift_h, 0), (turn_o, 3), (turn_h, 0),
                                  (turn_p_0, 2), (project, 3), (turn_p_1, 2), (attend, 2), (turn_qk, 1)])

                pe.wait_ge(a_sb, (l + 1) * NT)
                pe.wait_ge(ffn_w, 16 * N_FFN_W * (l + 1))

                def f_shift(g):
                    m = l * NG + g
                    pe.wait_ge(fcen, m)
                    out = ps[:, F_H, :].rearrange("p (t d) -> p t d", d=P)
                    pe.matmul(out[:, :, 0:64], ident[:, :], tokens(A, 4 * g + 8, 4, 0), start=True, stop=True)
                    pe.matmul(out[:, :, 64:128], shift[:, :], tokens(A, 4 * g + 8, 4, 1), start=True, stop=False)
                    pe.matmul(out[:, :, 64:128], carry[:, :], tokens(A, 4 * g, 4, 1), start=False, stop=True)\
                        .then_inc(fh_ps, 1)

                def f_turn(g):
                    m = l * NG + g
                    pe.wait_ge(fhn, m + 1)
                    pe.wait_ge(fT_sb, m)
                    for t in range(4):
                        mm = pe.transpose(ps[:, F_T, P * t:P * t + P], hn[:, t, :], ident[:, :])
                    mm.then_inc(fT_ps, 1)

                def f_up(g):
                    m = l * NG + g
                    pe.wait_ge(fT_sb, m + 1)
                    for c, (at, size) in enumerate(HC):
                        pe.wait_ge(hid_sb, 3 * m + (c - 1 if c else 0))
                        for bank, col in ((F_A, at), (F_G, HID + at)):
                            mm = pe.matmul(ps[0:size, bank + c % 2, :], w1[:, col:col + size], fT[:, :],
                                           start=True, stop=True)
                        mm.then_inc(fa_ps, 1)

                def f_down(g):
                    m = l * NG + g
                    pe.wait_ge(hid_sb, 3 * m + 3)
                    pe.wait_ge(y_sb, m)
                    for t in range(4):
                        for c, (at, size) in enumerate(HC):
                            mm = pe.matmul(ps[:, F_Y, P * t:P * t + P], hid[0:size, c, P * t:P * t + P],
                                           w2[0:size, c, :], start=(c == 0), stop=(c == 2))
                    mm.then_inc(fy_ps, 1)

                pipeline(pe, NG, [(f_shift, 0), (f_turn, 1), (f_down, 2), (f_up, 1)])

        @block.scalar
        def _(act):
            act.wait_ge(zeroed, N_ZERO)
            with act.Fori(0, LAYERS) as l:
                act.preload_act_table_set("natural_log_exp_and_others")

                def copy_h(n):
                    m = l * NT + n
                    act.wait_ge(h_ps, m + 1)
                    act.wait_ge(hT_ps, m)
                    act.copy(h[:, :], ps[:, T_H, 0:P]).then_inc(h_sb, 1)

                def copy_hT(n):
                    m = l * NT + n
                    act.wait_ge(hT_ps, m + 1)
                    act.wait_ge(qk_ps, 2 * m)
                    act.wait_ge(v_ps, m)
                    act.copy(hT[:, :], ps[:, T_H, P:2 * P]).then_inc(hT_sb, 1)

                def copy_and_square(n):
                    m = l * NT + n
                    for i in range(2):
                        act.wait_ge(qk_ps, 2 * m + 1 + i)
                        act.wait_ge(cos_done, m)
                        act.wait_ge(sin_done, 2 * m)
                        act.copy(raw[:, i * INNER:(i + 1) * INNER], ps[:, T_QK + i, :]).then_inc(raw_sb, 1)
                    act.wait_ge(raw_sb, 2 * m + 2)
                    act.wait_ge(summed, m)
                    act.activation(sq[:, :], raw[:, :], ACT.Square)\
                        .then_inc(squared, 1)

                def rnorms(n):
                    m = l * NT + n
                    act.wait_ge(clipped, m + 1)
                    act.activation(rn[:, :], ssum[:, :], ACT.Ln).then_inc(logged, 1)
                    act.wait_ge(logged, m + 1)
                    act.activation(rn[:, :], rn[:, :], ACT.Exp, scale=-0.5).then_inc(rnorm, 1)

                def exps(n, w):
                    m = l * NT + n
                    act.wait_ge(shifted, 2 * m + 1 + w)
                    part = prob[:, w, :, :]
                    act.activation(part, part, ACT.Exp).then_inc(expd, 1)

                def exps_0(n):
                    exps(n, 0)

                def exps_1(n):
                    exps(n, 1)

                def copy_pT(n, w):
                    m = l * NT + n
                    act.wait_ge(pT_ps, 2 * m + 1 + w)
                    act.wait_ge(pv_ps, 2 * m)
                    act.copy(pT[:, w, :], ps[:, T_S + w, :]).then_inc(pT_sb, 1)

                def copy_pT_0(n):
                    copy_pT(n, 0)

                def copy_pT_1(n):
                    copy_pT(n, 1)

                def copy_v(n):
                    m = l * NT + n
                    act.wait_ge(v_ps, m + 1)
                    act.wait_ge(v_moved, m)
                    vv = ps[:, T_V, :].rearrange("p (h d) -> p h d", d=LD)
                    act.copy(v_next[:, :], ps[:, T_V, :]).then_inc(v_sb, 1)
                    act.copy(v_pair[0:64, ds(n % 8, 1), :, 0:LD].rearrange("p a h d -> p (a h) d"), vv[0:64, :, :])\
                        .then_inc(v_sb, 1)

                def carry_v(n):
                    m = l * NT + n
                    act.wait_ge(v_moved, m + 1)
                    act.wait_ge(pv_ps, 2 * m + 2)
                    act.copy(v_pair[64:128, ds(n % 8, 1), :, 0:LD].rearrange("p a h d -> p (a h) d"),
                             v[64:128, :, 0:LD]).then_inc(v_carried, 1)

                def move_v(n):
                    m = l * NT + n
                    act.wait_ge(v_sb, 2 * m + 2)
                    act.wait_ge(v_carried, m)
                    act.copy(v[:, :, 0:LD], v_next[:, :].rearrange("p (h d) -> p h d", d=LD)).then_inc(v_moved, 1)

                def copy_q(n):
                    m = l * NT + n
                    act.wait_ge(qkT_ps, m + 1)
                    act.wait_ge(scored, 2 * m)
                    qT = ps[:, T_QK, :].rearrange("p (c w k) -> p c w k", c=LP, w=2)
                    for i in range(2):
                        rows = slice(64 * i, 64 * i + 64)
                        act.copy(qz[rows, :, :, i, :], qT[rows, :, :, :]).then_inc(q_sb, 1)

                def copy_oT(n):
                    m = l * NT + n
                    act.wait_ge(oT_ps, m + 1)
                    act.wait_ge(wo_ps, m)
                    act.copy(oT[:, :], ps[:, T_V, :]).then_inc(oT_sb, 1)

                pipeline(act, NT, [(copy_and_square, 1), (copy_v, 1), (exps_0, 2), (copy_h, 0), (copy_oT, 3),
                                   (copy_hT, 0), (exps_1, 2), (copy_pT_0, 2), (rnorms, 1), (copy_pT_1, 2),
                                   (copy_q, 1), (carry_v, 2), (move_v, 1)])

                act.preload_act_table_set("gelu_and_others")
                act.wait_ge(ffn_w, 16 * N_FFN_W * (l + 1))

                def f_square(g):
                    m = l * NG + g
                    act.wait_ge(fcen, m + 1)
                    act.wait_ge(fvar, m)
                    act.activation(fsq[:, :], cen[:, :, :].rearrange("p t d -> p (t d)"), ACT.Square)\
                        .then_inc(fsqd, 1)

                def f_copy(g):
                    m = l * NG + g
                    act.wait_ge(fT_ps, m + 1)
                    act.wait_ge(fa_ps, 3 * m)
                    act.activation(fT[:, :], ps[:, F_T, :], ACT.Identity, bias=lb[:, :], scale=lg[:, :])\
                        .then_inc(fT_sb, 1)

                def f_gelu(g):
                    m = l * NG + g
                    for c, (at, size) in enumerate(HC):
                        act.wait_ge(fa_ps, 3 * m + c + 1)
                        act.wait_ge(hid_sb, 3 * m + (c - 1 if c else 0))
                        act.activation(gate[0:size, c % 2, :], ps[0:size, F_G + c % 2, :], ACT.Gelu,
                                       bias=b1g[0:size, c:c + 1]).then_inc(gelu_sb, 1)

                pipeline(act, NG, [(f_copy, 1), (f_square, 0), (f_gelu, 1)])

        @block.vector
        def _(dve):
            dve.wait_ge(const_in, 16 * N_CONST)
            dve.tensor_copy(ident16[:, :], ident[:, :]).then_inc(const16, 1)
            dve.tensor_copy(masks16[:, :, :].rearrange("p i (c k) -> p i c k", c=LP),
                            masks[:, :, :].unsqueeze(2).to_broadcast([P, NB + 1, LP, P])).then_inc(const16, 1)
            with dve.Fori(0, LAYERS) as l:
                dve.wait_ge(attn_w, 16 * N_ATTN_W * (l + 1))
                dve.tensor_tensor(rot[:, :, :, :, :].rearrange("p i a b d -> p i (a b d)"), rot_base[:, :, :],
                                  qk_scale[:, :, :, :].rearrange("p a b d -> p (a b d)").unsqueeze(1)
                                  .to_broadcast([P, NB, 4 * LD]), ALU.mult).then_inc(rot_ready, 1)
                dve.wait_ge(rot_ready, l + 1)

                def norm_squares(n):
                    m = l * NT + n
                    dve.wait_ge(squared, m + 1)
                    dve.wait_ge(rnorm, m)
                    dve.tensor_reduce(ssum[:, :], sq[:, :].rearrange("p (g d) -> p g d", d=LD), AX, ALU.add)\
                        .then_inc(summed, 1)
                    dve.wait_ge(summed, m + 1)
                    dve.tensor_scalar(ssum[:, :], ssum[:, :], 1e-24, None, ALU.max).then_inc(clipped, 1)

                def cosines(n):
                    m = l * NT + n
                    dve.wait_ge(raw_sb, 2 * m + 2)
                    dve.wait_ge(qkT_ps, m)
                    r = rot[:, ds(n // 8, 1), 0, :, :].rearrange("p i a d -> p (i a) d")
                    dve.tensor_tensor(t_cos[:, :].rearrange("p (a h d) -> p a h d", a=2, d=LD),
                                      raw[:, :].rearrange("p (a h d) -> p a h d", a=2, d=LD),
                                      r.unsqueeze(2).to_broadcast([P, 2, LH, LD]), ALU.mult).then_inc(cos_done, 1)

                def unit_length(n):
                    m = l * NT + n
                    dve.wait_ge(roped, m + 1)
                    dve.wait_ge(rnorm, m + 1)
                    t = t_cos[:, :].rearrange("p (g d) -> p g d", d=LD)
                    dve.tensor_tensor(t, t, rn[:, :].unsqueeze(2).to_broadcast([P, 2 * LH, LD]), ALU.mult)\
                        .then_inc(united, 1)

                def copy_k(n):
                    m = l * NT + n
                    dve.wait_ge(qkT_ps, m + 1)
                    dve.wait_ge(scored, 2 * m)
                    dve.wait_ge(k_carried, l * (NT - 1) + n)
                    dve.tensor_copy(kT[:, :, :].rearrange("p c k -> p (c k)"), ps[:, T_QK + 1, :]).then_inc(k_sb, 1)

                def softmax_shift(n, w):
                    m = l * NT + n
                    s = ps[:, T_S + w, :].rearrange("p (c k) -> p c k", k=P)
                    dve.wait_ge(scored, 2 * m + 1 + w)
                    dve.tensor_reduce(mx[:, w, :], s, AX, ALU.max).then_inc(maxed, 1)
                    dve.wait_ge(maxed, 2 * m + 1 + w)
                    dve.wait_ge(pT_ps, 2 * m)
                    dve.tensor_tensor(prob[:, w, :, :], s, mx[:, w, :].unsqueeze(2).to_broadcast([P, LP, P]),
                                      ALU.subtract).then_inc(shifted, 1)

                def softmax_shift_0(n):
                    softmax_shift(n, 0)

                def softmax_shift_1(n):
                    softmax_shift(n, 1)

                def divide(n):
                    m = l * NT + n
                    out = ps[:, T_O:T_O + 2, 0:4 * (LD + 1)].rearrange("p a (h d) -> p a h d", d=LD + 1)
                    r = rden[:, :].rearrange("p (a h) -> p a h", a=2)
                    dve.wait_ge(pv_ps, 2 * m + 2)
                    dve.reciprocal(r.unsqueeze(3), out[:, :, :, LD:LD + 1]).then_inc(recip, 1)
                    dve.wait_ge(recip, m + 1)
                    dve.wait_ge(oT_ps, m)
                    dve.tensor_tensor(o[:, :].rearrange("p (a h d) -> p a h d", a=2, d=LD), out[:, :, :, 0:LD],
                                      r.unsqueeze(3).to_broadcast([P, 2, 4, LD]), ALU.mult).then_inc(o_sb, 1)

                def residual(n):
                    m = l * NT + n
                    dve.wait_ge(wo_ps, m + 1)
                    one = "p a d -> p (a d)"
                    dve.tensor_tensor(A[:, ds(n + 8, 1), :].rearrange(one), ps[:, T_H, 2 * P:3 * P],
                                      Y[:, ds(n + 8, 1), :].rearrange(one), ALU.add).then_inc(a_sb, 1)

                pipeline(dve, NT, [(cosines, 1), (softmax_shift_0, 2), (softmax_shift_1, 2), (norm_squares, 1),
                                   (unit_length, 1), (residual, 3), (copy_k, 1), (divide, 2)])

                dve.wait_ge(ffn_w, 16 * N_FFN_W * (l + 1))
                rows4 = ps[:, F_H, :].rearrange("p (t d) -> p t d", d=P)

                def f_centre(g):
                    m = l * NG + g
                    dve.wait_ge(fh_ps, m + 1)
                    dve.tensor_reduce(mean[:, :], rows4, AX, ALU.add).then_inc(fmean, 1)
                    dve.wait_ge(fmean, m + 1)
                    dve.tensor_scalar(mean[:, :], mean[:, :], 1.0 / P, None, ALU.mult).then_inc(fscaled, 1)
                    dve.wait_ge(fscaled, m + 1)
                    dve.wait_ge(fhn, m)
                    dve.tensor_tensor(cen[:, :, :], rows4, mean[:, :].unsqueeze(2).to_broadcast([P, 4, P]),
                                      ALU.subtract).then_inc(fcen, 1)

                def f_variance(g):
                    m = l * NG + g
                    dve.wait_ge(fsqd, m + 1)
                    dve.wait_ge(frstd, m)
                    dve.tensor_reduce(var[:, :], fsq[:, :].rearrange("p (t d) -> p t d", d=P), AX, ALU.add)\
                        .then_inc(fvar, 1)

                def f_scale(g):
                    m = l * NG + g
                    dve.wait_ge(frstd, m + 1)
                    dve.wait_ge(fT_ps, m)
                    dve.scalar_tensor_tensor(out=hn[:, :, :], in0=cen[:, :, :], scalar=float(np.sqrt(P)),
                                             in1=frs[:, :].unsqueeze(2).to_broadcast([P, 4, P]),
                                             op0=ALU.mult, op1=ALU.mult).then_inc(fhn, 1)

                def f_gate(g, c):
                    m = l * NG + g
                    for at, size in HC[c:c + 1]:
                        dve.wait_ge(gelu_sb, 3 * m + c + 1)
                        dve.wait_ge(fy_ps, m)
                        dve.scalar_tensor_tensor(out=hid[0:size, c, :], in0=ps[0:size, F_A + c % 2, :],
                                                 scalar=b1a[0:size, c:c + 1], in1=gate[0:size, c % 2, :],
                                                 op0=ALU.add, op1=ALU.mult).then_inc(hid_sb, 1)

                def f_gate_0(g):
                    f_gate(g, 0)

                def f_gate_1(g):
                    f_gate(g, 1)

                def f_gate_2(g):
                    f_gate(g, 2)

                def f_result(g):
                    m = l * NG + g
                    dve.wait_ge(fy_ps, m + 1)
                    dve.wait_ge(ab2_sb, m + 1)
                    dve.tensor_tensor(Y[:, ds(8 + 4 * g, 4), :], ps[:, F_Y, :].rearrange("p (t d) -> p t d", d=P),
                                      ab2[:, :, :], ALU.add).then_inc(y_sb, 1)

                pipeline(dve, NG, [(f_centre, 0), (f_result, 2), (f_gate_0, 1), (f_variance, 0), (f_gate_1, 1),
                                   (f_scale, 0), (f_gate_2, 1)])
                dve.wait_ge(v_carried, (l + 1) * NT)
                dve.memset(v_pair[64:128, :, :, 0:LD], 0.0).then_inc(cleared, 1)
            dve.wait_ge(y_sb, LAYERS * NG)


def recurrence_and_experts(nc, ps, X, Y, out_dram, u_in, w_in, b_in, gamma, beta,
                           wg_in, bg_in, w1_in, b1_in, w2_in, b2_in, c_ident, c_ties):
    with ExitStack() as ctx:
        def sb(name, shape, dt=F32):
            return ctx.enter_context(nc.sbuf_tensor("re_" + name, shape, dt))

        def sem(name):
            return nc.alloc_semaphore("re_" + name)

        ident, power8 = sb("ident", [P, P]), sb("power8", [P, B])
        eps8 = sb("eps8", [P, B])
        p_total, p_var, p_rs = sb("p_total", [P, 4]), sb("p_var", [P, 4]), sb("p_rs", [P, 4])
        p_cen, p_sq, p_yn = sb("p_cen", [P, 4, P]), sb("p_sq", [P, 4, P]), sb("p_yn", [P, B, P])
        total, var, rs = sb("total", [P, B]), sb("var", [P, B]), sb("rs", [P, B])
        cen, sq, yn = sb("cen", [P, B, P]), sb("sq", [P, B, P]), sb("yn", [P, B, P])
        r_total, r_var, r_rs = sb("r_total", [P, B]), sb("r_var", [P, B]), sb("r_rs", [P, B])
        r_cen = sb("r_cen", [P, B, P])
        w = sb("w", [P, 3 * P])
        u, g, b = sb("u", [P, 1]), sb("g", [P, 1]), sb("b", [P, 1])
        bc, bz, br = sb("bc", [P, 1]), sb("bz", [P, 1]), sb("br", [P, 1])
        xT, r = sb("xT", [P, 2, 4 * P]), sb("r", [P, 2, 4 * P])
        ROWS = P + 2
        mul, add = sb("mul", [P, ROWS, B, 3]), sb("add", [P, ROWS, B, 3])
        link, z = sb("link", [P, ROWS, B, 3]), sb("z", [P, ROWS, B])
        H_, S_, A_ = 0, 1, 2
        wg, bg = sb("wg", [P, E]), sb("bg", [P, E])
        w1, b1_rows, b1 = sb("w1", [P, E, H]), sb("b1_rows", [E * HCH, P]), sb("b1", [P, E, HCH])
        w2, b2 = sb("w2", [P, E, HCH, P]), sb("b2", [E, P])
        ties = sb("ties", [P, 2, E, E])
        xTs, wtT = sb("xTs", [P, B * P]), sb("wtT", [E, B * P])
        lgt, mx, ex, den = sb("lgt", [P, B, E]), sb("mx", [P, B]), sb("ex", [P, B, E]), sb("den", [P, B])
        ge, gt, rank, wt = sb("ge", [P, B, E, E]), sb("gt", [P, B, E, E]), sb("rank", [P, B, E]), sb("wt", [P, B, E])
        hid, accs = sb("hid", [P, 2, HCH, 4 * P]), sb("accs", [P, B, P])

        T_X, T_L, T_PROJ, T_Y, T_W, T_B, T_U, T_D = 0, 5, ((3, 4, 5), (6, 7, 2)), 6, 6, 6, 0, 4

        loaded, loaded_e, zeroed = sem("loaded"), sem("loaded_e"), sem("zeroed")
        p_totalled, p_centred, p_squared, p_summed, p_eps, p_rstd, p_normed, p_added = (
            sem("p_totalled"), sem("p_centred"), sem("p_squared"), sem("p_summed"), sem("p_eps"), sem("p_rstd"),
            sem("p_normed"), sem("p_added"))
        totalled, centred, squared, summed, eps_in, rstd, normed, added = (
            sem("totalled"), sem("centred"), sem("squared"), sem("summed"), sem("eps_in"), sem("rstd"),
            sem("normed"), sem("added"))
        r_totalled, r_centred, r_squared, r_summed, r_eps, r_rstd, r_normed, done, stored = (
            sem("r_totalled"), sem("r_centred"), sem("r_squared"), sem("r_summed"), sem("r_eps"), sem("r_rstd"),
            sem("r_normed"), sem("done"), sem("stored"))
        xT_ps, xT_sb, proj_ps, z_sb, r_sb, c_sb, zc_sb, ur_sb = (
            sem("xT_ps"), sem("xT_sb"), sem("proj_ps"), sem("z_sb"), sem("r_sb"), sem("c_sb"), sem("zc_sb"),
            sem("ur_sb"))
        a_part, linked, h_sb, zs_sb, y_ps = sem("a_part"), sem("linked"), sem("h_sb"), sem("zs_sb"), sem("y_ps")
        xTs_ps, xTs_sb, lgt_ps, biased, maxed, lshift, expd, denned, recip, probs = (
            sem("xTs_ps"), sem("xTs_sb"), sem("lgt_ps"), sem("biased"), sem("maxed"), sem("lshift"), sem("expd"),
            sem("denned"), sem("recip"), sem("probs"))
        compared, masked, both, ranked, wt_sb, wtT_ps, wtT_sb, base_ps, base_sb = (
            sem("compared"), sem("masked"), sem("both"), sem("ranked"), sem("wt_sb"), sem("wtT_ps"),
            sem("wtT_sb"), sem("base_ps"), sem("base_sb"))
        b1_ps, b1_sb, summed_x = sem("b1_ps"), sem("b1_sb"), sem("summed_x")
        up_ps, hid_sb, down_ps, acc_sb = sem("up_ps"), sem("hid_sb"), sem("down_ps"), sem("acc_sb")
        N_LOADS, N_LOADS_E, N_ZERO = 12, 3, 9
        GB = B // 4
        UNITS = GB * E
        SPU = P // UNITS

        block = ctx.enter_context(nc.Block())

        @block.sync
        def _(sp):
            sp.dma_start(ident[:, :], c_ident).then_inc(loaded, 16)
            sp.dma_start(w[:, :], w_in).then_inc(loaded, 16)
            for dst, src in ((u, u_in), (g, gamma), (b, beta), (bc, b_in[0:P]), (bz, b_in[P:2 * P]),
                             (br, b_in[2 * P:3 * P])):
                sp.dma_start(dst[:, :], src.unsqueeze(1)).then_inc(loaded, 16)
            sp.dma_start(wg[:, :], wg_in).then_inc(loaded, 16)
            sp.dma_start(bg[:, :], bg_in.partition_broadcast(P)).then_inc(loaded, 16)
            sp.dma_start(ties[:, :, :, :].rearrange("p a e j -> p (a e j)"), c_ties.to_broadcast([P, 2 * E * E]))\
                .then_inc(loaded, 16)
            sp.dma_start(b2[:, :], b2_in).then_inc(loaded, 16)
            sp.dma_start(b1_rows[:, :], b1_in.rearrange("e (c p) -> (e c) p", p=P)).then_inc(loaded_e, 16)
            sp.dma_start(w1[:, :, :], w1_in.rearrange("e d h -> d e h")).then_inc(loaded_e, 16)
            sp.dma_start(w2[:, :, :, :], w2_in.rearrange("e (c p) d -> p e c d", p=P)).then_inc(loaded_e, 16)
            out_tiles = out_dram.rearrange("b (i p) d -> i p b d", p=P)
            for i in range(NB):
                sp.wait_ge(done, i + 1)
                sp.dma_start(out_tiles[i], X[:, 8 * i:8 * i + 8, :]).then_inc(stored, 16)
            sp.wait_ge(stored, 16 * NB)

        @block.gpsimd
        def _(pool):
            pool.memset(eps8[:, :], EPS * P).then_inc(zeroed, 1)
            pool.memset(power8[:, :], -0.5).then_inc(zeroed, 1)
            pool.memset(mul[:, :, :, H_:H_ + 1], 0.0).then_inc(zeroed, 1)
            pool.memset(mul[:, P:P + 1, :, A_:A_ + 1], 0.0).then_inc(zeroed, 1)
            pool.memset(add[:, P:P + 1, :, A_:A_ + 1], 0.0).then_inc(zeroed, 1)
            pool.memset(z[:, P:P + 1, :], 0.0).then_inc(zeroed, 1)
            pool.memset(link[:, P:P + 1, :, :], 0.0).then_inc(zeroed, 1)
            pool.memset(z[:, P + 1:P + 2, :], 0.0).then_inc(zeroed, 1)
            pool.memset(add[:, 0:1, :, :], 0.0).then_inc(zeroed, 1)
            pool.wait_ge(zeroed, N_ZERO)

            def rsqrt(k, n, source, summed_, eps_, out, rstd_):
                pool.wait_ge(summed_, k + 1)
                pool.tensor_tensor(out[:, :], source[:, :], eps8[:, 0:n], ALU.add).then_inc(eps_, 1)
                pool.wait_ge(eps_, k + 1)
                pool.tensor_tensor(out[:, :], out[:, :], power8[:, 0:n], ALU.pow).then_inc(rstd_, 1)

            def before(n):
                for j in range(2 * GB):
                    rsqrt(2 * GB * n + j, 4, p_var, p_summed, p_eps, p_rs, p_rstd)

            def behind_experts(n):
                rsqrt(n, B, r_var, r_summed, r_eps, r_rs, r_rstd)
                pool.wait_ge(r_normed, n + 1)
                Xn = X[:, ds(8 * n, 8), :]
                pool.tensor_tensor(Xn, Xn, r_cen[:, :, :], ALU.add).then_inc(done, 1)

            def time_block(i, first=False, last=False):
                if not last:
                    before(i + 1)
                rsqrt(2 * i, B, var, summed, eps_in, rs, rstd)
                rsqrt(2 * i + 1, B, var, summed, eps_in, rs, rstd)
                if not first:
                    behind_experts(i - 1)

            before(0)
            time_block(0, first=True)
            with pool.Fori(1, NB - 1) as i:
                time_block(i)
            time_block(NB - 1, last=True)
            behind_experts(NB - 1)

        @block.tensor
        def _(pe):
            pe.wait_ge(loaded, 16 * N_LOADS)

            def project(n):
                pe.wait_ge(p_normed, 2 * GB * (n + 1))
                if not (isinstance(n, int) and n < 2):
                    pe.wait_ge(hid_sb, HCH * UNITS * (n - 1))
                for t in range(B):
                    mm = pe.transpose(ps[:, T_X + t // 4, P * (t % 4):P * (t % 4) + P], p_yn[:, t, :], ident[:, :])
                mm.then_inc(xT_ps, 1)
                for h in range(GB):
                    pe.wait_ge(xT_sb, GB * n + h + 1)
                    if not (isinstance(n, int) and n == 0):
                        pe.wait_ge(centred, 2 * n - 1)
                        pe.wait_ge(acc_sb, UNITS * (n - 1))
                    for c, bank in enumerate(T_PROJ[h]):
                        mm = pe.matmul(ps[:, bank, :], w[:, P * c:P * c + P], xT[:, h, :], start=True, stop=True)
                    mm.then_inc(proj_ps, 1)

            def up(j, m):
                M = UNITS * j + m
                for c in range(HCH):
                    if m:
                        pe.wait_ge(hid_sb, HCH * M + c - HCH + 1)
                    pe.matmul(ps[:, T_U + c, :], w1[:, m % E, P * c:P * c + P],
                              xTs[:, 4 * P * (m // E):4 * P * (m // E) + 4 * P], start=True, stop=True)\
                        .then_inc(up_ps, 1)

            def down(j, m):
                M = UNITS * j + m
                pe.wait_ge(hid_sb, HCH * (M + 1))
                pe.wait_ge(acc_sb, M - 1 if m else M)
                if m == 1:
                    pe.wait_ge(biased, j + 1)
                for t in range(4):
                    for c in range(HCH):
                        mm = pe.matmul(ps[:, T_D + m % 2, P * t:P * t + P], hid[:, m % 2, c, P * t:P * t + P],
                                       w2[:, m % E, c, :], start=(c == 0), stop=(c == HCH - 1))
                mm.then_inc(down_ps, 1)

            def products(j):
                up(j, 0)
                for m in range(1, UNITS - 1):
                    up(j, m)
                    if m == 2:
                        biases(j)
                    down(j, m - 1)
                    if m == 1:
                        turn_weights(j)
                up(j, UNITS - 1)

            def turn_states(i):
                pe.wait_ge(linked, (i + 1) * (P + 1))
                for t in range(B):
                    mm = pe.transpose(ps[:, T_Y + t // 4, P * (t % 4):P * (t % 4) + P],
                                      link[:, 1:P + 1, t:t + 1, S_:S_ + 1].rearrange("p t b s -> p (t b s)"),
                                      ident[:, :])
                mm.then_inc(y_ps, 1)

            def logits(i, last):
                pe.wait_ge(normed, 2 * i + 2)
                n = i + 1 if last else i + 2
                pe.wait_ge(xT_sb, GB * n)
                pe.wait_ge(c_sb, GB * n)
                pe.wait_ge(z_sb, GB * n)
                pe.wait_ge(r_sb, GB * n)
                if not (isinstance(i, int) and i == 0):
                    pe.wait_ge(hid_sb, HCH * UNITS * i)
                    pe.wait_ge(acc_sb, UNITS * i)
                for t in range(B):
                    mm = pe.transpose(ps[:, T_X + t // 4, P * (t % 4):P * (t % 4) + P], yn[:, t, :], ident[:, :])
                    if t % 4 == 3:
                        mm.then_inc(xTs_ps, 1)
                for t in range(B):
                    if t % 4 == 0:
                        pe.wait_ge(xTs_sb, 2 * i + 1 + t // 4)
                    mm = pe.matmul(ps[:, T_L, E * t:E * t + E], xTs[:, P * t:P * t + P], wg[:, :],
                                   start=True, stop=True)
                mm.then_inc(lgt_ps, 1)

            def turn_weights(i):
                pe.wait_ge(wt_sb, i + 1)
                for t in range(B):
                    mm = pe.transpose(ps[0:E, T_W + t // 4, P * (t % 4):P * (t % 4) + P], wt[:, t, :], ident[:, :])
                mm.then_inc(wtT_ps, 1)

            def biases(i):
                pe.wait_ge(wtT_sb, i + 1)
                for t in range(B):
                    mm = pe.matmul(ps[:, T_B + t // 4, P * (t % 4):P * (t % 4) + P], wtT[:, P * t:P * t + P],
                                   b2[:, :], start=True, stop=True)
                mm.then_inc(base_ps, 1)

            def time_block(i, first=False, last=False):
                if not first:
                    products(i - 1)
                turn_states(i)
                if not first:
                    down(i - 1, UNITS - 2)
                    down(i - 1, UNITS - 1)
                if not last:
                    project(i + 1)
                logits(i, last)

            project(0)
            pe.wait_ge(loaded_e, 16 * N_LOADS_E)
            pe.transpose(ps[:, T_X, 0:E * HCH], b1_rows[:, :], ident[0:E * HCH, 0:E * HCH]).then_inc(b1_ps, 1)
            pe.wait_ge(b1_sb, 1)
            time_block(0, first=True)
            with pe.Fori(1, NB - 1) as i:
                time_block(i)
            time_block(NB - 1, last=True)
            products(NB - 1)
            down(NB - 1, UNITS - 2)
            down(NB - 1, UNITS - 1)

        @block.scalar
        def _(act):
            act.preload_act_table_set("sigmoid_and_others")

            def flat(x):
                return x.rearrange("p t d -> p (t d)")

            def p_square(k):
                act.wait_ge(p_centred, k + 1)
                act.activation(flat(p_sq[:, :, :]), flat(p_cen[:, :, :]), ACT.Square).then_inc(p_squared, 1)

            def square(k):
                act.wait_ge(centred, k + 1)
                act.activation(flat(sq[:, :, :]), flat(cen[:, :, :]), ACT.Square).then_inc(squared, 1)

            def r_square(k):
                act.wait_ge(r_centred, k + 1)
                act.activation(flat(accs[:, :, :]), flat(r_cen[:, :, :]), ACT.Square).then_inc(r_squared, 1)

            def copy_x(n):
                act.wait_ge(xT_ps, n + 1)
                for h in range(GB):
                    act.activation(xT[:, h, :], ps[:, T_X + h, :], ACT.Identity, bias=b[:, :], scale=g[:, :])\
                        .then_inc(xT_sb, 1)

            def gates(n, h):
                act.wait_ge(proj_ps, GB * n + h + 1)
                act.wait_ge(linked, n * (P + 1))
                act.wait_ge(zs_sb, n * (P + 1))
                act.wait_ge(ur_sb, GB * n)
                act.activation(z[:, 0:P, 4 * h:4 * h + 4].rearrange("p t b -> p b t"),
                               ps[:, T_PROJ[h][1], :].rearrange("p (b t) -> p b t", b=4), ACT.Sigmoid,
                               bias=bz[:, :]).then_inc(z_sb, 1)
                act.activation(r[:, h, :], ps[:, T_PROJ[h][2], :], ACT.Sigmoid, bias=br[:, :]).then_inc(r_sb, 1)
                act.activation(add[:, 0:P, 4 * h:4 * h + 4, A_].rearrange("p t b -> p b t"),
                               ps[:, T_PROJ[h][0], :].rearrange("p (b t) -> p b t", b=4), ACT.Identity,
                               bias=bc[:, :]).then_inc(c_sb, 1)

            def gelu(j, m, c):
                M = UNITS * j + m
                act.wait_ge(up_ps, HCH * M + c + 1)
                act.wait_ge(down_ps, M - 1 if m else M)
                act.activation(hid[:, m % 2, c, :], ps[:, T_U + c, :], ACT.Gelu, bias=b1[:, m % E, c:c + 1])\
                    .then_inc(hid_sb, 1)

            def steps(i, first, last):
                for t in range(P):
                    act.wait_ge(linked, i * (P + 1) + t + 1)
                    act.activation(add[:, t + 1, :, H_], link[:, t, :, A_], ACT.Tanh).then_inc(h_sb, 1)
                    if not first and t % 2:
                        gelu(i - 1, t // SPU, t % SPU // 2)
                    if not first and t == 2 * SPU - 1:
                        copy_weights(i - 1)
                    if not first and t == 3 * SPU - 1:
                        copy_biases(i - 1)
                    if not last and t < 64 and t % 16 == 4:
                        p_square(2 * GB * (i + 1) + t // 16)

            def copy_xs(i):
                for h in range(GB):
                    act.wait_ge(xTs_ps, GB * i + h + 1)
                    act.copy(xTs[:, 4 * P * h:4 * P * h + 4 * P], ps[:, T_X + h, :]).then_inc(xTs_sb, 1)

            def exps(i):
                act.wait_ge(lshift, i + 1)
                act.activation(flat(ex[:, :, :]), flat(lgt[:, :, :]), ACT.Exp).then_inc(expd, 1)

            def copy_weights(i):
                act.wait_ge(wtT_ps, i + 1)
                act.copy(wtT[:, :], ps[0:E, T_W:T_W + 2, :].rearrange("p a n -> p (a n)")).then_inc(wtT_sb, 1)

            def copy_biases(i):
                act.wait_ge(base_ps, i + 1)
                act.wait_ge(r_summed, i)
                act.copy(flat(accs[:, :, :]), ps[:, T_B:T_B + 2, :].rearrange("p a n -> p (a n)"))\
                    .then_inc(base_sb, 1)

            def time_block(i, first=False, last=False):
                steps(i, first, last)
                act.preload_act_table_set("sigmoid_and_others")
                square(2 * i)
                if not last:
                    copy_x(i + 1)
                    gates(i + 1, 0)
                square(2 * i + 1)
                if not last:
                    gates(i + 1, 1)
                copy_xs(i)
                if not first:
                    r_square(i - 1)
                act.preload_act_table_set("natural_log_exp_and_others")
                exps(i)
                act.preload_act_table_set("gelu_and_others")

            for k in range(2 * GB):
                p_square(k)
            act.wait_ge(loaded, 16 * N_LOADS)
            act.wait_ge(zeroed, N_ZERO)
            copy_x(0)
            gates(0, 0)
            gates(0, 1)
            act.wait_ge(b1_ps, 1)
            act.copy(b1[:, :, :].rearrange("p e c -> p (e c)"), ps[:, T_X, 0:E * HCH]).then_inc(b1_sb, 1)
            act.wait_ge(b1_sb, 1)
            act.preload_act_table_set("gelu_and_others")
            time_block(0, first=True)
            with act.Fori(1, NB - 1) as i:
                time_block(i)
            time_block(NB - 1, last=True)
            for m in range(UNITS):
                for c in range(HCH):
                    gelu(NB - 1, m, c)
                if m == 1:
                    copy_weights(NB - 1)
                if m == 2:
                    copy_biases(NB - 1)
            r_square(NB - 1)

        @block.vector
        def _(dve):

            def wide(x, n):
                return x[:, :].unsqueeze(2).to_broadcast([P, n, P])

            def centre(out, total_, src, n, k, totalled_, centred_):
                dve.tensor_reduce(total_[:, :], src, AX, ALU.add).then_inc(totalled_, 1)
                dve.wait_ge(totalled_, k + 1)
                dve.scalar_tensor_tensor(out=out[:, :, :], in0=wide(total_, n), scalar=-1.0 / P, in1=src,
                                         op0=ALU.mult, op1=ALU.add).then_inc(centred_, 1)

            def scale(out, cen_, rs_, n, k, rstd_, normed_):
                dve.wait_ge(rstd_, k + 1)
                dve.scalar_tensor_tensor(out=out, in0=cen_[:, :, :], scalar=float(np.sqrt(P)), in1=wide(rs_, n),
                                         op0=ALU.mult, op1=ALU.mult).then_inc(normed_, 1)

            def p_index(n, h, a):
                return 2 * (GB * n + h) + a

            def p_wait(n, h, a):
                dve.wait_ge(p_normed, p_index(n, h, a))
                dve.wait_ge(p_added, GB * n + h + a)

            def p_centre(n, h, a):
                src = X[:, ds(8 * n + 4 * h, 4), :] if a else Y[:, ds(8 * n + 4 * h + 8, 4), :]
                centre(p_cen, p_total, src, 4, p_index(n, h, a), p_totalled, p_centred)

            def p_variance(n, h, a):
                dve.wait_ge(p_squared, p_index(n, h, a) + 1)
                dve.tensor_reduce(p_var[:, :], p_sq[:, :, :], AX, ALU.add).then_inc(p_summed, 1)

            def p_scale(n, h, a):
                dve.wait_ge(xT_ps, n)
                scale(p_yn[:, 4 * h:4 * h + 4, :], p_cen, p_rs, 4, p_index(n, h, a), p_rstd, p_normed)

            def p_add(n, h):
                Xg = X[:, ds(8 * n + 4 * h, 4), :]
                dve.wait_ge(p_normed, p_index(n, h, 0) + 1)
                dve.tensor_tensor(Xg, Xg, p_yn[:, 4 * h:4 * h + 4, :], ALU.add).then_inc(p_added, 1)

            def tables(n):
                for h in range(GB):
                    rows = slice(4 * h, 4 * h + 4)
                    dve.wait_ge(linked, n * (P + 1))
                    dve.wait_ge(z_sb, GB * n + h + 1)
                    dve.tensor_scalar(mul[:, 1:P + 1, rows, S_], z[:, 0:P, rows], -1.0, 1.0, ALU.mult, ALU.add)\
                        .then_inc(zc_sb, 1)
                    dve.wait_ge(r_sb, GB * n + h + 1)
                    dve.tensor_scalar(mul[:, 0:P, rows, A_].rearrange("p t b -> p b t"),
                                      r[:, h, :].rearrange("p (b t) -> p b t", b=4), u[:, :], None, ALU.mult)\
                        .then_inc(ur_sb, 1)
                state = link[:, P, :, S_]
                dve.wait_ge(ur_sb, GB * (n + 1))
                dve.wait_ge(c_sb, GB * (n + 1))
                dve.wait_ge(y_ps, n)
                dve.tensor_tensor(link[:, 0, :, S_], mul[:, 0, :, A_], state, ALU.mult).then_inc(a_part, 1)
                dve.tensor_tensor(add[:, 1, :, S_], z[:, 0, :], state, ALU.mult).then_inc(zs_sb, 1)
                dve.wait_ge(a_part, n + 1)
                dve.tensor_tensor(link[:, 0, :, A_], link[:, 0, :, S_], add[:, 0, :, A_], ALU.add).then_inc(linked, 1)

            def weigh(j, m, t):
                M = UNITS * j + m
                if t == 0:
                    dve.wait_ge(down_ps, M + 1)
                    dve.wait_ge(acc_sb, M)
                    dve.wait_ge(base_sb, j + 1)
                acc = accs[:, 4 * (m // E) + t, :]
                op = dve.scalar_tensor_tensor(out=acc, in0=ps[:, T_D + m % 2, P * t:P * t + P],
                                              scalar=wt[:, 4 * (m // E) + t, m % E:m % E + 1], in1=acc,
                                              op0=ALU.mult, op1=ALU.add)
                if t == 3:
                    op.then_inc(acc_sb, 1)

            def steps(i, first, last):
                for t in range(P):
                    h, a, at = t // 32, t % 32 // 16, t % 16
                    norms = not last and t < 64
                    if norms and at == 1:
                        p_wait(i + 1, h, a)
                    row = [x[:, t + 1, :, :].rearrange("p b s -> p (b s)") for x in (link, mul, add)]
                    dve.wait_ge(h_sb, i * P + t + 1)
                    dve.wait_ge(zs_sb, i * (P + 1) + t + 1)
                    dve.tensor_tensor_scan(row[0], row[1], row[2], 0.0, ALU.mult, ALU.add).then_inc(linked, 1)
                    dve.wait_ge(linked, i * (P + 1) + t + 2)
                    dve.tensor_tensor(add[:, t + 2, :, S_], link[:, t + 1, :, S_], z[:, t + 1, :], ALU.mult)\
                        .then_inc(zs_sb, 1)
                    if not first and t < ROUTING:
                        routing(i - 1, t)
                    if not first and t // SPU == 3:
                        weigh(i - 1, t % SPU // 4, t % 4)
                    if not first and t // SPU > 3 and t % 2:
                        weigh(i - 1, t // SPU - 2, t % SPU // 2)
                    if norms and at == 2:
                        p_centre(i + 1, h, a)
                    if norms and at == 6:
                        p_variance(i + 1, h, a)
                    if norms and at == 10:
                        p_scale(i + 1, h, a)
                    if norms and at == 12 and a == 0:
                        p_add(i + 1, h)

            def norm_states(i, first):
                Xi = X[:, ds(8 * i, 8), :]
                k = 2 * i
                dve.wait_ge(y_ps, i + 1)
                dve.wait_ge(normed, k)
                centre(cen, total, ps[:, T_Y:T_Y + 2, :].rearrange("p a (t d) -> p (a t) d", d=P), B, k,
                       totalled, centred)
                if not first:
                    for t in range(4):
                        weigh(i - 1, UNITS - 2, t)
                dve.wait_ge(squared, k + 1)
                dve.tensor_reduce(var[:, :], sq[:, :, :], AX, ALU.add).then_inc(summed, 1)
                if not first:
                    for t in range(4):
                        weigh(i - 1, UNITS - 1, t)
                scale(yn[:, :, :], cen, rs, B, k, rstd, normed)
                dve.wait_ge(normed, k + 1)
                dve.tensor_tensor(cen[:, :, :], Xi, yn[:, :, :], ALU.add).then_inc(summed_x, 1)
                dve.wait_ge(summed_x, i + 1)
                centre(cen, total, cen[:, :, :], B, k + 1, totalled, centred)
                dve.wait_ge(summed_x, i + 1)
                dve.tensor_tensor(Xi, Xi, yn[:, :, :], ALU.add).then_inc(added, 1)

            def by_expert(x):
                return x.unsqueeze(2).to_broadcast([P, B, E])

            def r_centre(j):
                dve.wait_ge(acc_sb, UNITS * (j + 1))
                dve.wait_ge(done, j)
                centre(r_cen, r_total, accs[:, :, :], B, j, r_totalled, r_centred)

            def r_variance(j):
                dve.wait_ge(r_squared, j + 1)
                dve.tensor_reduce(r_var[:, :], accs[:, :, :], AX, ALU.add).then_inc(r_summed, 1)

            def r_scale(j):
                dve.wait_ge(r_summed, j + 1)
                scale(r_cen[:, :, :], r_cen, r_rs, B, j, r_rstd, r_normed)

            def route(i, first, last):
                k = 2 * i + 1
                dve.wait_ge(squared, k + 1)
                dve.tensor_reduce(var[:, :], sq[:, :, :], AX, ALU.add).then_inc(summed, 1)
                dve.wait_ge(added, i + 1)
                scale(yn[:, :, :], cen, rs, B, k, rstd, normed)
                if not first:
                    r_centre(i - 1)
                if not last:
                    tables(i + 1)
                if not first:
                    r_variance(i - 1)

                dve.wait_ge(lgt_ps, i + 1)
                dve.tensor_tensor(lgt[:, :, :], ps[:, T_L, 0:B * E].rearrange("p (t e) -> p t e", e=E),
                                  bg[:, :].unsqueeze(1).to_broadcast([P, B, E]), ALU.add).then_inc(biased, 1)
                dve.wait_ge(biased, i + 1)
                dve.tensor_reduce(mx[:, :], lgt[:, :, :], AX, ALU.max).then_inc(maxed, 1)
                dve.wait_ge(maxed, i + 1)
                dve.tensor_tensor(lgt[:, :, :], lgt[:, :, :], by_expert(mx[:, :]), ALU.subtract).then_inc(lshift, 1)
                if not first:
                    r_scale(i - 1)
                if last:
                    for part in range(ROUTING):
                        routing(i, part)

            ROUTING = 10

            def routing(i, part):
                if part == 0:
                    dve.wait_ge(expd, i + 1)
                    dve.tensor_reduce(den[:, :], ex[:, :, :], AX, ALU.add).then_inc(denned, 1)
                if part == 1:
                    dve.wait_ge(denned, i + 1)
                    dve.reciprocal(den[:, :], den[:, :]).then_inc(recip, 1)
                if part == 2:
                    dve.wait_ge(recip, i + 1)
                    dve.tensor_tensor(wt[:, :, :], ex[:, :, :], by_expert(den[:, :]), ALU.mult).then_inc(probs, 1)
                if part in (3, 4):
                    x, op = ((ge, ALU.is_ge), (gt, ALU.is_gt))[part - 3]
                    dve.wait_ge(probs, i + 1)
                    dve.tensor_tensor(x[:, :, :, :], wt[:, :, :].unsqueeze(2).to_broadcast([P, B, E, E]),
                                      wt[:, :, :].unsqueeze(3).to_broadcast([P, B, E, E]), op).then_inc(compared, 1)
                if part in (5, 6):
                    x = (ge, gt)[part - 5]
                    dve.wait_ge(compared, 2 * i + part - 4)
                    dve.tensor_tensor(x[:, :, :, :].rearrange("p t e j -> p t (e j)"),
                                      x[:, :, :, :].rearrange("p t e j -> p t (e j)"),
                                      ties[:, part - 5, :, :].rearrange("p e j -> p (e j)").unsqueeze(1)
                                      .to_broadcast([P, B, E * E]), ALU.mult).then_inc(masked, 1)
                if part == 7:
                    dve.wait_ge(masked, 2 * i + 2)
                    dve.tensor_tensor(ge[:, :, :, :], ge[:, :, :, :], gt[:, :, :, :], ALU.add).then_inc(both, 1)
                if part == 8:
                    dve.wait_ge(both, i + 1)
                    dve.tensor_reduce(rank[:, :, :], ge[:, :, :, :], AX, ALU.add).then_inc(ranked, 1)
                if part == 9:
                    dve.wait_ge(ranked, i + 1)
                    dve.scalar_tensor_tensor(out=wt[:, :, :], in0=rank[:, :, :], scalar=1.5, in1=wt[:, :, :],
                                             op0=ALU.is_lt, op1=ALU.mult).then_inc(wt_sb, 1)

            def time_block(i, first=False, last=False):
                steps(i, first, last)
                norm_states(i, first)
                route(i, first, last)

            for h in range(GB):
                for a in range(2):
                    p_wait(0, h, a)
                    p_centre(0, h, a)
                    p_variance(0, h, a)
                    p_scale(0, h, a)
                    if a == 0:
                        p_add(0, h)
            dve.wait_ge(loaded, 16 * N_LOADS)
            dve.wait_ge(zeroed, N_ZERO)
            tables(0)
            time_block(0, first=True)
            with dve.Fori(1, NB - 1) as i:
                time_block(i)
            time_block(NB - 1, last=True)
            for m in range(UNITS):
                for t in range(4):
                    weigh(NB - 1, m, t)
            r_centre(NB - 1)
            r_variance(NB - 1)
            r_scale(NB - 1)
            dve.wait_ge(done, NB)


def sandwich_kernel(nc, L0_attn_x, L0_attn_W_qkv, L0_attn_ln_gamma, L0_attn_ln_beta, L0_attn_W_proj, L0_attn_b_proj,
                    L0_ffn_wqkv, L0_ffn_q_scale, L0_ffn_k_scale, L0_ffn_wo, L0_ffn_ln_g, L0_ffn_ln_b,
                    L0_ffn_w1, L0_ffn_b1, L0_ffn_w2, L0_ffn_b2, L1_attn_u, L1_attn_W, L1_attn_b,
                    L1_attn_gamma, L1_attn_beta, L1_ffn_Wg, L1_ffn_bg, L1_ffn_W1, L1_ffn_b1, L1_ffn_W2, L1_ffn_b2,
                    const_ident, const_shift, const_carry, const_lane, const_masks, const_rot, const_ties, out_0):
    with ExitStack() as ctx:
        X = ctx.enter_context(nc.sbuf_tensor("X", [P, NT, P], F32))
        Y = ctx.enter_context(nc.sbuf_tensor("Y", [P, NT + 8, P], F32))
        ps = ctx.enter_context(nc.psum_tensor("ps", [P, 8, 512], F32))
        with nc.cleanup_on_exit():
            window_attention(nc, ps, X, Y, L0_attn_x, L0_attn_W_qkv, L0_attn_ln_gamma, L0_attn_ln_beta, L0_attn_W_proj,
                             L0_attn_b_proj, const_ident, const_lane)
        with nc.cleanup_on_exit(), nc.sbuf_tensor("A", [P, NT + 8, P], F32) as A:
            local_transformer(nc, ps, Y, A, L0_ffn_wqkv, L0_ffn_q_scale, L0_ffn_k_scale, L0_ffn_wo, L0_ffn_ln_g,
                              L0_ffn_ln_b, L0_ffn_w1, L0_ffn_b1, L0_ffn_w2, L0_ffn_b2, const_ident, const_shift,
                              const_carry, const_masks, const_rot)
        with nc.cleanup_on_exit():
            recurrence_and_experts(nc, ps, X, Y, out_0, L1_attn_u, L1_attn_W, L1_attn_b, L1_attn_gamma, L1_attn_beta,
                                   L1_ffn_Wg, L1_ffn_bg, L1_ffn_W1, L1_ffn_b1, L1_ffn_W2, L1_ffn_b2, const_ident,
                                   const_ties)


def shape_constants():
    f = np.float32
    ident = np.eye(P, dtype=f)
    shift = np.zeros((P, P), f)
    shift[np.arange(P - 1), np.arange(1, P)] = 1
    carry = np.zeros((P, P), f)
    carry[P - 1, 0] = 1
    lane = np.zeros((P, 4), f)
    lane[np.arange(P), (np.arange(P) // WD) % 4] = 1
    q = np.arange(P)[:, None] % WIN
    c = np.arange(WIN)[None, :]
    own = np.where(c <= q, 0, NEG).astype(f)
    prev = np.where(c >= q, 0, NEG).astype(f)
    none = np.full((P, WIN), NEG, f)
    first = np.stack([np.concatenate([own, none if i == 0 else prev], 1) for i in range(NB)], 1)
    second = np.concatenate([prev, own], 1)[:, None]
    masks = np.concatenate([first, second], 1)
    half = np.arange(0, LD, 2, dtype=f)
    inv = (f(1.0) / f(10000.0) ** (half / f(LD))).astype(f)
    t = np.arange(T, dtype=f)
    fr = (t[:, None] * inv[None, :]).astype(f)
    base = ((half + f(0.4 * LD)) / f(1.4 * LD)).astype(f)
    power = ((t - T // 2) / f(WIN // 2)).astype(f)
    scale = (base[None, :].astype(np.float64) ** power[:, None]).astype(f)
    cos, sin = np.cos(fr), np.sin(fr)
    tabs = []
    for s in (scale * f(8.0), f(1) / scale):
        tabs.append((np.concatenate([cos * s, cos * s], 1), np.concatenate([-sin * s, sin * s], 1)))
    rot = np.stack([np.stack([a[0] for a in tabs], 1), np.stack([a[1] for a in tabs], 1)], 1)
    rot = rot.reshape(NB, P, 2, 2, LD).transpose(1, 0, 2, 3, 4).astype(f)
    before = np.tril(np.ones((E, E), f), -1)
    ties = np.stack([before, 1 - before - np.eye(E, dtype=f)]).reshape(1, -1)
    return {
        "ident": ident, "shift": shift, "carry": carry, "lane": lane,
        "masks": np.ascontiguousarray(masks.reshape(P, -1)), "rot": np.ascontiguousarray(rot.reshape(P, -1)),
        "ties": np.ascontiguousarray(ties.astype(f)),
    }


_INS = ['L0_attn_x', 'L0_attn_W_qkv', 'L0_attn_ln_gamma', 'L0_attn_ln_beta', 'L0_attn_W_proj', 'L0_attn_b_proj',
        'L0_ffn_wqkv', 'L0_ffn_q_scale', 'L0_ffn_k_scale', 'L0_ffn_wo', 'L0_ffn_ln_g', 'L0_ffn_ln_b',
        'L0_ffn_w1', 'L0_ffn_b1', 'L0_ffn_w2', 'L0_ffn_b2', 'L1_attn_u', 'L1_attn_W', 'L1_attn_b',
        'L1_attn_gamma', 'L1_attn_beta', 'L1_ffn_Wg', 'L1_ffn_bg', 'L1_ffn_W1', 'L1_ffn_b1', 'L1_ffn_W2',
        'L1_ffn_b2']
_OUTS = [((8, 512, 128), 'float32')]


def kernel(**inputs):
    import numpy as _np
    import concourse.bacc as _bacc
    from concourse import mybir as _mybir
    from concourse.bass_utils import run_bass_kernel_spmd as _run

    nc = _bacc.Bacc("TRN2", target_bir_lowering=False, num_devices=1)
    arrays = {}
    for name in _INS:
        a = _np.asarray(inputs[name])
        if name == 'L1_attn_W':
            a = a.T
        arrays[name] = _np.ascontiguousarray(a)
    for name, a in shape_constants().items():
        arrays["const_" + name] = a
    args = {name: nc.dram_tensor(name + "_dram", a.shape, _mybir.dt.from_np(a.dtype), kind="ExternalInput").ap()
            for name, a in arrays.items()}
    arrays = {name + "_dram": a for name, a in arrays.items()}
    for i, (shape, dtype) in enumerate(_OUTS):
        dt = _mybir.dt.from_np(_np.dtype(dtype))
        args[f"out_{i}"] = nc.dram_tensor(f"out_{i}_dram", shape, dt, kind="ExternalOutput").ap()
    sandwich_kernel(nc, **args)
    r = _run(nc, [arrays], core_ids=[0])
    got = tuple(r.results[0][f"out_{i}_dram"] for i in range(len(_OUTS)))
    return got[0]
```
